# Optimizing a Trainium2 kernel written in Bass

```python
import numpy as np
import jax
import jax.numpy as jnp

def _softmax(x, axis=-1):
    return jax.nn.softmax(x, axis=axis)

def _gelu(x):
    return jax.nn.gelu(x, approximate=True)

def _silu(x):
    return jax.nn.silu(x)

def _sigmoid(x):
    return jax.nn.sigmoid(x)

def _layernorm(x, axis=-1, eps=1e-05):
    m = jnp.mean(x, axis=axis, keepdims=True)
    v = jnp.var(x, axis=axis, keepdims=True)
    return (x - m) / jnp.sqrt(v + eps)

def _scatter_add(tgt, idx, src, axis=0):
    return tgt.at[idx].add(src)

def _segment_sum(src, seg, n):
    return jax.ops.segment_sum(src, seg, n)
kernel_name = 'mk_macaron_d1_jaxref_r4_b54d39'

def setup_inputs(seed: int=0):
    np.random.seed(seed)
    _w = jnp.asarray

    def _L0_attn_setup():
        import jax, jax.numpy as jnp
        import numpy as np
        D_MODEL = 256
        NUM_HEADS = 16
        D_K = D_MODEL // NUM_HEADS
        THETA = 10000.0
        NEG_INF = -1000000000.0

        def _rope(x, positions):
            half = D_K // 2
            inv_freq = 1.0 / THETA ** (jnp.arange(0, D_K, 2, dtype=jnp.float32) / D_K)
            angles = positions.astype(jnp.float32)[:, None] * inv_freq
            cos, sin = (jnp.cos(angles), jnp.sin(angles))
            xe = x[..., 0::2]
            xo = x[..., 1::2]
            re = xe * cos - xo * sin
            ro = xe * sin + xo * cos
            return jnp.stack([re, ro], axis=-1).reshape(x.shape).astype(x.dtype)
        key = jax.random.key(seed)
        ks = jax.random.split(key, 5)
        sigma = np.sqrt(2.0 / (D_MODEL + D_MODEL))
        x = jax.random.normal(ks[0], (2, 512, D_MODEL), dtype=jnp.float32)
        mk = lambda k: (sigma * jax.random.normal(k, (D_MODEL, D_MODEL))).astype(jnp.float32)
        return {'x': x, 'Wq': mk(ks[1]), 'bq': jnp.zeros((D_MODEL,), jnp.float32), 'Wk': mk(ks[2]), 'bk': jnp.zeros((D_MODEL,), jnp.float32), 'Wv': mk(ks[3]), 'bv': jnp.zeros((D_MODEL,), jnp.float32), 'Wo': mk(ks[4]), 'bo': jnp.zeros((D_MODEL,), jnp.float32), 'token_positions': jnp.arange(512, dtype=jnp.int64) if jax.config.jax_enable_x64 else jnp.arange(512, dtype=jnp.int32)}
    _L0_attn_in = _L0_attn_setup()

    def _L0_ffn_setup():
        import jax, jax.numpy as jnp
        import numpy as np
        TOP_K = 2
        key = jax.random.key(seed)
        k1, k2, k3 = jax.random.split(key, 3)
        B, S, H, E = (4, 512, 256, 8)
        hidden_states = jax.random.normal(k1, (B, S, H), dtype=jnp.float32)
        Wg = jax.random.normal(k2, (H, E), dtype=jnp.float32) * H ** (-0.5)
        We = jax.random.normal(k3, (E, H, H), dtype=jnp.float32) * H ** (-0.5)
        be = jnp.zeros((E, H), dtype=jnp.float32)
        return {'hidden_states': hidden_states, 'Wg': Wg, 'We': We, 'be': be}
    _L0_ffn_in = _L0_ffn_setup()
    _d = {'L0_attn_x': _L0_attn_in['x'], 'L0_attn_Wq': _L0_attn_in['Wq'], 'L0_attn_bq': _L0_attn_in['bq'], 'L0_attn_Wk': _L0_attn_in['Wk'], 'L0_attn_bk': _L0_attn_in['bk'], 'L0_attn_Wv': _L0_attn_in['Wv'], 'L0_attn_bv': _L0_attn_in['bv'], 'L0_attn_Wo': _L0_attn_in['Wo'], 'L0_attn_bo': _L0_attn_in['bo'], 'L0_attn_token_positions': _L0_attn_in['token_positions'], 'L0_ffn_Wg': _L0_ffn_in['Wg'], 'L0_ffn_We': _L0_ffn_in['We'], 'L0_ffn_be': _L0_ffn_in['be']}
    _x0 = _d['L0_attn_x']
    _d['L0_attn_x'] = jax.random.normal(jax.random.fold_in(jax.random.key(seed), 1), (16, 1024, 256), dtype=_x0.dtype)
    del _x0
    return _d

def reference(L0_attn_x, L0_attn_Wq, L0_attn_bq, L0_attn_Wk, L0_attn_bk, L0_attn_Wv, L0_attn_bv, L0_attn_Wo, L0_attn_bo, L0_attn_token_positions, L0_ffn_Wg, L0_ffn_We, L0_ffn_be):

    def _L0_attn_ref(x, Wq, bq, Wk, bk, Wv, bv, Wo, bo, token_positions):
        import jax, jax.numpy as jnp
        import numpy as np
        D_MODEL = 256
        NUM_HEADS = 16
        D_K = D_MODEL // NUM_HEADS
        THETA = 10000.0
        NEG_INF = -1000000000.0

        def _rope(x, positions):
            half = D_K // 2
            inv_freq = 1.0 / THETA ** (jnp.arange(0, D_K, 2, dtype=jnp.float32) / D_K)
            angles = positions.astype(jnp.float32)[:, None] * inv_freq
            cos, sin = (jnp.cos(angles), jnp.sin(angles))
            xe = x[..., 0::2]
            xo = x[..., 1::2]
            re = xe * cos - xo * sin
            ro = xe * sin + xo * cos
            return jnp.stack([re, ro], axis=-1).reshape(x.shape).astype(x.dtype)
        B, S, D = x.shape
        Q = x @ Wq.T + bq
        K = x @ Wk.T + bk
        V = x @ Wv.T + bv

        def split_heads(t):
            return t.reshape(B, S, NUM_HEADS, D_K).transpose(0, 2, 1, 3)
        Q, K, V = (split_heads(Q), split_heads(K), split_heads(V))
        pos = jnp.arange(S)
        Q = _rope(Q, pos)
        K = _rope(K, pos)
        scale = 1.0 / jnp.sqrt(jnp.float32(D_K))
        scores = jnp.einsum('bhqd,bhkd->bhqk', Q, K) * scale
        causal = jnp.tril(jnp.ones((S, S), dtype=bool))
        scores = jnp.where(causal, scores, NEG_INF)
        weights = jax.nn.softmax(scores, axis=-1)
        attn = jnp.einsum('bhqk,bhkd->bhqd', weights, V)
        concat = attn.transpose(0, 2, 1, 3).reshape(B, S, D)
        return concat @ Wo.T + bo

    def _L0_ffn_ref(hidden_states, Wg, We, be):
        import jax, jax.numpy as jnp
        import numpy as np
        TOP_K = 2
        B, S, H = hidden_states.shape
        T = B * S
        x = hidden_states.reshape(T, H)
        probs = jax.nn.softmax(x @ Wg, axis=-1)
        top_vals, top_idx = jax.lax.top_k(probs, TOP_K)
        gates = top_vals / jnp.sum(top_vals, axis=-1, keepdims=True)
        expert_out = jnp.einsum('th,ehd->etd', x, We) + be[:, None, :]
        tok = jnp.arange(T)[:, None]
        sel = expert_out[top_idx, tok, :]
        out = jnp.sum(gates[..., None] * sel, axis=1)
        return out.reshape(B, S, H)
    x = L0_attn_x
    x = x + 0.5 * _L0_ffn_ref(_layernorm(x, axis=-1), L0_ffn_Wg, L0_ffn_We, L0_ffn_be)
    x = x + _L0_attn_ref(_layernorm(x, axis=-1), L0_attn_Wq, L0_attn_bq, L0_attn_Wk, L0_attn_bk, L0_attn_Wv, L0_attn_bv, L0_attn_Wo, L0_attn_bo, L0_attn_token_positions)
    x = x + 0.5 * _L0_ffn_ref(_layernorm(x, axis=-1), L0_ffn_Wg, L0_ffn_We, L0_ffn_be)
    return x

_drawn_inputs = setup_inputs


def setup_inputs(seed=0):
    import zlib

    import numpy as np

    out = dict(_drawn_inputs(seed))
    spreads = {'L0_attn_bq': (0.0, 0.314),
     'L0_attn_bk': (0.0, 0.393),
     'L0_attn_bv': (0.0, 0.1),
     'L0_attn_bo': (0.0, 0.1),
     'L0_ffn_be': (0.0, 0.1)}
    factors = {}
    for name, (base, spread) in spreads.items():
        noise = np.random.default_rng([zlib.crc32(name.encode()), seed]).standard_normal(out[name].shape)
        drawn = base * np.exp(spread * noise) if base else spread * noise
        out[name] = jnp.asarray(drawn.astype(out[name].dtype))
    for name, factor in factors.items():
        out[name] = (out[name] * factor).astype(out[name].dtype)
    return out
```

```python
from contextlib import ExitStack

import numpy as np

import concourse.bass as bass
from concourse import mybir

F32 = mybir.dt.float32
FR = mybir.dt.float32r
BF16 = mybir.dt.bfloat16
U32 = mybir.dt.uint32
ALU = mybir.AluOpType
ACT = mybir.ActivationFunctionType

P = 128
B, S, D = 16, 1024, 256
H, DK, E = 16, 16, 8
KC = D // P
UNIT = 512
TILES = UNIT // P
UNITS = B * S // UNIT
HG = 4
GROUPS = H // HG
KT = S // P
EPS = 1e-5
THETA = 10000.0
MASKED = -1e30
LOWEST = -3e38


class Chain:

    def __init__(self, eng, sem):
        self.eng, self.sem, self.base, self.k = eng, sem, 0, 0

    def done(self, ins):
        ins.then_inc(self.sem, 1)
        self.k += 1
        return self.base + self.k

    def wait(self, at=None):
        self.eng.wait_ge(self.sem, self.base + self.k if at is None else at)

    def wait_apart(self):
        wait_apart(self.eng, self.sem, self.base + self.k)


def wait_apart(eng, sem, value):
    if not isinstance(value, int):
        eng.wait_ge(sem, value)
        eng.nop(nofuse=True)
    else:
        eng.wait_ge(sem, value)


def over_units(eng, step, chain=None, per_step=0, first=0, last=UNITS - 1):
    def at(u):
        return (u // 2, u % 2)

    def count(n):
        if chain is not None:
            assert chain.k == per_step * n, f"steps per unit: {chain.k} for {n}"

    for u in (-2, -1, 0, 1):
        step(at(u))
    k0 = chain.k if chain else 0
    with eng.Fori(1, UNITS // 2 - 2) as b:
        if chain:
            chain.base, chain.k = (b - 1) * (2 * per_step) + k0, 0
        step((b, 0))
        step((b, 1))
        count(2)
    if chain:
        chain.base, chain.k = k0 + (UNITS // 2 - 3) * 2 * per_step, 0
    for u in range(UNITS - 4, UNITS + 1):
        step(at(u))


def shift(unit, by):
    b, h = unit
    n = h + by
    return (b + n // 2, n % 2)


def num(unit):
    return unit[0] * 2 + unit[1]


def exists(unit):
    b = unit[0]
    return not isinstance(b, int) or 0 <= b < B


def rows(ap, unit):
    return ap[:, bass.ds(num(unit) * TILES, TILES), :]


class State:
    pass


class Kernel:
    def __init__(self, nc, args):
        self.nc = nc
        (self.x, self.Wq, self.bq, self.Wk, self.bk, self.Wv, self.bv, self.Wo, self.bo,
         self.Wg, self.We, self.be, self.cos, self.sin, self.out) = args
        nt = "(n p) d -> p n d"
        self.x_v = self.x.rearrange("b s d -> (b s) d").rearrange(nt, p=P)
        self.out_v = self.out.rearrange("b s d -> (b s) d").rearrange(nt, p=P)
        self.x1_v = nc.dram_tensor("x1", (B * S, D), F32, kind="Internal").ap().rearrange(nt, p=P)
        v = nc.dram_tensor("v", (B * S, D), F32, kind="Internal").ap()
        self.v_v = v.rearrange(nt, p=P)
        self.qs = nc.dram_tensor("q_split", (B, 2, DK, H, S), F32, kind="Internal").ap()
        self.ks = nc.dram_tensor("k_split", (B, 2, DK, H, S), F32, kind="Internal").ap()
        self.os = nc.dram_tensor("o_sums", (B, GROUPS, P, S), F32, kind="Internal").ap()
        self.nsem = 0

    def sem(self, ctx, name):
        self.nsem += 1
        return ctx.enter_context(self.nc.semaphore(name))

    def sb(self, ctx, name, shape, dt=F32):
        return ctx.enter_context(self.nc.sbuf_tensor(name, shape, dt))

    def weights(self, ctx, tag, squares):
        nc = self.nc
        w = {}
        sb = lambda n, s, dt=F32: self.sb(ctx, f"{n}_{tag}", s, dt)
        w["ident"] = sb("ident", [P, P])
        w["We"] = [sb(f"We{k}", [P, KC, E * D], FR) for k in range(2)]
        w["Wg"] = [sb(f"Wg{k}", [P, KC, P], FR) for k in range(2)]
        w["be"] = sb("be", [P, D], FR)
        w["iota"] = sb("iota", [P, E])
        w["nhalf"] = sb("nhalf", [P, TILES])
        for name in squares:
            w[name] = [sb(f"{name}{k}", [P, KC, D], FR) for k in range(2)]
        with ExitStack() as tmp:
            raw = self.sb(tmp, f"raw_{tag}", [P, KC, E * D])
            rawg = self.sb(tmp, f"rawg_{tag}", [P, KC, E])
            rawb = self.sb(tmp, f"rawb_{tag}", [P, D])
            rawi = self.sb(tmp, f"rawi_{tag}", [P, E], mybir.dt.int32)
            sq = self.sb(tmp, f"sq_{tag}", [P, max(1, len(squares)), KC, D])
            ps = tmp.enter_context(nc.psum_tensor(f"ps_{tag}", [P, 4, 512], F32))
            s_ld, s_ldg, s_ldb, s_lds, s_id, s_set, s_tr, s_own = (
                self.sem(ctx, f"{n}_{tag}") for n in
                ("w_loaded", "wg_loaded", "be_loaded", "sq_loaded", "ident_set", "zeros_set", "sq_turned", "w_own"))
            with nc.Block() as block:
                @block.sync
                def _(sp):
                    for e in range(E):
                        sp.dma_start(raw[:, :, e * D:(e + 1) * D],
                                     self.We[e].rearrange("(k p) n -> p k n", p=P)).then_inc(s_ld, 16)
                    sp.dma_start(rawg[:], self.Wg.rearrange("(k p) e -> p k e", p=P)).then_inc(s_ldg, 16)
                    for n in range(3):
                        sp.dma_start(rawb[32 * n:32 * n + E, :], self.be).then_inc(s_ldb, 16)
                    for n, name in enumerate(squares):
                        src = {"Wq": self.Wq, "Wk": self.Wk, "Wv": self.Wv, "Wo": self.Wo}[name]
                        sp.dma_start(sq[:, n], src.rearrange("(k p) n -> p k n", p=P)).then_inc(s_lds, 16)

                @block.gpsimd
                def _(pool):
                    pool.memset(w["ident"][:], 0.0).then_inc(s_id, 1)
                    pool.wait_ge(s_id, 1)
                    pool.affine_select(out=w["ident"][:], in_=w["ident"][:], compare_op=ALU.not_equal, fill=1.0,
                                       base=0, pattern=[[-1, P]], channel_multiplier=1).then_inc(s_id, 1)
                    pool.iota(rawi[:], pattern=[[1, E]], base=0, channel_multiplier=0).then_inc(s_id, 1)
                    pool.wait_ge(s_id, 3)
                    pool.tensor_copy(w["iota"][:], rawi[:]).then_inc(s_id, 1)
                    pool.memset(w["nhalf"][:], -0.5).then_inc(s_id, 1)

                @block.tensor
                def _(pe):
                    pe.wait_ge(s_id, 2)
                    if squares:
                        pe.wait_ge(s_lds, 16 * len(squares))
                    for n in range(len(squares)):
                        for ki in range(KC):
                            for ko in range(KC):
                                ins = pe.transpose(ps[:, n, ki * D + ko * P:ki * D + (ko + 1) * P],
                                                   sq[:, n, ko, ki * P:(ki + 1) * P], w["ident"][:])
                        ins.then_inc(s_tr, 1)

                @block.vector
                def _(dve):
                    own = Chain(dve, s_own)

                    def split(hi, lo, src):
                        own.done(dve.tensor_copy(hi, src))
                        own.wait()
                        own.done(dve.tensor_tensor(lo, src, hi.bitcast(F32), ALU.subtract))

                    dve.memset(w["be"][:].bitcast(F32), 0.0).then_inc(s_set, 1)
                    for k in range(2):
                        dve.memset(w["Wg"][k][:].bitcast(F32), 0.0).then_inc(s_set, 1)
                    dve.wait_ge(s_set, 3)
                    dve.wait_ge(s_ld, 16 * E)
                    for k in range(KC):
                        split(w["We"][0][:, k], w["We"][1][:, k], raw[:, k])
                    dve.wait_ge(s_ldg, 16)
                    split(w["Wg"][0][:, :, 0:E], w["Wg"][1][:, :, 0:E], rawg[:])
                    dve.wait_ge(s_ldb, 48)
                    for n in range(3):
                        a = slice(32 * n, 32 * n + E)
                        own.done(dve.tensor_copy(w["be"][a, :], rawb[a, :]))
                    own.wait()
                    own.done(dve.tensor_tensor(w["be"][64:64 + E, :], rawb[64:64 + E, :],
                                               w["be"][64:64 + E, :].bitcast(F32), ALU.subtract))
                    for n, name in enumerate(squares):
                        dve.wait_ge(s_tr, n + 1)
                        split(w[name][0][:].rearrange("p k n -> p (k n)"),
                              w[name][1][:].rearrange("p k n -> p (k n)"), ps[:, n, :])
                    own.wait()
        return w

    def ffn_state(self, ctx, tag):
        s = State()
        sb = lambda n, sh, dt=F32: self.sb(ctx, f"{n}_{tag}", sh, dt)
        s.st, s.mv, s.rs = sb("st", [P, TILES, 6]), sb("mv", [P, TILES, 2]), sb("rs", [P, TILES])
        s.xn = sb("xn", [P, TILES, D])
        s.xT = [[sb(f"xT{h}{k}", [P, KC, UNIT], FR) for k in range(2)] for h in range(2)]
        s.lT = sb("lT", [P, UNIT])
        s.m8, s.i8 = sb("m8", [P, TILES, 8]), sb("i8", [P, TILES, 8], U32)
        s.top = sb("top", [P, TILES, 2])
        s.d, s.e2, s.den, s.rden = (sb(n, [P, TILES]) for n in ("gap", "e2", "den", "rden"))
        s.g1, s.g2 = sb("g1", [P, TILES]), sb("g2", [P, TILES])
        s.G = [sb(f"G{k}", [P, TILES, E]) for k in range(2)]
        s.Gb = sb("Gb", [P, TILES, E])
        s.Gh = sb("Gh", [P, TILES, E], FR)
        s.Gw = sb("Gw", [P, TILES, P])
        s.GT = sb("GT", [P, UNIT], FR)
        s.acc = [sb(f"acc{h}", [P, TILES, D]) for h in range(2)]
        psum = lambda n, sh: ctx.enter_context(self.nc.psum_tensor(f"{n}_{tag}", sh, F32))
        s.psE = psum("psE", [P, 4, 512])
        s.psW = psum("psW", [P, 4, 512])
        s.mv_ready = self.sem(ctx, f"mv_ready_{tag}")
        s.rs_ready = self.sem(ctx, f"rs_ready_{tag}")
        s.xn_ready = self.sem(ctx, f"xn_ready_{tag}")
        s.turned = self.sem(ctx, f"turned_{tag}")
        s.hi_ready = self.sem(ctx, f"hi_ready_{tag}")
        s.lo_ready = self.sem(ctx, f"lo_ready_{tag}")
        s.logitsT = self.sem(ctx, f"logitsT_{tag}")
        s.logitsT_out = self.sem(ctx, f"logitsT_out_{tag}")
        s.logits = self.sem(ctx, f"logits_{tag}")
        s.gap_ready = self.sem(ctx, f"gap_ready_{tag}")
        s.e2_ready = self.sem(ctx, f"e2_ready_{tag}")
        s.gates_ready = self.sem(ctx, f"gates_ready_{tag}")
        s.gates_turned = self.sem(ctx, f"gates_turned_{tag}")
        s.gates_out = self.sem(ctx, f"gates_out_{tag}")
        s.bias_ready = self.sem(ctx, f"bias_ready_{tag}")
        s.acc_set = self.sem(ctx, f"acc_set_{tag}")
        s.experts = self.sem(ctx, f"experts_{tag}")
        s.combined = self.sem(ctx, f"combined_{tag}")
        s.own = self.sem(ctx, f"own_{tag}")
        return s

    def turn(self, pe, s, w, src, bank, pair, signal):
        for i in range(2):
            for k in range(KC):
                ins = pe.transpose(s.psW[:, bank, (k * 2 + i) * P:(k * 2 + i + 1) * P],
                                   src[:, 2 * pair + i, k * P:(k + 1) * P], w["ident"][:])
        ins.then_inc(signal, 1)

    def turned_view(self, s, bank):
        return s.psW[:, bank, :].rearrange("p (k n) -> p k n", k=KC)

    def three(self, pe, out, stationary, moving, first=True, last=True):
        n, total = 0, 3 * KC
        for k in range(KC):
            for a, b in ((0, 0), (0, 1), (1, 0)):
                ins = pe.matmul(out, stationary(a, k), moving(b, k), start=(n == 0), stop=(n == total - 1))
                n += 1
        return ins

    def pe_experts(self, pe, s, w, unit, i):
        xT = s.xT[unit[1]]
        if i == 0:
            pass
        for c in range(4):
            tile = num(unit) * TILES + i
            if not (isinstance(tile, int) and tile == 0):
                pe.wait_ge(s.combined, (tile - 1) * 4 + c + 1)
            self.three(pe, s.psE[:, c, :], lambda a, k: xT[a][:, k, i * P:(i + 1) * P],
                       lambda a, k: w["We"][a][:, k, c * 512:(c + 1) * 512]).then_inc(s.experts, 1)

    def pe_turn_unit(self, pe, s, w, v):
        pe.wait_ge(s.xn_ready, num(v) + 1)
        for pair in range(2):
            if not (isinstance(v[0], int) and num(v) == 0):
                pe.wait_ge(s.acc_set, 2 * num(v))
            self.turn(pe, s, w, s.xn, pair, pair, s.turned)

    def pe_router(self, pe, s, w, v):
        pe.wait_ge(s.hi_ready, 2 * num(v) + 2)
        pe.wait_ge(s.lo_ready, 2 * num(v) + 2)
        xT = s.xT[v[1]]
        self.three(pe, s.psW[:, 0, :], lambda a, k: w["Wg"][a][:, k, :],
                   lambda a, k: xT[a][:, k, :]).then_inc(s.logitsT, 1)

    def pe_logits(self, pe, s, w, v):
        pe.wait_ge(s.logitsT_out, num(v) + 1)
        for i in range(TILES):
            ins = pe.transpose(s.psW[:, 1, i * P:(i + 1) * P], s.lT[:, i * P:(i + 1) * P], w["ident"][:])
        ins.then_inc(s.logits, 1)

    def pe_gates(self, pe, s, w, v):
        pe.wait_ge(s.gates_ready, num(v) + 1)
        for i in range(TILES):
            ins = pe.transpose(s.psW[:, 0, i * P:(i + 1) * P], s.Gw[:, i, :], w["ident"][:])
        ins.then_inc(s.gates_turned, 1)

    def pe_bias(self, pe, s, w, v):
        pe.wait_ge(s.gates_out, num(v) + 1)
        for pair in range(2):
            for i in range(2):
                t = 2 * pair + i
                ins = pe.matmul(s.psW[:, 1 - pair, i * D:(i + 1) * D], s.GT[:, t * P:(t + 1) * P], w["be"][:],
                                start=(i == 0), stop=True, skip_group_check=True)
            ins.then_inc(s.bias_ready, 1)

    def act_hi(self, act, s, v):
        for pair in range(2):
            act.wait_ge(s.turned, 2 * num(v) + pair + 1)
            act.activation(s.xT[v[1]][0][:, :, pair * 2 * P:(pair + 1) * 2 * P],
                           self.turned_view(s, pair), ACT.Copy).then_inc(s.hi_ready, 1)

    def act_router(self, act, s, v):
        act.wait_ge(s.logitsT, num(v) + 1)
        act.activation(s.lT[:], s.psW[:, 0, :], ACT.Copy).then_inc(s.logitsT_out, 1)
        
    def act_gates(self, act, s, v):
        act.wait_ge(s.gap_ready, num(v) + 1)
        act.activation(s.e2[:], s.d[:], ACT.Exp).then_inc(s.e2_ready, 1)
        act.wait_ge(s.gates_turned, num(v) + 1)
        act.activation(s.GT[:], s.psW[:, 0, :], ACT.Copy).then_inc(s.gates_out, 1)

    def dve_stats(self, dve, own, src, st, mv, signal):
        for i in range(TILES):
            own.done(dve.bn_stats(st[:, i, :], src[:, i, :]))
        own.wait_apart()
        for i in range(TILES):
            ins = dve.bn_aggr(mv[:, i, :], st[:, i, :])
        ins.then_inc(signal, 1)

    def pool_rs(self, pool, s, w, mv, rs, own, ready, signal, n):
        wait_apart(pool, ready, n + 1)
        own.done(pool.tensor_scalar(rs[:], mv[:, :, 1], EPS, None, ALU.add))
        own.wait()
        pool.tensor_tensor(rs[:], rs[:], w["nhalf"][:], ALU.pow).then_inc(signal, 1)

    def dve_norm(self, dve, src, dst, mv, rs, ready, signal, n):
        dve.wait_ge(ready, n + 1)
        for i in range(TILES):
            ins = dve.tensor_scalar(dst[:, i, :], src[:, i, :], mv[:, i, 0:1], rs[:, i:i + 1],
                                    ALU.subtract, ALU.mult)
        ins.then_inc(signal, 1)

    def dve_lo(self, dve, s, v):
        for pair in range(2):
            dve.wait_ge(s.hi_ready, 2 * num(v) + pair + 1)
            a = slice(pair * 2 * P, (pair + 1) * 2 * P)
            dve.tensor_tensor(s.xT[v[1]][1][:, :, a], self.turned_view(s, pair),
                              s.xT[v[1]][0][:, :, a].bitcast(F32), ALU.subtract).then_inc(s.lo_ready, 1)

    def dve_router(self, dve, s, w, own, v):
        wait_apart(dve, s.logits, num(v) + 1)
        L = s.psW[:, 1, :].rearrange("p (i n) -> p i n", i=TILES)
        for i in range(TILES):
            own.done(dve.max(s.m8[:, i, :], L[:, i, 0:E]))
        own.wait_apart()
        for i in range(TILES):
            own.done(dve.max_index(s.i8[:, i, :], s.m8[:, i, :], L[:, i, 0:E]))
        dve.tensor_tensor(s.d[:], s.m8[:, :, 1], s.m8[:, :, 0], ALU.subtract).then_inc(s.gap_ready, 1)
        own.wait()
        own.done(dve.tensor_copy(s.top[:], s.i8[:, :, 0:2]))
        dve.wait_ge(s.e2_ready, num(v) + 1)
        own.done(dve.tensor_scalar(s.den[:], s.e2[:], 2.0, 2.0, ALU.mult, ALU.add))
        own.wait()
        own.done(dve.reciprocal(s.g1[:], s.den[:]))
        own.wait()
        own.done(dve.tensor_tensor(s.g2[:], s.e2[:], s.g1[:], ALU.mult))
        own.wait()
        for i in range(TILES):
            for k, g in enumerate((s.g1, s.g2)):
                own.done(dve.tensor_scalar(s.G[k][:, i, :], w["iota"][:], s.top[:, i, k:k + 1], g[:, i:i + 1],
                                           ALU.is_equal, ALU.mult))
        own.wait()
        own.done(dve.tensor_tensor(s.Gb[:], s.G[0][:], s.G[1][:], ALU.add))
        own.wait()
        own.done(dve.tensor_copy(s.Gh[:], s.Gb[:]))
        own.wait()
        own.done(dve.tensor_copy(s.Gw[:, :, 0:E], s.Gh[:].bitcast(F32)))
        own.done(dve.tensor_copy(s.Gw[:, :, 64:64 + E], s.Gh[:].bitcast(F32)))
        dve.tensor_tensor(s.Gw[:, :, 32:32 + E], s.Gb[:], s.Gh[:].bitcast(F32),
                          ALU.subtract).then_inc(s.gates_ready, 1)

    def dve_acc_set(self, dve, s, v, x_of):
        for pair in range(2):
            dve.wait_ge(s.bias_ready, 2 * num(v) + pair + 1)
            t = slice(2 * pair, 2 * pair + 2)
            dve.tensor_tensor(s.acc[v[1]][:, t, :], s.psW[:, 1 - pair, :].rearrange("p (i n) -> p i n", i=2),
                              x_of(v)[:, t, :], ALU.add).then_inc(s.acc_set, 1)

    def dve_combine(self, dve, s, own, unit, i):
        acc = s.acc[unit[1]][:, i, :]
        if i == 0:
            dve.wait_ge(s.acc_set, 2 * num(unit) + 2)
        for e in range(E):
            if e % 2 == 0:
                dve.wait_ge(s.experts, (num(unit) * TILES + i) * 4 + e // 2 + 1)
            ins = dve.scalar_tensor_tensor(out=acc, in0=s.psE[:, e // 2, (e % 2) * D:(e % 2 + 1) * D],
                                           scalar=self.gate(s, unit)[:, i, e:e + 1], in1=acc,
                                           op0=ALU.mult, op1=ALU.add)
            if e % 2 == 1:
                ins.then_inc(s.combined, 1)
                dve.wait_ge(s.combined, (num(unit) * TILES + i) * 4 + e // 2 + 1)
            else:
                own.done(ins)
                own.wait()

    def gate(self, s, unit):
        return s.gates[unit[1]]

    def pass_a(self):
        nc = self.nc
        with ExitStack() as ctx:
            w = self.weights(ctx, "a", ["Wq", "Wk", "Wv"])
            s = self.ffn_state(ctx, "a")
            sb = lambda n, sh, dt=F32: self.sb(ctx, n, sh, dt)
            sem = lambda n: self.sem(ctx, n)
            s.gates = [sb(f"gates{h}", [P, TILES, E]) for h in range(2)]
            X = [sb(f"X{h}", [P, TILES, D]) for h in range(2)]
            st2, mv2, rs2 = sb("st2", [P, TILES, 6]), sb("mv2", [P, TILES, 2]), sb("rs2", [P, TILES])
            xn2 = sb("xn2", [P, TILES, D])
            x2T = [sb(f"x2T{k}", [P, KC, UNIT], FR) for k in range(2)]
            cos, sin = sb("cos", [P, S]), sb("sin", [P, S])
            bqk = sb("bqk", [P, 2, 2])
            bv = sb("bv", [P, D])
            raw = [[sb(f"raw{t}{e}", [P, UNIT]) for e in range(2)] for t in range(2)]
            prod = [[sb(f"prod{t}{n}", [P, UNIT]) for n in range(2)] for t in range(2)]
            rot = [[sb(f"rot{t}{e}", [P, UNIT]) for e in range(2)] for t in range(2)]
            parts = [[[sb(f"part{t}{e}{k}", [P, UNIT], FR) for k in range(2)] for e in range(2)] for t in range(2)]
            V = sb("V", [P, TILES, D])
            x_loaded = [sem(f"x_loaded{h}") for h in range(2)]
            x1_stored = [sem(f"x1_stored{h}") for h in range(2)]
            (consts, mv2_ready, rs2_ready, xn2_ready, turned2, hi2, lo2, qk_ready, qk_out, v_ready, v_out,
             rot_q, rot_k, qk_hi, qk_lo, qk_stored, v_stored, pool_own, x1_done) = (sem(n) for n in (
                 "consts", "mv2_ready", "rs2_ready", "xn2_ready", "turned2", "hi2", "lo2", "qk_ready", "qk_out",
                 "v_ready", "v_out", "rot_q", "rot_k", "qk_hi", "qk_lo", "qk_stored", "v_stored", "pool_own",
                 "x1_done"))
            gw_zero = sem("gw_zero")

            block = ctx.enter_context(nc.Block())

            @block.sync
            def _(sp):
                sp.dma_start(cos[:], self.cos).then_inc(consts, 16)
                sp.dma_start(sin[:], self.sin).then_inc(consts, 16)
                for t, b in enumerate((self.bq, self.bk)):
                    sp.dma_start(bqk[:, t, :], b.rearrange("(p e) -> p e", e=2)).then_inc(consts, 16)
                sp.dma_start(bv[:], self.bv.partition_broadcast(P)).then_inc(consts, 16)
                sp.dma_start(X[0][:], rows(self.x_v, (0, 0))).then_inc(x_loaded[0], 16)

                def step(u):
                    v, p, c = shift(u, 2), shift(u, -1), u
                    if exists(v) and not num_is(v, 0):
                        if not num_below(v, 2):
                            sp.wait_ge(s.acc_set, 2 * num(v) - 2)
                        sp.dma_start(X[v[1]][:], rows(self.x_v, v)).then_inc(x_loaded[v[1]], 16)
                    if exists(p):
                        for t in range(2):
                            dst = (self.qs, self.ks)[t].rearrange("b t (e i) h n -> b t e h i n", e=2)
                            for e in range(2):
                                n = (num(p) * 2 + t) * 2 + e
                                for k in range(2):
                                    sp.wait_ge((qk_hi, qk_lo)[k], n + 1)
                                    sp.dma_start(dst[p[0], k, e, :, :, bass.ds(p[1] * UNIT, UNIT)],
                                                 parts[t][e][k][:].bitcast(F32)).then_inc(qk_stored, 16)
                        sp.wait_ge(v_out, 2 * num(p) + 2)
                        sp.dma_start(rows(self.v_v, p), V[:]).then_inc(v_stored, 16)
                        sp.wait_ge(qk_stored, 128 * num(p) + 128)
                        sp.wait_ge(v_stored, 16 * num(p) + 16)
                    if exists(c):
                        sp.wait_ge(s.combined, 16 * num(c) + 16)
                        sp.dma_start(rows(self.x1_v, c), s.acc[c[1]][:]).then_inc(x1_stored[c[1]], 16)

                over_units(sp, step)
                for h in range(2):
                    sp.wait_ge(x1_stored[h], 16 * UNITS // 2)

            @block.tensor
            def _(pe):
                def step(u):
                    v, p = shift(u, 1), shift(u, -1)
                    if exists(u):
                        self.pe_experts(pe, s, w, u, 0)
                    if exists(v):
                        self.pe_turn_unit(pe, s, w, v)
                    if exists(u):
                        self.pe_experts(pe, s, w, u, 1)
                    if exists(v):
                        self.pe_router(pe, s, w, v)
                    if exists(p):
                        pe.wait_ge(xn2_ready, num(p) + 1)
                        for pair in range(2):
                            if not num_is(p, 0):
                                pe.wait_ge(v_out, 2 * num(p) - 1 + pair)
                            self.turn(pe, s, w, xn2, 2 + pair, pair, turned2)
                    if exists(u):
                        self.pe_experts(pe, s, w, u, 2)
                    if exists(v):
                        self.pe_logits(pe, s, w, v)
                    if exists(p):
                        pe.wait_ge(hi2, 2 * num(p) + 2)
                        pe.wait_ge(lo2, 2 * num(p) + 2)
                        for t in range(2):
                            for e in range(2):
                                n = num(p) * 4 + 2 * t + e
                                if t == 1:
                                    pe.wait_ge(qk_out, n - 1)
                                W = w["WqWk"[2 * t:2 * t + 2]]
                                self.three(pe, s.psW[:, 2 + e, :], lambda a, k: W[a][:, k, e:D:2],
                                           lambda a, k: x2T[a][:, k, :]).then_inc(qk_ready, 1)
                        for pair in range(2):
                            pe.wait_ge(qk_out, num(p) * 4 + 3 + pair)
                            for i in range(2):
                                t = 2 * pair + i
                                ins = self.three(pe, s.psW[:, 2 + pair, i * D:(i + 1) * D],
                                                 lambda a, k: x2T[a][:, k, t * P:(t + 1) * P],
                                                 lambda a, k: w["Wv"][a][:, k, :])
                            ins.then_inc(v_ready, 1)
                    if exists(v):
                        self.pe_gates(pe, s, w, v)
                    if exists(u):
                        self.pe_experts(pe, s, w, u, 3)
                    if exists(v):
                        self.pe_bias(pe, s, w, v)

                over_units(pe, step)

            @block.scalar
            def _(act):
                act.wait_ge(consts, 80)

                def step(u):
                    v, p = shift(u, 1), shift(u, -1)
                    if exists(v):
                        self.act_hi(act, s, v)
                        self.act_router(act, s, v)
                    if exists(p):
                        for pair in range(2):
                            act.wait_ge(turned2, 2 * num(p) + pair + 1)
                            act.activation(x2T[0][:, :, pair * 2 * P:(pair + 1) * 2 * P],
                                           self.turned_view(s, 2 + pair), ACT.Copy).then_inc(hi2, 1)
                        for t in range(2):
                            for e in range(2):
                                n = num(p) * 4 + 2 * t + e
                                if not num_is(p, 0):
                                    act.wait_ge((rot_q, rot_k)[t], 2 * num(p))
                                act.wait_ge(qk_ready, n + 1)
                                act.activation(raw[t][e][:], s.psW[:, 2 + e, :], ACT.Identity,
                                               bias=bqk[:, t, e:e + 1]).then_inc(qk_out, 1)
                    if exists(v):
                        self.act_gates(act, s, v)
                    if exists(p):
                        if not num_is(p, 0):
                            act.wait_ge(qk_stored, 128 * num(p))
                        for t in range(2):
                            for e in range(2):
                                act.wait_ge((rot_q, rot_k)[t], 2 * num(p) + e + 1)
                                act.activation(parts[t][e][0][:], rot[t][e][:], ACT.Copy).then_inc(qk_hi, 1)

                over_units(act, step)

            def rotate(eng, own, t, p, signal):
                at = slice(p[1] * UNIT, (p[1] + 1) * UNIT)
                eng.wait_ge(qk_out, num(p) * 4 + 2 * t + 2)
                for e in range(2):
                    own.done(eng.tensor_tensor(prod[t][0][:], raw[t][0][:], (cos, sin)[e][:, at], ALU.mult))
                    own.done(eng.tensor_tensor(prod[t][1][:], raw[t][1][:], (sin, cos)[e][:, at], ALU.mult))
                    own.wait()
                    if not num_is(p, 0) and e == 0:
                        eng.wait_ge(qk_lo, 4 * num(p))
                        eng.wait_ge(qk_hi, 4 * num(p))
                    eng.tensor_tensor(rot[t][e][:], prod[t][0][:], prod[t][1][:],
                                      (ALU.subtract, ALU.add)[e]).then_inc(signal, 1)
                    eng.wait_ge(signal, 2 * num(p) + e + 1)

            @block.gpsimd
            def _(pool):
                own = Chain(pool, pool_own)
                pool.wait_ge(consts, 80)

                def step(u):
                    v, p = shift(u, 1), shift(u, -1)
                    if exists(v):
                        self.pool_rs(pool, s, w, s.mv, s.rs, own, s.mv_ready, s.rs_ready, num(v))
                    if exists(p):
                        self.pool_rs(pool, s, w, mv2, rs2, own, mv2_ready, rs2_ready, num(p))
                        rotate(pool, own, 1, p, rot_k)

                over_units(pool, step, own, 6)

            @block.vector
            def _(dve):
                own = Chain(dve, s.own)
                dve.memset(s.Gw[:], 0.0).then_inc(gw_zero, 1)
                dve.wait_ge(gw_zero, 1)
                dve.wait_ge(consts, 80)

                def step(u):
                    v, p = shift(u, 1), shift(u, -1)
                    if exists(v):
                        dve.wait_ge(x_loaded[v[1]], 16 * v[0] + 16)
                        self.dve_stats(dve, own, X[v[1]], s.st, s.mv, s.mv_ready)
                    if exists(p):
                        self.dve_stats(dve, own, s.acc[p[1]], st2, mv2, mv2_ready)
                    if exists(v):
                        if not num_is(v, 0):
                            dve.wait_ge(s.turned, 2 * num(v))
                        self.dve_norm(dve, X[v[1]], s.xn, s.mv, s.rs, s.rs_ready, s.xn_ready, num(v))
                    if exists(p):
                        if not num_is(p, 0):
                            dve.wait_ge(turned2, 2 * num(p))
                        self.dve_norm(dve, s.acc[p[1]], xn2, mv2, rs2, rs2_ready, xn2_ready, num(p))
                    if exists(v):
                        self.dve_lo(dve, s, v)
                    if exists(u):
                        self.dve_combine(dve, s, own, u, 0)
                    if exists(p):
                        for pair in range(2):
                            dve.wait_ge(hi2, 2 * num(p) + pair + 1)
                            a = slice(pair * 2 * P, (pair + 1) * 2 * P)
                            dve.tensor_tensor(x2T[1][:, :, a], self.turned_view(s, 2 + pair),
                                              x2T[0][:, :, a].bitcast(F32), ALU.subtract).then_inc(lo2, 1)
                    if exists(u):
                        self.dve_combine(dve, s, own, u, 1)
                        self.dve_combine(dve, s, own, u, 2)
                    if exists(v):
                        self.dve_router(dve, s, w, own, v)
                        own.done(dve.tensor_copy(s.gates[v[1]][:], s.Gb[:]))
                    if exists(p):
                        if not num_is(p, 0):
                            dve.wait_ge(v_stored, 16 * num(p))
                        for pair in range(2):
                            dve.wait_ge(v_ready, 2 * num(p) + pair + 1)
                            for i in range(2):
                                ins = dve.tensor_tensor(V[:, 2 * pair + i, :], s.psW[:, 2 + pair, i * D:(i + 1) * D],
                                                        bv[:], ALU.add)
                            ins.then_inc(v_out, 1)
                        rotate(dve, own, 0, p, rot_q)
                    if exists(u):
                        self.dve_combine(dve, s, own, u, 3)
                    if exists(p):
                        if not num_is(p, 0):
                            dve.wait_ge(qk_stored, 128 * num(p))
                        for t in range(2):
                            for e in range(2):
                                dve.wait_ge(qk_hi, num(p) * 4 + 2 * t + e + 1)
                                dve.tensor_tensor(parts[t][e][1][:], rot[t][e][:], parts[t][e][0][:].bitcast(F32),
                                                  ALU.subtract).then_inc(qk_lo, 1)
                    if exists(v):
                        if not num_below(v, 2):
                            dve.wait_ge(x1_stored[v[1]], 16 * v[0])
                        self.dve_acc_set(dve, s, v, lambda q: X[q[1]])

                over_units(dve, step, own, DVE_A)

    def pass_b(self):
        nc = self.nc
        with ExitStack() as ctx:
            sb = lambda n, sh, dt=F32: self.sb(ctx, n, sh, dt)
            sem = lambda n: self.sem(ctx, n)
            ROWS, MAXROWS = P, P - 2
            Q = [sb(f"Qop{g}", [P, HG, S], FR) for g in range(GROUPS)]
            K = [sb(f"Kop{g}", [P, HG, S], FR) for g in range(GROUPS)]
            Vraw = sb("Vraw", [P, KT, D])
            V1 = [sb(f"V1{g}", [P, KT, HG, 2 * DK]) for g in range(2)]
            W = [sb(f"W{n}", [P, HG, 512]) for n in range(3)]
            mask = sb("mask", [P, S])
            ident = sb("ident_b", [P, P])
            mx, nm = sb("mx", [P, KT, HG]), sb("nm", [P, KT, HG])
            nh = sb("nh", [P, KT, HG], FR)
            NB = sb("NB", [P, KT, P])
            mT = sb("mT", [2 * HG, S], FR)
            O = [sb(f"O{n}", [P, 512]) for n in range(2)]
            psM = [ctx.enter_context(nc.psum_tensor(f"psM{n}", [P, S], F32)) for n in range(2)]
            psS = [ctx.enter_context(nc.psum_tensor(f"psS{n}", [P, 512], F32)) for n in range(3)]
            psO = ctx.enter_context(nc.psum_tensor("psO", [P, 512], F32))
            qk_loaded = [sem(f"qk_loaded{g}") for g in range(GROUPS)]
            m_loaded = [sem(f"m_loaded{g}") for g in range(GROUPS)]
            o_stored = [sem(f"o_stored{n}") for n in range(2)]
            (v_loaded, v_spread, setup, own_p, scores_m, maxed, nb_ready, m_turned, m_out, scores, exps, kept,
             rows_used, sums_out, own_d) = (sem(n) for n in (
                 "v_loaded", "v_spread", "setup", "own_p", "scores_m", "maxed", "nb_ready", "m_turned", "m_out",
                 "scores", "exps", "kept", "rows_used", "sums_out", "own_d"))

            plan = [(j, kt, max(0, kt - 4 * j) * P, kt >= 4 * j) for j in range(2) for kt in range(4 * j + 4)]
            R = len(plan)
            DIAG = sum(r[3] for r in plan)
            MT = HG * KT
            share = [MT * (r + 1) // R - MT * r // R for r in range(R)]

            def g_of(b, hg):
                return b * GROUPS + hg

            def after(b, hg, by):
                n = hg + by
                return b + n // GROUPS, n % GROUPS

            def there(b):
                return not isinstance(b, int) or 0 <= b < B

            def over_groups(eng, step, chain=None, per_step=0):
                for hg in range(GROUPS):
                    step(0, hg)
                k0 = chain.k if chain else 0
                with eng.Fori(1, B - 1) as b:
                    if chain:
                        chain.base, chain.k = (b - 1) * (GROUPS * per_step) + k0, 0
                    for hg in range(GROUPS):
                        step(b, hg)
                    assert not chain or chain.k == GROUPS * per_step, chain.k
                if chain:
                    chain.base, chain.k = k0 + (B - 2) * GROUPS * per_step, 0
                for hg in range(GROUPS):
                    step(B - 1, hg)

            block = ctx.enter_context(nc.Block())

            @block.sync
            def _(sp):
                def load(b, hg):
                    h = slice(hg * HG, (hg + 1) * HG)
                    for n, part in enumerate((0, 0, 1, 1)):
                        sp.dma_start(Q[hg][16 * n:16 * n + 16].bitcast(F32),
                                     self.qs[b, part, :, h, :]).then_inc(qk_loaded[hg], 16)
                    for n in range(2):
                        sp.dma_start(K[hg][32 * n:32 * n + 32].bitcast(F32),
                                     self.ks[b, :, :, h, :].rearrange("t d h n -> (t d) h n")
                                     ).then_inc(qk_loaded[hg], 16)

                def load_v(b):
                    sp.dma_start(Vraw[:], self.v_v[:, bass.ds(b * KT, KT), :]).then_inc(v_loaded, 16)

                sp.wait_ge(setup, 8)
                load_v(0)
                for hg in range(3):
                    load(0, hg)
                for hg in range(2):
                    for part in range(2):
                        if part == 0:
                            sp.wait_ge(m_out, hg + 1)
                        sp.dma_start(Q[hg][MAXROWS + part:MAXROWS + part + 1].bitcast(F32),
                                     mT[part * HG:(part + 1) * HG, :].bitcast(F32)).then_inc(m_loaded[hg], 16)

                def step(b, hg):
                    b3, g3 = after(b, hg, 3)
                    if there(b3):
                        if not (isinstance(b3, int) and g_of(b3, g3) < GROUPS):
                            sp.wait_ge(rows_used, R * g_of(b, hg))
                        load(b3, g3)
                    if hg == 2 and there(b + 1):
                        sp.wait_ge(v_spread, g_of(b, 3) + 1)
                        load_v(b + 1)
                    for j in range(2):
                        wait_apart(sp, sums_out, 2 * g_of(b, hg) + j + 1)
                        sp.dma_start(self.os[b, hg, :, j * 512:(j + 1) * 512], O[j][:]).then_inc(o_stored[j], 16)
                    b2, g2 = after(b, hg, 2)
                    if there(b2):
                        sp.wait_ge(m_out, g_of(b2, g2) + 1)
                        for part in range(2):
                            sp.dma_start(Q[g2][MAXROWS + part:MAXROWS + part + 1].bitcast(F32),
                                         mT[part * HG:(part + 1) * HG, :].bitcast(F32)).then_inc(m_loaded[g2], 16)

                over_groups(sp, step)
                for j in range(2):
                    sp.wait_ge(o_stored[j], 16 * B * GROUPS)

            @block.gpsimd
            def _(pool):
                own = Chain(pool, own_p)
                own.done(pool.memset(ident[:], 0.0))
                own.done(pool.memset(mask[:], 0.0))
                own.wait()
                own.done(pool.affine_select(out=ident[:], in_=ident[:], compare_op=ALU.not_equal, fill=1.0, base=0,
                                            pattern=[[-1, P]], channel_multiplier=1))
                own.done(pool.affine_select(out=mask[:, S - P:S], in_=mask[:, S - P:S], compare_op=ALU.is_ge,
                                            fill=MASKED, base=0, pattern=[[-1, P]], channel_multiplier=1))
                own.wait()
                for g in range(2):
                    own.done(pool.memset(V1[g][:], 1.0))
                own.done(pool.memset(NB[:], 0.0))
                own.wait()
                pool.drain().then_inc(setup, 1)

                def spread(b, hg):
                    g = g_of(b, hg)
                    wait_apart(pool, v_loaded, 16 * b + 16)
                    if not (isinstance(g, int) and g < 2):
                        wait_apart(pool, rows_used, R * g - R)
                    pool.tensor_copy(V1[hg % 2][:, :, :, 0:DK],
                                     Vraw[:, :, hg * HG * DK:(hg + 1) * HG * DK].rearrange(
                                         "p k (h d) -> p k h d", h=HG)).then_inc(v_spread, 1)

                spread(0, 0)

                def step(b, hg):
                    b1, g1 = after(b, hg, 1)
                    if there(b1):
                        spread(b1, g1)
                    n = 0
                    for r, (j, kt, c0, diag) in enumerate(plan):
                        if diag:
                            row = g_of(b, hg) * R + r
                            wait_apart(pool, exps, HG * (row + 1))
                            Wd = W[r % 3][:, :, c0:c0 + P]
                            pool.affine_select(out=Wd, in_=Wd, compare_op=ALU.is_ge, fill=0.0, base=0,
                                               pattern=[[0, HG], [1, P]], channel_multiplier=-1).then_inc(kept, 1)

                over_groups(pool, step)

            @block.vector
            def _(dve):
                own = Chain(dve, own_d)
                for g in range(GROUPS):
                    own.done(dve.memset(Q[g][64:P].bitcast(F32), 0.0))
                for g in range(GROUPS):
                    own.done(dve.memset(K[g][64:P].bitcast(F32), 1.0))
                own.wait()
                dve.drain().then_inc(setup, 7)
                dve.wait_ge(setup, 8)

                def max_tile(b, hg, t):
                    h, qt = t // KT, t % KT
                    w = (qt + 1) * P
                    n = g_of(b, hg) * MT + t
                    wait_apart(dve, scores_m, n + 1)
                    dve.tensor_tensor_reduce(psM[(t + hg) % 2][:, 0:w], psM[(t + hg) % 2][:, 0:w], mask[:, S - w:S], 1.0, LOWEST,
                                             ALU.add, ALU.max, mx[:, qt, h:h + 1]).then_inc(maxed, 1)

                def negate(b, hg):
                    g = g_of(b, hg)
                    dve.wait_ge(maxed, (g + 1) * MT)
                    own.done(dve.tensor_scalar(nm[:], mx[:], -1.0, None, ALU.mult))
                    own.wait()
                    own.done(dve.tensor_copy(nh[:], nm[:]))
                    own.wait()
                    if not (isinstance(g, int) and g == 0):
                        dve.wait_ge(m_turned, g)
                    own.done(dve.tensor_copy(NB[:, :, 0:HG], nh[:].bitcast(F32)))
                    dve.tensor_tensor(NB[:, :, HG:2 * HG], nm[:], nh[:].bitcast(F32),
                                      ALU.subtract).then_inc(nb_ready, 1)

                for g in range(2):
                    for t in range(MT):
                        max_tile(0, g, t)
                    negate(0, g)

                def step(b, hg):
                    b2, g2 = after(b, hg, 2)
                    t = 0
                    for r, (j, kt, c0, diag) in enumerate(plan):
                        for _ in range(share[r]):
                            if there(b2):
                                max_tile(b2, g2, t)
                                t += 1
                        if r in (4, R - 1):
                            half = 0 if r == 4 else 1
                            g = g_of(b, hg)
                            dve.wait_ge(rows_used, g * R + (4, R)[half])
                            if not (isinstance(g, int) and g == 0):
                                dve.wait_ge(o_stored[half], 16 * g)
                            dve.tensor_copy(O[half][:], psO[:]).then_inc(sums_out, 1)
                    if there(b2):
                        negate(b2, g2)

                over_groups(dve, step, own, 3)

            @block.scalar
            def _(act):
                def m_copy(b, hg):
                    g = g_of(b, hg)
                    act.wait_ge(m_turned, g + 1)
                    if not (isinstance(g, int) and g == 0):
                        pb, pg = after(b, hg, -1)
                        act.wait_ge(m_loaded[pg], 32 * pb + 32)
                    act.activation(mT[:], psM[(MT + hg) % 2][0:2 * HG, :], ACT.Copy).then_inc(m_out, 1)

                for g in range(2):
                    m_copy(0, g)

                def step(b, hg):
                    for r, (j, kt, c0, diag) in enumerate(plan):
                        row = g_of(b, hg) * R + r
                        for h in range(HG):
                            n = row * HG + h
                            act.wait_ge(scores, n + 1)
                            if h == 0 and not (isinstance(row, int) and row < 3):
                                act.wait_ge(rows_used, row - 2)
                            act.activation(W[r % 3][:, h, c0:512], psS[(r * HG + h) % 3][:, c0:512], ACT.Exp,
                                           scale=float(DK) ** -0.5).then_inc(exps, 1)
                    b2, g2 = after(b, hg, 2)
                    if there(b2):
                        m_copy(b2, g2)

                over_groups(act, step)

            @block.tensor
            def _(pe):
                pe.wait_ge(setup, 8)

                def max_tile(b, hg, t):
                    h, qt = t // KT, t % KT
                    g = g_of(b, hg)
                    if t == 0:
                        pe.wait_ge(qk_loaded[hg], 96 * b + 96)
                    if t >= 2:
                        pe.wait_ge(maxed, g * MT + t - 1)
                    elif t == 1 and not (isinstance(g, int) and g == 0):
                        pe.wait_ge(m_out, g)
                    w = (qt + 1) * P
                    for c in range(0, w, 512):
                        n = min(512, max(w - c, 256))
                        ins = pe.matmul(psM[(t + hg) % 2][:, c:c + n], Q[hg][0:MAXROWS, h, qt * P:(qt + 1) * P],
                                        K[hg][0:MAXROWS, h, c:c + n], start=True, stop=True)
                    ins.then_inc(scores_m, 1)

                def turn_maxima(b, hg):
                    pe.wait_ge(nb_ready, g_of(b, hg) + 1)
                    for qt in range(KT):
                        ins = pe.transpose(psM[(MT + hg) % 2][:, qt * P:(qt + 1) * P], NB[:, qt, :], ident[:])
                    ins.then_inc(m_turned, 1)

                for g in range(2):
                    for t in range(MT):
                        max_tile(0, g, t)
                    turn_maxima(0, g)

                def score(b, hg, r, h):
                    j, kt, c0, diag = plan[r]
                    n = (g_of(b, hg) * R + r) * HG + h
                    if not (isinstance(n, int) and n < 3):
                        pe.wait_ge(exps, n - 2)
                    c = min(c0, 256)
                    pe.matmul(psS[(r * HG + h) % 3][:, c:512], K[hg][0:ROWS, h, kt * P:(kt + 1) * P],
                              Q[hg][0:ROWS, h, j * 512 + c:(j + 1) * 512], start=True, stop=True).then_inc(scores, 1)

                def weigh(b, hg, r):
                    j, kt, c0, diag = plan[r]
                    g = g_of(b, hg)
                    if diag:
                        pe.wait_ge(kept, g * DIAG + sum(q[3] for q in plan[:r + 1]))
                    else:
                        pe.wait_ge(exps, (g * R + r + 1) * HG)
                    if r == 0:
                        pe.wait_ge(v_spread, g + 1)
                    if kt == 0 and not (isinstance(g, int) and g == 0 and j == 0):
                        pe.wait_ge(sums_out, 2 * g + j)
                    last = kt == 4 * j + 3
                    for h in range(HG):
                        ins = pe.matmul(psO[32 * h:32 * h + 32, c0:512], V1[hg % 2][:, kt, h, :],
                                        W[r % 3][:, h, c0:512], start=(kt == 0), stop=last)
                    ins.then_inc(rows_used, 1)

                def step(b, hg):
                    g = g_of(b, hg)
                    b2, g2 = after(b, hg, 2)
                    pe.wait_ge(m_loaded[hg], 32 * b + 32)
                    t = 0
                    for r in range(R):
                        for h in range(2):
                            score(b, hg, r, h)
                        for k in range(share[r]):
                            if k == 1 and r:
                                weigh(b, hg, r - 1)
                            if k == 1:
                                score(b, hg, r, 2)
                            if there(b2):
                                max_tile(b2, g2, t)
                                t += 1
                        score(b, hg, r, 3)
                    weigh(b, hg, R - 1)
                    if there(b2):
                        turn_maxima(b2, g2)

                over_groups(pe, step)

    def pass_c(self):
        nc = self.nc
        with ExitStack() as ctx:
            w = self.weights(ctx, "c", ["Wo"])
            s = self.ffn_state(ctx, "c")
            sb = lambda n, sh, dt=F32: self.sb(ctx, n, sh, dt)
            sem = lambda n: self.sem(ctx, n)
            s.gates = [sb(f"gates_c{h}", [P, TILES, E]) for h in range(2)]
            X1 = [sb(f"X1{h}", [P, TILES, D]) for h in range(2)]
            OT = [sb(f"OT{h}", [P, GROUPS, UNIT]) for h in range(2)]
            attn, rc = sb("attn", [P, TILES, D]), sb("rc", [P, TILES, H])
            aT = [sb(f"aT{k}", [P, KC, UNIT], FR) for k in range(2)]
            bo = sb("bo", [P, D])
            x1_loaded = [sem(f"x1_loaded{h}") for h in range(2)]
            o_loaded = [sem(f"o_loaded{h}") for h in range(2)]
            out_stored = [sem(f"out_stored{h}") for h in range(2)]
            (bo_loaded, o_turned, attn_ready, a_turned, a_hi, a_lo, proj, x2_ready, x1_biased, pool_own, gw_zero) = (
                sem(n) for n in ("bo_loaded", "o_turned", "attn_ready", "a_turned", "a_hi", "a_lo", "proj",
                                 "x2_ready", "x1_biased", "pool_own_c", "gw_zero_c"))
            block = ctx.enter_context(nc.Block())

            @block.sync
            def _(sp):
                sp.dma_start(bo[:], self.bo.partition_broadcast(P)).then_inc(bo_loaded, 16)

                def load(v):
                    sp.dma_start(X1[v[1]][:], rows(self.x1_v, v)).then_inc(x1_loaded[v[1]], 16)
                    sp.dma_start(OT[v[1]][:], self.os[v[0], :, :, v[1] * UNIT:(v[1] + 1) * UNIT].rearrange(
                        "g p n -> p g n")).then_inc(o_loaded[v[1]], 16)

                load((0, 0))

                def step(u):
                    v = shift(u, 3)
                    if exists(v):
                        if not num_below(v, 2):
                            wait_apart(sp, s.acc_set, 2 * num(v) - 2)
                            wait_apart(sp, o_turned, TILES * (num(v) - 1))
                        load(v)
                    if exists(u):
                        sp.wait_ge(s.combined, 16 * num(u) + 16)
                        sp.dma_start(rows(self.out_v, u), s.acc[u[1]][:]).then_inc(out_stored[u[1]], 16)

                over_units(sp, step)
                for h in range(2):
                    sp.wait_ge(out_stored[h], 16 * UNITS // 2)

            @block.tensor
            def _(pe):
                def step(u):
                    v, n = shift(u, 1), shift(u, 2)
                    if exists(u):
                        self.pe_experts(pe, s, w, u, 0)
                    if exists(v):
                        self.pe_turn_unit(pe, s, w, v)
                    if exists(n):
                        pe.wait_ge(o_loaded[n[1]], 16 * n[0] + 16)
                        for i in range(TILES):
                            if i < 2 and not num_is(n, 0):
                                pe.wait_ge(x2_ready, 2 * num(n) - 1 + i)
                            if i >= 2:
                                pe.wait_ge(attn_ready, TILES * num(n) + i - 1)
                            for g in range(GROUPS):
                                ins = pe.transpose(s.psW[:, 2 + i % 2, g * P:(g + 1) * P],
                                                   OT[n[1]][:, g, i * P:(i + 1) * P], w["ident"][:])
                            ins.then_inc(o_turned, 1)
                            if i == 1 and exists(u):
                                self.pe_experts(pe, s, w, u, 1)
                    elif exists(u):
                        self.pe_experts(pe, s, w, u, 1)
                    if exists(v):
                        self.pe_router(pe, s, w, v)
                    if exists(u):
                        self.pe_experts(pe, s, w, u, 2)
                    if exists(v):
                        self.pe_logits(pe, s, w, v)
                    if exists(n):
                        pe.wait_ge(attn_ready, TILES * num(n) + 4)
                        for pair in range(2):
                            self.turn(pe, s, w, attn, 2 + pair, pair, a_turned)
                    if exists(v):
                        self.pe_gates(pe, s, w, v)
                    if exists(u):
                        self.pe_experts(pe, s, w, u, 3)
                    if exists(n):
                        pe.wait_ge(a_hi, 2 * num(n) + 2)
                        pe.wait_ge(a_lo, 2 * num(n) + 2)
                        for pair in range(2):
                            for i in range(2):
                                t = 2 * pair + i
                                ins = self.three(pe, s.psW[:, 2 + pair, i * D:(i + 1) * D],
                                                 lambda a, k: aT[a][:, k, t * P:(t + 1) * P],
                                                 lambda a, k: w["Wo"][a][:, k, :])
                            ins.then_inc(proj, 1)
                    if exists(v):
                        self.pe_bias(pe, s, w, v)

                over_units(pe, step)

            @block.scalar
            def _(act):
                def step(u):
                    v, n = shift(u, 1), shift(u, 2)
                    if exists(v):
                        self.act_hi(act, s, v)
                        self.act_router(act, s, v)
                    if exists(n):
                        for pair in range(2):
                            act.wait_ge(a_turned, 2 * num(n) + pair + 1)
                            act.activation(aT[0][:, :, pair * 2 * P:(pair + 1) * 2 * P],
                                           self.turned_view(s, 2 + pair), ACT.Copy).then_inc(a_hi, 1)
                    if exists(v):
                        self.act_gates(act, s, v)

                over_units(act, step)

            @block.gpsimd
            def _(pool):
                own = Chain(pool, pool_own)
                pool.wait_ge(bo_loaded, 16)

                def step(u):
                    v, n = shift(u, 1), shift(u, 2)
                    if exists(v):
                        self.pool_rs(pool, s, w, s.mv, s.rs, own, s.mv_ready, s.rs_ready, num(v))
                    if exists(n):
                        pool.wait_ge(x1_loaded[n[1]], 16 * n[0] + 16)
                        for i in range(TILES):
                            ins = pool.tensor_tensor(X1[n[1]][:, i, :], X1[n[1]][:, i, :], bo[:], ALU.add)
                        ins.then_inc(x1_biased, 1)

                over_units(pool, step, own, 1)

            @block.vector
            def _(dve):
                own = Chain(dve, s.own)
                dve.memset(s.Gw[:], 0.0).then_inc(gw_zero, 1)
                dve.wait_ge(gw_zero, 1)

                def attend(n, i):
                    dve.wait_ge(o_turned, TILES * num(n) + i + 1)
                    if i == 0 and not num_is(n, 0):
                        dve.wait_ge(a_turned, 2 * num(n))
                    ps = s.psW[:, 2 + i % 2, :].rearrange("p (h d) -> p h d", d=2 * DK)
                    own.done(dve.reciprocal(rc[:, i, :], ps[:, :, DK]))
                    own.wait()
                    dve.tensor_tensor(attn[:, i, :].rearrange("p (h d) -> p h d", d=DK), ps[:, :, 0:DK],
                                      rc[:, i, :].unsqueeze(2).to_broadcast([P, H, DK]),
                                      ALU.mult).then_inc(attn_ready, 1)

                def step(u):
                    v, n = shift(u, 1), shift(u, 2)
                    if exists(v):
                        dve.wait_ge(x2_ready, 2 * num(v) + 2)
                        self.dve_stats(dve, own, X1[v[1]], s.st, s.mv, s.mv_ready)
                        if not num_is(v, 0):
                            dve.wait_ge(s.turned, 2 * num(v))
                        self.dve_norm(dve, X1[v[1]], s.xn, s.mv, s.rs, s.rs_ready, s.xn_ready, num(v))
                        self.dve_lo(dve, s, v)
                    if exists(n):
                        attend(n, 0)
                        attend(n, 1)
                    if exists(u):
                        self.dve_combine(dve, s, own, u, 0)
                        self.dve_combine(dve, s, own, u, 1)
                    if exists(n):
                        attend(n, 2)
                        attend(n, 3)
                    if exists(u):
                        self.dve_combine(dve, s, own, u, 2)
                    if exists(v):
                        self.dve_router(dve, s, w, own, v)
                        own.done(dve.tensor_copy(s.gates[v[1]][:], s.Gb[:]))
                    if exists(n):
                        for pair in range(2):
                            dve.wait_ge(a_hi, 2 * num(n) + pair + 1)
                            a = slice(pair * 2 * P, (pair + 1) * 2 * P)
                            dve.tensor_tensor(aT[1][:, :, a], self.turned_view(s, 2 + pair),
                                              aT[0][:, :, a].bitcast(F32), ALU.subtract).then_inc(a_lo, 1)
                    if exists(u):
                        self.dve_combine(dve, s, own, u, 3)
                    if exists(n):
                        dve.wait_ge(x1_biased, num(n) + 1)
                        for pair in range(2):
                            dve.wait_ge(proj, 2 * num(n) + pair + 1)
                            t = slice(2 * pair, 2 * pair + 2)
                            dve.tensor_tensor(X1[n[1]][:, t, :],
                                              s.psW[:, 2 + pair, :].rearrange("p (i n) -> p i n", i=2),
                                              X1[n[1]][:, t, :], ALU.add).then_inc(x2_ready, 1)
                    if exists(v):
                        if not num_below(v, 2):
                            dve.wait_ge(out_stored[v[1]], 16 * v[0])
                        self.dve_acc_set(dve, s, v, lambda q: X1[q[1]])

                over_units(dve, step, own, DVE_C)


def num_is(unit, n):
    return isinstance(unit[0], int) and num(unit) == n


def num_below(unit, n):
    return isinstance(unit[0], int) and num(unit) < n


DVE_A = 4 + 4 + 4 * 4 + (8 + 1 + 3 + 8 + 1 + 1 + 2) + 1 + 4
DVE_C = 4 + 4 + 4 * 4 + (8 + 1 + 3 + 8 + 1 + 1 + 2) + 1


def macaron_kernel(nc, *args):
    k = Kernel(nc, args)
    k.pass_a()
    k.pass_b()
    k.pass_c()


_INS = ["L0_attn_x", "L0_attn_Wq", "L0_attn_bq", "L0_attn_Wk", "L0_attn_bk", "L0_attn_Wv", "L0_attn_bv",
        "L0_attn_Wo", "L0_attn_bo", "L0_ffn_Wg", "L0_ffn_We", "L0_ffn_be"]


def rope_tables():
    freq = (np.float32(1.0) / np.float32(THETA) ** (np.arange(0, DK, 2, dtype=np.float32) / np.float32(DK)))
    angle = freq.astype(np.float32)[:, None] * np.arange(S, dtype=np.float32)[None, :]
    return [np.ascontiguousarray(np.tile(f(angle).astype(np.float32), (H, 1))) for f in (np.cos, np.sin)]


def kernel(**inputs):
    import concourse.bacc as _bacc
    from concourse.bass_utils import run_bass_kernel_spmd as _run

    nc = _bacc.Bacc("TRN2", target_bir_lowering=False, num_devices=1)
    arrays, args = {}, []
    given = [(n, np.ascontiguousarray(inputs[n])) for n in _INS]
    given += list(zip(("rope_cos", "rope_sin"), rope_tables()))
    for name, a in given:
        arrays[f"in_{name}_dram"] = a
        args.append(nc.dram_tensor(f"in_{name}_dram", a.shape, mybir.dt.from_np(a.dtype), kind="ExternalInput").ap())
    args.append(nc.dram_tensor("out_0_dram", (B, S, D), F32, kind="ExternalOutput").ap())
    macaron_kernel(nc, *args)
    r = _run(nc, [arrays], core_ids=[0])
    return r.results[0]["out_0_dram"]
```

```python
from contextlib import ExitStack

import numpy as np

import concourse.bass as bass
from concourse import mybir

F32 = mybir.dt.float32
FR = mybir.dt.float32r
BF16 = mybir.dt.bfloat16
U32 = mybir.dt.uint32
ALU = mybir.AluOpType
ACT = mybir.ActivationFunctionType

P = 128
B, S, D = 16, 1024, 256
H, DK, E = 16, 16, 8
KC = D // P
UNIT = 512
TILES = UNIT // P
UNITS = B * S // UNIT
HG = 4
GROUPS = H // HG
KT = S // P
EPS = 1e-5
THETA = 10000.0
MASKED = -1e30
LOWEST = -3e38


class Chain:

    def __init__(self, eng, sem):
        self.eng, self.sem, self.base, self.k = eng, sem, 0, 0

    def done(self, ins):
        ins.then_inc(self.sem, 1)
        self.k += 1
        return self.base + self.k

    def wait(self, at=None):
        self.eng.wait_ge(self.sem, self.base + self.k if at is None else at)

    def wait_apart(self):
        wait_apart(self.eng, self.sem, self.base + self.k)


def wait_apart(eng, sem, value):
    if not isinstance(value, int):
        eng.wait_ge(sem, value)
        eng.nop(nofuse=True)
    else:
        eng.wait_ge(sem, value)


def over_units(eng, step, chain=None, per_step=0, first=0, last=UNITS - 1):
    def at(u):
        return (u // 2, u % 2)

    def count(n):
        if chain is not None:
            assert chain.k == per_step * n, f"steps per unit: {chain.k} for {n}"

    for u in (-2, -1, 0, 1):
        step(at(u))
    k0 = chain.k if chain else 0
    with eng.Fori(1, UNITS // 2 - 2) as b:
        if chain:
            chain.base, chain.k = (b - 1) * (2 * per_step) + k0, 0
        step((b, 0))
        step((b, 1))
        count(2)
    if chain:
        chain.base, chain.k = k0 + (UNITS // 2 - 3) * 2 * per_step, 0
    for u in range(UNITS - 4, UNITS + 1):
        step(at(u))


def shift(unit, by):
    b, h = unit
    n = h + by
    return (b + n // 2, n % 2)


def num(unit):
    return unit[0] * 2 + unit[1]


def exists(unit):
    b = unit[0]
    return not isinstance(b, int) or 0 <= b < B


def rows(ap, unit):
    return ap[:, bass.ds(num(unit) * TILES, TILES), :]


class State:
    pass


LAG = 2
TURN_AT = 6
SLOTS = 4
BANKS = 4


def max_ring():
    ring, pos = {}, 0
    for t in range(HG * KT):
        if t == TURN_AT:
            ring["turn"] = (pos, 2)
            pos += 2
        size = 1 if t % KT < 4 else 2
        ring[t] = (pos, size)
        pos += size
    assert all(p % size == 0 for p, size in ring.values())
    return ring, pos


def interleave(plan):
    R, hop = len(plan), 250
    ring, length = max_ring()
    scores = [(r, h) for r in range(R) for h in range(HG)]
    weighs = [(r - LAG) % R for r in range(R)]
    free = [0.0] * BANKS
    exp_done = [0.0] * len(scores)
    row_ready = [0.0] * R
    used = [0.0] * R
    pe = dve = act = pool = 0.0
    for group in range(3):
        order, si, wi, items = [], 0, 0, list(ring)
        base = length * group
        negated = dve + 4 * 150
        while si < len(scores) or wi < R or items:
            can = []
            if items:
                p, size = ring[items[0]]
                at = max(free[(base + p + k) % BANKS] for k in range(size))
                can.append((max(pe, at, negated if items[0] == "turn" else 0), 0, "max"))
            if si < len(scores) and (si // HG < LAG or si // HG - (SLOTS - LAG) < wi):
                can.append((max(pe, exp_done[si - 3]), 1, "score"))
            if wi < R and (wi < LAG or (wi - LAG) * HG + HG <= si):
                can.append((max(pe, row_ready[weighs[wi]]), 2, "weigh"))
            start, _, kind = min(can)
            if kind == "max":
                item = items.pop(0)
                p, size = ring[item]
                if item == "turn":
                    order.append(("turn", 0, 0))
                    pe = start + 860
                    act = done = max(act, pe + hop) + 900
                else:
                    order.append(("max", 0, item))
                    width = (item % KT + 1) * P
                    pe = start + max(width, 256) * 0.42
                    dve = done = max(dve, pe + hop) + width * 1.05 + 70
                for k in range(size):
                    free[(base + p + k) % BANKS] = done + hop
            elif kind == "score":
                r, h = scores[si]
                c0 = plan[r][2]
                order.append(("score", r, h))
                pe = start + (512 - min(c0, 256)) * 0.42
                act = max(act, pe + hop, used[(r - SLOTS) % R]) + (512 - c0) * 0.83 + 60
                exp_done[si] = act + hop
                if h == HG - 1:
                    row_ready[r] = act + hop
                    if plan[r][3]:
                        pool = max(pool, act + hop) + 700
                        row_ready[r] = pool + hop
                si += 1
            else:
                r = weighs[wi]
                order.append(("weigh", r, 0))
                pe = start + HG * (512 - plan[r][2]) * 0.45
                used[r] = pe + hop
                if r in (3, R - 1):
                    dve = max(dve, pe + hop) + 600
                wi += 1
    return order


class Kernel:
    def __init__(self, nc, args):
        self.nc = nc
        (self.x, self.Wq, self.bq, self.Wk, self.bk, self.Wv, self.bv, self.Wo, self.bo,
         self.Wg, self.We, self.be, self.cos, self.sin, self.out) = args
        nt = "(n p) d -> p n d"
        self.x_v = self.x.rearrange("b s d -> (b s) d").rearrange(nt, p=P)
        self.out_v = self.out.rearrange("b s d -> (b s) d").rearrange(nt, p=P)
        self.x1_v = nc.dram_tensor("x1", (B * S, D), F32, kind="Internal").ap().rearrange(nt, p=P)
        v = nc.dram_tensor("v", (B * S, D), F32, kind="Internal").ap()
        self.v_v = v.rearrange(nt, p=P)
        self.qs = nc.dram_tensor("q_split", (B, 2, DK, H, S), F32, kind="Internal").ap()
        self.ks = nc.dram_tensor("k_split", (B, 2, DK, H, S), F32, kind="Internal").ap()
        self.os = nc.dram_tensor("o_sums", (B, GROUPS, P, S), F32, kind="Internal").ap()
        self.nsem = 0

    def sem(self, ctx, name):
        self.nsem += 1
        return ctx.enter_context(self.nc.semaphore(name))

    def sb(self, ctx, name, shape, dt=F32):
        return ctx.enter_context(self.nc.sbuf_tensor(name, shape, dt))

    def weights(self, ctx, tag, squares):
        nc = self.nc
        w = {}
        sb = lambda n, s, dt=F32: self.sb(ctx, f"{n}_{tag}", s, dt)
        w["ident"] = sb("ident", [P, P])
        w["We"] = [sb(f"We{k}", [P, KC, E * D], FR) for k in range(2)]
        w["Wg"] = [sb(f"Wg{k}", [P, KC, P], FR) for k in range(2)]
        w["be"] = sb("be", [P, D], FR)
        w["iota"] = sb("iota", [P, E])
        w["nhalf"] = sb("nhalf", [P, TILES])
        for name in squares:
            w[name] = [sb(f"{name}{k}", [P, KC, D], FR) for k in range(2)]
        with ExitStack() as tmp:
            raw = self.sb(tmp, f"raw_{tag}", [P, KC, E * D])
            rawg = self.sb(tmp, f"rawg_{tag}", [P, KC, E])
            rawb = self.sb(tmp, f"rawb_{tag}", [P, D])
            rawi = self.sb(tmp, f"rawi_{tag}", [P, E], mybir.dt.int32)
            sq = self.sb(tmp, f"sq_{tag}", [P, max(1, len(squares)), KC, D])
            ps = tmp.enter_context(nc.psum_tensor(f"ps_{tag}", [P, 4, 512], F32))
            s_ld, s_ldg, s_ldb, s_lds, s_id, s_set, s_tr, s_own = (
                self.sem(ctx, f"{n}_{tag}") for n in
                ("w_loaded", "wg_loaded", "be_loaded", "sq_loaded", "ident_set", "zeros_set", "sq_turned", "w_own"))
            with nc.Block() as block:
                @block.sync
                def _(sp):
                    for e in range(E):
                        sp.dma_start(raw[:, :, e * D:(e + 1) * D],
                                     self.We[e].rearrange("(k p) n -> p k n", p=P)).then_inc(s_ld, 16)
                    sp.dma_start(rawg[:], self.Wg.rearrange("(k p) e -> p k e", p=P)).then_inc(s_ldg, 16)
                    for n in range(3):
                        sp.dma_start(rawb[32 * n:32 * n + E, :], self.be).then_inc(s_ldb, 16)
                    for n, name in enumerate(squares):
                        src = {"Wq": self.Wq, "Wk": self.Wk, "Wv": self.Wv, "Wo": self.Wo}[name]
                        sp.dma_start(sq[:, n], src.rearrange("(k p) n -> p k n", p=P)).then_inc(s_lds, 16)

                @block.gpsimd
                def _(pool):
                    pool.memset(w["ident"][:], 0.0).then_inc(s_id, 1)
                    pool.wait_ge(s_id, 1)
                    pool.affine_select(out=w["ident"][:], in_=w["ident"][:], compare_op=ALU.not_equal, fill=1.0,
                                       base=0, pattern=[[-1, P]], channel_multiplier=1).then_inc(s_id, 1)
                    pool.iota(rawi[:], pattern=[[1, E]], base=0, channel_multiplier=0).then_inc(s_id, 1)
                    pool.wait_ge(s_id, 3)
                    pool.tensor_copy(w["iota"][:], rawi[:]).then_inc(s_id, 1)
                    pool.memset(w["nhalf"][:], -0.5).then_inc(s_id, 1)

                @block.tensor
                def _(pe):
                    pe.wait_ge(s_id, 2)
                    if squares:
                        pe.wait_ge(s_lds, 16 * len(squares))
                    for n in range(len(squares)):
                        for ki in range(KC):
                            for ko in range(KC):
                                ins = pe.transpose(ps[:, n, ki * D + ko * P:ki * D + (ko + 1) * P],
                                                   sq[:, n, ko, ki * P:(ki + 1) * P], w["ident"][:])
                        ins.then_inc(s_tr, 1)

                @block.vector
                def _(dve):
                    own = Chain(dve, s_own)

                    def split(hi, lo, src):
                        own.done(dve.tensor_copy(hi, src))
                        own.wait()
                        own.done(dve.tensor_tensor(lo, src, hi.bitcast(F32), ALU.subtract))

                    dve.memset(w["be"][:].bitcast(F32), 0.0).then_inc(s_set, 1)
                    for k in range(2):
                        dve.memset(w["Wg"][k][:].bitcast(F32), 0.0).then_inc(s_set, 1)
                    dve.wait_ge(s_set, 3)
                    dve.wait_ge(s_ld, 16 * E)
                    for k in range(KC):
                        split(w["We"][0][:, k], w["We"][1][:, k], raw[:, k])
                    dve.wait_ge(s_ldg, 16)
                    split(w["Wg"][0][:, :, 0:E], w["Wg"][1][:, :, 0:E], rawg[:])
                    dve.wait_ge(s_ldb, 48)
                    for n in range(3):
                        a = slice(32 * n, 32 * n + E)
                        own.done(dve.tensor_copy(w["be"][a, :], rawb[a, :]))
                    own.wait()
                    own.done(dve.tensor_tensor(w["be"][64:64 + E, :], rawb[64:64 + E, :],
                                               w["be"][64:64 + E, :].bitcast(F32), ALU.subtract))
                    for n, name in enumerate(squares):
                        dve.wait_ge(s_tr, n + 1)
                        split(w[name][0][:].rearrange("p k n -> p (k n)"),
                              w[name][1][:].rearrange("p k n -> p (k n)"), ps[:, n, :])
                    own.wait()
        return w

    def ffn_state(self, ctx, tag):
        s = State()
        sb = lambda n, sh, dt=F32: self.sb(ctx, f"{n}_{tag}", sh, dt)
        s.ln = self.layernorm_state(ctx, tag)
        s.xT = [[sb(f"xT{h}{k}", [P, KC, UNIT], FR) for k in range(2)] for h in range(2)]
        s.lT = sb("lT", [P, UNIT])
        s.m8, s.i8 = sb("m8", [P, TILES, 8]), sb("i8", [P, TILES, 8], U32)
        s.top = sb("top", [P, TILES, 2])
        s.d, s.e2, s.den = (sb(n, [P, TILES]) for n in ("gap", "e2", "den"))
        s.g = sb("g", [P, TILES, 2])
        s.hot, s.G = sb("hot", [P, TILES, 2, E]), sb("G", [P, TILES, 2, E])
        s.gates = [sb(f"gates{h}", [P, TILES, E]) for h in range(2)]
        s.odd = [sb(f"odd{h}", [P, TILES, D]) for h in range(2)]
        s.Gh = sb("Gh", [P, TILES, E], FR)
        s.Gw = sb("Gw", [P, TILES, P])
        s.GT = sb("GT", [P, UNIT], FR)
        s.acc = [sb(f"acc{h}", [P, TILES, D]) for h in range(2)]
        psum = lambda n, sh: ctx.enter_context(self.nc.psum_tensor(f"{n}_{tag}", sh, F32))
        s.psE = psum("psE", [P, 4, 512])
        s.psW = psum("psW", [P, 4, 512])
        s.turned = self.sem(ctx, f"turned_{tag}")
        s.hi_ready = self.sem(ctx, f"hi_ready_{tag}")
        s.lo_ready = self.sem(ctx, f"lo_ready_{tag}")
        s.logitsT = self.sem(ctx, f"logitsT_{tag}")
        s.logitsT_out = self.sem(ctx, f"logitsT_out_{tag}")
        s.logits = self.sem(ctx, f"logits_{tag}")
        s.gap_ready = self.sem(ctx, f"gap_ready_{tag}")
        s.e2_ready = self.sem(ctx, f"e2_ready_{tag}")
        s.gates_ready = self.sem(ctx, f"gates_ready_{tag}")
        s.gates_turned = self.sem(ctx, f"gates_turned_{tag}")
        s.gates_out = self.sem(ctx, f"gates_out_{tag}")
        s.bias_ready = self.sem(ctx, f"bias_ready_{tag}")
        s.acc_set = self.sem(ctx, f"acc_set_{tag}")
        s.experts = self.sem(ctx, f"experts_{tag}")
        s.combined = self.sem(ctx, f"combined_{tag}")
        s.summed = self.sem(ctx, f"summed_{tag}")
        s.own = self.sem(ctx, f"own_{tag}")
        return s

    def turn(self, pe, s, w, src, bank, pair, signal):
        for i in range(2):
            for k in range(KC):
                ins = pe.transpose(s.psW[:, bank, (k * 2 + i) * P:(k * 2 + i + 1) * P],
                                   src[:, 2 * pair + i, k * P:(k + 1) * P], w["ident"][:])
        ins.then_inc(signal, 1)

    def turned_view(self, s, bank):
        return s.psW[:, bank, :].rearrange("p (k n) -> p k n", k=KC)

    def three(self, pe, out, stationary, moving, first=True, last=True):
        n, total = 0, 3 * KC
        for k in range(KC):
            for a, b in ((0, 0), (0, 1), (1, 0)):
                ins = pe.matmul(out, stationary(a, k), moving(b, k), start=(n == 0), stop=(n == total - 1))
                n += 1
        return ins

    def pe_experts(self, pe, s, w, unit, i, half):
        xT = s.xT[unit[1]]
        for c in (2 * half, 2 * half + 1):
            tile = num(unit) * TILES + i
            if not (isinstance(tile, int) and tile == 0):
                pe.wait_ge(s.combined, (tile - 1) * 4 + c + 1)
            self.three(pe, s.psE[:, c, :], lambda a, k: xT[a][:, k, i * P:(i + 1) * P],
                       lambda a, k: w["We"][a][:, k, c * 512:(c + 1) * 512]).then_inc(s.experts, 1)

    def pe_turn_unit(self, pe, s, w, v):
        pe.wait_ge(s.ln.xn_ready, num(v) + 1)
        for pair in range(2):
            if not (isinstance(v[0], int) and num(v) == 0):
                pe.wait_ge(s.acc_set, 2 * num(v))
            self.turn(pe, s, w, s.ln.xn, pair, pair, s.turned)

    def pe_router(self, pe, s, w, v):
        pe.wait_ge(s.hi_ready, 2 * num(v) + 2)
        pe.wait_ge(s.lo_ready, 2 * num(v) + 2)
        xT = s.xT[v[1]]
        self.three(pe, s.psW[:, 0, :], lambda a, k: w["Wg"][a][:, k, :],
                   lambda a, k: xT[a][:, k, :]).then_inc(s.logitsT, 1)

    def pe_logits(self, pe, s, w, v):
        pe.wait_ge(s.logitsT_out, num(v) + 1)
        for i in range(TILES):
            ins = pe.transpose(s.psW[:, 1, i * P:(i + 1) * P], s.lT[:, i * P:(i + 1) * P], w["ident"][:])
        ins.then_inc(s.logits, 1)

    def pe_gates(self, pe, s, w, v):
        pe.wait_ge(s.gates_ready, num(v) + 1)
        for i in range(TILES):
            ins = pe.transpose(s.psW[:, 0, i * P:(i + 1) * P], s.Gw[:, i, :], w["ident"][:])
        ins.then_inc(s.gates_turned, 1)

    def pe_bias(self, pe, s, w, v):
        pe.wait_ge(s.gates_out, num(v) + 1)
        for pair in range(2):
            for i in range(2):
                t = 2 * pair + i
                ins = pe.matmul(s.psW[:, 1 - pair, i * D:(i + 1) * D], s.GT[:, t * P:(t + 1) * P], w["be"][:],
                                start=(i == 0), stop=True, skip_group_check=True)
            ins.then_inc(s.bias_ready, 1)

    def act_hi(self, act, s, v):
        for pair in range(2):
            act.wait_ge(s.turned, 2 * num(v) + pair + 1)
            act.activation(s.xT[v[1]][0][:, :, pair * 2 * P:(pair + 1) * 2 * P],
                           self.turned_view(s, pair), ACT.Copy).then_inc(s.hi_ready, 1)

    def act_router(self, act, s, v):
        act.wait_ge(s.logitsT, num(v) + 1)
        act.activation(s.lT[:], s.psW[:, 0, :], ACT.Copy).then_inc(s.logitsT_out, 1)
        
    def act_gap(self, act, s, v):
        act.wait_ge(s.gap_ready, num(v) + 1)
        act.activation(s.e2[:], s.d[:], ACT.Exp).then_inc(s.e2_ready, 1)

    def act_gates(self, act, s, v):
        act.wait_ge(s.gates_turned, num(v) + 1)
        act.activation(s.GT[:], s.psW[:, 0, :], ACT.Copy).then_inc(s.gates_out, 1)

    def dve_stats(self, dve, own, src, ln):
        for i in range(TILES):
            own.done(dve.bn_stats(ln.st[:, i, :], src[:, i, :]))
        own.wait_apart()
        for i in range(TILES):
            ins = dve.bn_aggr(ln.mv[:, i, :], ln.st[:, i, :])
        ins.then_inc(ln.mv_ready, 1)

    def pool_rs(self, pool, w, ln, own, n):
        wait_apart(pool, ln.mv_ready, n + 1)
        own.done(pool.tensor_scalar(ln.ve[:], ln.mv[:, :, 1], EPS, None, ALU.add))
        own.done(pool.tensor_scalar(ln.nm[:], ln.mv[:, :, 0], -1.0, None, ALU.mult))
        own.wait()
        own.done(pool.tensor_tensor(ln.rs[:], ln.ve[:], w["nhalf"][:], ALU.pow))
        own.wait()
        pool.tensor_tensor(ln.nb[:], ln.nm[:], ln.rs[:], ALU.mult).then_inc(ln.rs_ready, 1)

    def act_norm(self, act, ln, src, n):
        act.wait_ge(ln.rs_ready, n + 1)
        for i in range(TILES):
            ins = act.activation(ln.xn[:, i, :], src[:, i, :], ACT.Identity, scale=ln.rs[:, i:i + 1],
                                 bias=ln.nb[:, i:i + 1])
        ins.then_inc(ln.xn_ready, 1)

    def layernorm_state(self, ctx, tag):
        ln = State()
        sb = lambda n, sh: self.sb(ctx, f"{n}_{tag}", sh)
        ln.st, ln.mv = sb("st", [P, TILES, 6]), sb("mv", [P, TILES, 2])
        ln.ve, ln.nm, ln.rs, ln.nb = (sb(n, [P, TILES]) for n in ("ve", "nmean", "rs", "nb"))
        ln.xn = sb("xn", [P, TILES, D])
        ln.mv_ready = self.sem(ctx, f"mv_ready_{tag}")
        ln.rs_ready = self.sem(ctx, f"rs_ready_{tag}")
        ln.xn_ready = self.sem(ctx, f"xn_ready_{tag}")
        return ln

    def dve_lo(self, dve, s, v):
        for pair in range(2):
            dve.wait_ge(s.hi_ready, 2 * num(v) + pair + 1)
            a = slice(pair * 2 * P, (pair + 1) * 2 * P)
            dve.tensor_tensor(s.xT[v[1]][1][:, :, a], self.turned_view(s, pair),
                              s.xT[v[1]][0][:, :, a].bitcast(F32), ALU.subtract).then_inc(s.lo_ready, 1)

    def dve_router(self, dve, s, w, own, v):
        wait_apart(dve, s.logits, num(v) + 1)
        L = s.psW[:, 1, :].rearrange("p (i n) -> p i n", i=TILES)
        for i in range(TILES):
            own.done(dve.max(s.m8[:, i, :], L[:, i, 0:E]))
        own.wait_apart()
        for i in range(TILES):
            own.done(dve.max_index(s.i8[:, i, :], s.m8[:, i, :], L[:, i, 0:E]))
        dve.tensor_tensor(s.d[:], s.m8[:, :, 1], s.m8[:, :, 0], ALU.subtract).then_inc(s.gap_ready, 1)
        own.wait()
        own.done(dve.tensor_copy(s.top[:], s.i8[:, :, 0:2]))
        dve.wait_ge(s.e2_ready, num(v) + 1)
        own.done(dve.tensor_scalar(s.den[:], s.e2[:], 2.0, 2.0, ALU.mult, ALU.add))
        own.wait()
        own.done(dve.reciprocal(s.g[:, :, 0], s.den[:]))
        own.wait()
        own.done(dve.tensor_tensor(s.g[:, :, 1], s.e2[:], s.g[:, :, 0], ALU.mult))
        wide = [P, TILES, 2, E]
        own.done(dve.tensor_tensor(s.hot[:], w["iota"][:].unsqueeze(1).unsqueeze(1).to_broadcast(wide),
                                   s.top[:].unsqueeze(3).to_broadcast(wide), ALU.is_equal))
        own.wait()
        own.done(dve.tensor_tensor(s.G[:], s.hot[:], s.g[:].unsqueeze(3).to_broadcast(wide), ALU.mult))
        own.wait()
        gates = s.gates[v[1]]
        own.done(dve.tensor_tensor(gates[:], s.G[:, :, 0, :], s.G[:, :, 1, :], ALU.add))
        own.wait()
        own.done(dve.tensor_copy(s.Gh[:], gates[:]))
        own.wait()
        own.done(dve.tensor_copy(s.Gw[:, :, 0:E], s.Gh[:].bitcast(F32)))
        own.done(dve.tensor_copy(s.Gw[:, :, 64:64 + E], s.Gh[:].bitcast(F32)))
        dve.tensor_tensor(s.Gw[:, :, 32:32 + E], gates[:], s.Gh[:].bitcast(F32),
                          ALU.subtract).then_inc(s.gates_ready, 1)

    def dve_acc_set(self, dve, s, v, x_of):
        for pair in range(2):
            dve.wait_ge(s.bias_ready, 2 * num(v) + pair + 1)
            t = slice(2 * pair, 2 * pair + 2)
            dve.tensor_tensor(s.acc[v[1]][:, t, :], s.psW[:, 1 - pair, :].rearrange("p (i n) -> p i n", i=2),
                              x_of(v)[:, t, :], ALU.add).then_inc(s.acc_set, 1)

    def dve_combine(self, dve, s, own, unit, i, half):
        acc, odd, gates = s.acc[unit[1]][:, i, :], s.odd[unit[1]][:, i, :], s.gates[unit[1]]
        tile = num(unit) * TILES + i
        if i == 0 and half == 0:
            dve.wait_ge(s.acc_set, 2 * num(unit) + 2)
        for c in (2 * half, 2 * half + 1):
            if c:
                own.wait()
            dve.wait_ge(s.experts, tile * 4 + c + 1)
            own.done(dve.scalar_tensor_tensor(out=acc, in0=s.psE[:, c, 0:D], scalar=gates[:, i, 2 * c:2 * c + 1],
                                              in1=acc, op0=ALU.mult, op1=ALU.add))
            gate = gates[:, i, 2 * c + 1:2 * c + 2]
            if c == 0:
                ins = dve.tensor_scalar(odd, s.psE[:, c, D:2 * D], gate, None, ALU.mult)
            else:
                dve.wait_ge(s.combined, tile * 4 + c)
                ins = dve.scalar_tensor_tensor(out=odd, in0=s.psE[:, c, D:2 * D], scalar=gate, in1=odd,
                                               op0=ALU.mult, op1=ALU.add)
            ins.then_inc(s.combined, 1)

    def pool_sum(self, pool, s, unit, i):
        pool.wait_ge(s.combined, (num(unit) * TILES + i) * 4 + 4)
        acc = s.acc[unit[1]][:, i, :]
        pool.tensor_tensor(acc, acc, s.odd[unit[1]][:, i, :], ALU.add).then_inc(s.summed, 1)

    def pass_a(self):
        nc = self.nc
        with ExitStack() as ctx:
            w = self.weights(ctx, "a", ["Wq", "Wk", "Wv"])
            s = self.ffn_state(ctx, "a")
            sb = lambda n, sh, dt=F32: self.sb(ctx, n, sh, dt)
            sem = lambda n: self.sem(ctx, n)
            X = [sb(f"X{h}", [P, TILES, D]) for h in range(2)]
            ln2 = self.layernorm_state(ctx, "a2")
            x2T = [sb(f"x2T{k}", [P, KC, UNIT], FR) for k in range(2)]
            cos, sin = sb("cos", [P, S]), sb("sin", [P, S])
            bqk = sb("bqk", [P, 2, 2])
            raw = [[sb(f"raw{t}{e}", [P, UNIT]) for e in range(2)] for t in range(2)]
            prod = [[sb(f"prod{t}{n}", [P, UNIT]) for n in range(2)] for t in range(2)]
            rot = [[sb(f"rot{t}{e}", [P, UNIT]) for e in range(2)] for t in range(2)]
            parts = [[[sb(f"part{t}{e}{k}", [P, UNIT], FR) for k in range(2)] for e in range(2)] for t in range(2)]
            V = sb("V", [P, TILES, D])
            x_loaded = [sem(f"x_loaded{h}") for h in range(2)]
            x1_stored = [sem(f"x1_stored{h}") for h in range(2)]
            (consts, turned2, hi2, lo2, qk_ready, qk_out, v_ready, v_out,
             rot_q, rot_k, qk_stored, v_stored, pool_own, x1_done) = (sem(n) for n in (
                 "consts", "turned2", "hi2", "lo2", "qk_ready", "qk_out",
                 "v_ready", "v_out", "rot_q", "rot_k", "qk_stored", "v_stored", "pool_own",
                 "x1_done"))
            gw_zero = sem("gw_zero")
            qk_hi, qk_lo = ([sem(f"{q}_{k}") for q in ("q", "k")] for k in ("hi", "lo"))

            block = ctx.enter_context(nc.Block())

            @block.sync
            def _(sp):
                sp.dma_start(cos[:], self.cos).then_inc(consts, 16)
                sp.dma_start(sin[:], self.sin).then_inc(consts, 16)
                for t, b in enumerate((self.bq, self.bk)):
                    sp.dma_start(bqk[:, t, :], b.rearrange("(p e) -> p e", e=2)).then_inc(consts, 16)
                sp.dma_start(X[0][:], rows(self.x_v, (0, 0))).then_inc(x_loaded[0], 16)

                def step(u):
                    v, p, c = shift(u, 3), shift(u, -1), u
                    if exists(p):
                        for t in range(2):
                            dst = (self.qs, self.ks)[t].rearrange("b t (e i) h n -> b t e h i n", e=2)
                            for e in range(2):
                                for k in range(2):
                                    sp.wait_ge((qk_hi, qk_lo)[k][t], 2 * num(p) + e + 1)
                                    sp.dma_start(dst[p[0], k, e, :, :, bass.ds(p[1] * UNIT, UNIT)],
                                                 parts[t][e][k][:].bitcast(F32)).then_inc(qk_stored, 16)
                        sp.wait_ge(v_out, 2 * num(p) + 2)
                        sp.dma_start(rows(self.v_v, p), V[:]).then_inc(v_stored, 16)
                        sp.wait_ge(qk_stored, 128 * num(p) + 128)
                        sp.wait_ge(v_stored, 16 * num(p) + 16)
                    if exists(c):
                        sp.wait_ge(s.summed, TILES * num(c) + TILES)
                        sp.dma_start(rows(self.x1_v, c), s.acc[c[1]][:]).then_inc(x1_stored[c[1]], 16)
                    if exists(v) and not num_is(v, 0):
                        if not num_below(v, 2):
                            wait_apart(sp, s.acc_set, 2 * num(v) - 2)
                        sp.dma_start(X[v[1]][:], rows(self.x_v, v)).then_inc(x_loaded[v[1]], 16)

                over_units(sp, step)
                for h in range(2):
                    sp.wait_ge(x1_stored[h], 16 * UNITS // 2)

            @block.tensor
            def _(pe):
                def turn_x1(p):
                    pe.wait_ge(ln2.xn_ready, num(p) + 1)
                    for pair in range(2):
                        if not num_is(p, 0):
                            pe.wait_ge(v_out, 2 * num(p) - 1 + pair)
                        self.turn(pe, s, w, ln2.xn, 2 + pair, pair, turned2)

                def project(p, t):
                    if t == 0:
                        pe.wait_ge(hi2, 2 * num(p) + 2)
                        pe.wait_ge(lo2, 2 * num(p) + 2)
                    for e in range(2):
                        if t == 1:
                            pe.wait_ge(qk_out, num(p) * 4 + e + 1)
                        W = w["WqWk"[2 * t:2 * t + 2]]
                        self.three(pe, s.psW[:, 2 + e, :], lambda a, k: W[a][:, k, e:D:2],
                                   lambda a, k: x2T[a][:, k, :]).then_inc(qk_ready, 1)

                def project_v(p):
                    for pair in range(2):
                        pe.wait_ge(qk_out, num(p) * 4 + 3 + pair)
                        for i in range(2):
                            t = 2 * pair + i
                            ins = self.three(pe, s.psW[:, 2 + pair, i * D:(i + 1) * D],
                                             lambda a, k: x2T[a][:, k, t * P:(t + 1) * P],
                                             lambda a, k: w["Wv"][a][:, k, :])
                        ins.then_inc(v_ready, 1)

                def step(u):
                    v, p = shift(u, 1), shift(u, -1)
                    if exists(u):
                        self.pe_experts(pe, s, w, u, 0, 0)
                        self.pe_experts(pe, s, w, u, 0, 1)
                    if exists(v):
                        self.pe_turn_unit(pe, s, w, v)
                    if exists(u):
                        self.pe_experts(pe, s, w, u, 1, 0)
                    if exists(v):
                        self.pe_router(pe, s, w, v)
                    if exists(u):
                        self.pe_experts(pe, s, w, u, 1, 1)
                    if exists(p):
                        turn_x1(p)
                    if exists(v):
                        self.pe_logits(pe, s, w, v)
                    if exists(u):
                        self.pe_experts(pe, s, w, u, 2, 0)
                    if exists(p):
                        project(p, 0)
                    if exists(v):
                        self.pe_gates(pe, s, w, v)
                    if exists(p):
                        project(p, 1)
                    if exists(u):
                        self.pe_experts(pe, s, w, u, 2, 1)
                    if exists(v):
                        self.pe_bias(pe, s, w, v)
                    if exists(p):
                        project_v(p)
                    if exists(u):
                        self.pe_experts(pe, s, w, u, 3, 0)
                        self.pe_experts(pe, s, w, u, 3, 1)

                over_units(pe, step)

            @block.scalar
            def _(act):
                act.wait_ge(consts, 64)

                def evacuate(p, t):
                    for e in range(2):
                        act.wait_ge(qk_ready, num(p) * 4 + 2 * t + e + 1)
                        act.activation(raw[t][e][:], s.psW[:, 2 + e, :], ACT.Identity,
                                       bias=bqk[:, t, e:e + 1]).then_inc(qk_out, 1)

                def part_hi(p, t):
                    for e in range(2):
                        act.wait_ge((rot_q, rot_k)[t], 2 * num(p) + e + 1)
                        act.activation(parts[t][e][0][:], rot[t][e][:], ACT.Copy).then_inc(qk_hi[t], 1)

                def step(u):
                    v, n, p = shift(u, 1), shift(u, 2), shift(u, -1)
                    if exists(v):
                        self.act_hi(act, s, v)
                    if exists(p):
                        if not num_is(p, 0):
                            act.wait_ge(turned2, 2 * num(p))
                        self.act_norm(act, ln2, s.acc[p[1]], num(p))
                    if exists(v):
                        self.act_router(act, s, v)
                    if exists(p):
                        for pair in range(2):
                            act.wait_ge(turned2, 2 * num(p) + pair + 1)
                            act.activation(x2T[0][:, :, pair * 2 * P:(pair + 1) * 2 * P],
                                           self.turned_view(s, 2 + pair), ACT.Copy).then_inc(hi2, 1)
                    if exists(n):
                        if not num_is(n, 0):
                            act.wait_ge(s.turned, 2 * num(n))
                        self.act_norm(act, s.ln, X[n[1]], num(n))
                    if exists(v):
                        self.act_gap(act, s, v)
                    if exists(p):
                        if not num_is(p, 0):
                            act.wait_ge(rot_q, 2 * num(p))
                            act.wait_ge(rot_k, 2 * num(p))
                        evacuate(p, 0)
                    if exists(v):
                        self.act_gates(act, s, v)
                    if exists(p):
                        evacuate(p, 1)
                        if not num_is(p, 0):
                            act.wait_ge(qk_stored, 128 * num(p))
                        part_hi(p, 0)
                        if not num_is(p, 0):
                            act.wait_ge(v_stored, 16 * num(p))
                        for pair in range(2):
                            act.wait_ge(v_ready, 2 * num(p) + pair + 1)
                            act.activation(V[:, 2 * pair:2 * pair + 2, :],
                                           s.psW[:, 2 + pair, :].rearrange("p (i n) -> p i n", i=2),
                                           ACT.Copy).then_inc(v_out, 1)
                        part_hi(p, 1)

                over_units(act, step)

            def rotate(eng, own, t, p, signal):
                at = slice(p[1] * UNIT, (p[1] + 1) * UNIT)
                eng.wait_ge(qk_out, num(p) * 4 + 2 * t + 2)
                for e in range(2):
                    own.done(eng.tensor_tensor(prod[t][0][:], raw[t][0][:], (cos, sin)[e][:, at], ALU.mult))
                    own.done(eng.tensor_tensor(prod[t][1][:], raw[t][1][:], (sin, cos)[e][:, at], ALU.mult))
                    own.wait()
                    if not num_is(p, 0) and e == 0:
                        eng.wait_ge(qk_lo[t], 2 * num(p))
                        eng.wait_ge(qk_hi[t], 2 * num(p))
                    eng.tensor_tensor(rot[t][e][:], prod[t][0][:], prod[t][1][:],
                                      (ALU.subtract, ALU.add)[e]).then_inc(signal, 1)
                    eng.wait_ge(signal, 2 * num(p) + e + 1)

            def split_lo(eng, t, p):
                if not num_is(p, 0):
                    eng.wait_ge(qk_stored, 128 * num(p))
                for e in range(2):
                    eng.wait_ge(qk_hi[t], 2 * num(p) + e + 1)
                    eng.tensor_tensor(parts[t][e][1][:], rot[t][e][:], parts[t][e][0][:].bitcast(F32),
                                      ALU.subtract).then_inc(qk_lo[t], 1)

            @block.gpsimd
            def _(pool):
                own = Chain(pool, pool_own)
                pool.wait_ge(consts, 64)

                def step(u):
                    n, p = shift(u, 2), shift(u, -1)
                    if exists(p):
                        self.pool_rs(pool, w, ln2, own, num(p))
                    if exists(u):
                        self.pool_sum(pool, s, u, 0)
                    if exists(n):
                        self.pool_rs(pool, w, s.ln, own, num(n))
                    if exists(u):
                        self.pool_sum(pool, s, u, 1)
                    if exists(p):
                        rotate(pool, own, 1, p, rot_k)
                        split_lo(pool, 1, p)
                    if exists(u):
                        self.pool_sum(pool, s, u, 2)
                        self.pool_sum(pool, s, u, 3)

                over_units(pool, step, own, 3 + 3 + 4)

            @block.vector
            def _(dve):
                own = Chain(dve, s.own)
                dve.memset(s.Gw[:], 0.0).then_inc(gw_zero, 1)
                dve.wait_ge(gw_zero, 1)
                dve.wait_ge(consts, 64)

                def step(u):
                    v, n, p = shift(u, 1), shift(u, 2), shift(u, -1)
                    if exists(u):
                        self.dve_combine(dve, s, own, u, 0, 0)
                    if exists(p):
                        dve.wait_ge(s.summed, TILES * num(p) + TILES)
                        self.dve_stats(dve, own, s.acc[p[1]], ln2)
                    if exists(u):
                        self.dve_combine(dve, s, own, u, 0, 1)
                    if exists(v):
                        self.dve_lo(dve, s, v)
                    if exists(u):
                        self.dve_combine(dve, s, own, u, 1, 0)
                    if exists(n):
                        dve.wait_ge(x_loaded[n[1]], 16 * n[0] + 16)
                        self.dve_stats(dve, own, X[n[1]], s.ln)
                    if exists(u):
                        self.dve_combine(dve, s, own, u, 1, 1)
                    if exists(p):
                        for pair in range(2):
                            dve.wait_ge(hi2, 2 * num(p) + pair + 1)
                            a = slice(pair * 2 * P, (pair + 1) * 2 * P)
                            dve.tensor_tensor(x2T[1][:, :, a], self.turned_view(s, 2 + pair),
                                              x2T[0][:, :, a].bitcast(F32), ALU.subtract).then_inc(lo2, 1)
                    if exists(v):
                        self.dve_router(dve, s, w, own, v)
                    if exists(u):
                        self.dve_combine(dve, s, own, u, 2, 0)
                    if exists(p):
                        rotate(dve, own, 0, p, rot_q)
                    if exists(u):
                        self.dve_combine(dve, s, own, u, 2, 1)
                    if exists(v):
                        if not num_below(v, 2):
                            dve.wait_ge(x1_stored[v[1]], 16 * v[0])
                            dve.wait_ge(ln2.xn_ready, num(v) - 1)
                        self.dve_acc_set(dve, s, v, lambda q: X[q[1]])
                    if exists(p):
                        split_lo(dve, 0, p)
                    if exists(u):
                        self.dve_combine(dve, s, own, u, 3, 0)
                        self.dve_combine(dve, s, own, u, 3, 1)

                over_units(dve, step, own, DVE_A)

    def pass_b(self):
        nc = self.nc
        with ExitStack() as ctx:
            sb = lambda n, sh, dt=F32: self.sb(ctx, n, sh, dt)
            sem = lambda n: self.sem(ctx, n)
            ROWS, MAXROWS = P, P - 2
            Q = [sb(f"Qop{g}", [P, HG, S], FR) for g in range(GROUPS)]
            K = [sb(f"Kop{g}", [P, HG, S], FR) for g in range(GROUPS)]
            Vraw = sb("Vraw", [P, KT, D])
            V1 = [sb(f"V1{g}", [P, KT, HG, 2 * DK]) for g in range(2)]
            W = [sb(f"W{n}", [P, HG, 512]) for n in range(SLOTS)]
            bv = sb("bv_b", [P, D])
            mask = sb("mask", [P, S])
            ident = sb("ident_b", [P, P])
            mx, nm = sb("mx", [P, KT, HG]), sb("nm", [P, KT, HG])
            nh = sb("nh", [P, KT, HG], FR)
            NB = sb("NB", [P, KT, P])
            mT = sb("mT", [2 * HG, S], FR)
            O = [sb(f"O{n}", [P, 512]) for n in range(2)]
            psM = ctx.enter_context(nc.psum_tensor("psM", [P, BANKS * 512], F32))
            psS = [ctx.enter_context(nc.psum_tensor(f"psS{n}", [P, 512], F32)) for n in range(3)]
            psO = ctx.enter_context(nc.psum_tensor("psO", [P, 512], F32))
            qk_loaded = [sem(f"qk_loaded{g}") for g in range(GROUPS)]
            bv_loaded = sem("bv_loaded")
            m_loaded = [sem(f"m_loaded{g}") for g in range(GROUPS)]
            o_stored = [sem(f"o_stored{n}") for n in range(2)]
            (v_loaded, v_spread, setup, own_p, scores_m, maxed, nb_ready, m_turned, m_out, scores, exps, kept,
             rows_used, sums_out, own_d) = (sem(n) for n in (
                 "v_loaded", "v_spread", "setup", "own_p", "scores_m", "maxed", "nb_ready", "m_turned", "m_out",
                 "scores", "exps", "kept", "rows_used", "sums_out", "own_d"))

            plan = [(j, kt, max(0, kt - 4 * j) * P, kt >= 4 * j) for j in range(2) for kt in range(4 * j + 4)]
            R = len(plan)
            DIAG = sum(r[3] for r in plan)
            MT = HG * KT
            TURN = TURN_AT
            order = interleave(plan)

            def g_of(b, hg):
                return b * GROUPS + hg

            ring, ring_length = max_ring()

            def columns(hg, item, width):
                c = (ring_length * hg + ring[item][0]) % BANKS * 512
                return slice(c, c + width)

            assert GROUPS * ring_length % BANKS == 0

            def last_user(item):
                p = ring[item][0] + ring[item][1] - 1 - BANKS
                for back in range(2):
                    for other, (q, size) in ring.items():
                        if q <= p + back * ring_length < q + size:
                            return other, back

            def after(b, hg, by):
                n = hg + by
                return b + n // GROUPS, n % GROUPS

            def there(b):
                return not isinstance(b, int) or 0 <= b < B

            def over_groups(eng, step, chain=None, per_step=0):
                for hg in range(GROUPS):
                    step(0, hg)
                k0 = chain.k if chain else 0
                with eng.Fori(1, B - 1) as b:
                    if chain:
                        chain.base, chain.k = (b - 1) * (GROUPS * per_step) + k0, 0
                    for hg in range(GROUPS):
                        step(b, hg)
                    assert not chain or chain.k == GROUPS * per_step, chain.k
                if chain:
                    chain.base, chain.k = k0 + (B - 2) * GROUPS * per_step, 0
                for hg in range(GROUPS):
                    step(B - 1, hg)

            block = ctx.enter_context(nc.Block())

            @block.sync
            def _(sp):
                def load(b, hg):
                    h = slice(hg * HG, (hg + 1) * HG)
                    for n, part in enumerate((0, 0, 1, 1)):
                        sp.dma_start(Q[hg][16 * n:16 * n + 16].bitcast(F32),
                                     self.qs[b, part, :, h, :]).then_inc(qk_loaded[hg], 16)
                    for n in range(2):
                        sp.dma_start(K[hg][32 * n:32 * n + 32].bitcast(F32),
                                     self.ks[b, :, :, h, :].rearrange("t d h n -> (t d) h n")
                                     ).then_inc(qk_loaded[hg], 16)

                def load_v(b):
                    sp.dma_start(Vraw[:], self.v_v[:, bass.ds(b * KT, KT), :]).then_inc(v_loaded, 16)

                sp.dma_start(bv[:], self.bv.partition_broadcast(P)).then_inc(bv_loaded, 16)
                sp.wait_ge(setup, 8)
                load_v(0)
                for hg in range(3):
                    load(0, hg)

                def load_maxima(b, hg):
                    sp.wait_ge(m_out, g_of(b, hg) + 1)
                    for part in range(2):
                        sp.dma_start(Q[hg][MAXROWS + part:MAXROWS + part + 1].bitcast(F32),
                                     mT[part * HG:(part + 1) * HG, :].bitcast(F32)).then_inc(m_loaded[hg], 16)

                def store(b, hg, j):
                    wait_apart(sp, sums_out, 2 * g_of(b, hg) + j + 1)
                    sp.dma_start(self.os[b, hg, :, j * 512:(j + 1) * 512], O[j][:]).then_inc(o_stored[j], 16)

                load_maxima(0, 0)

                def step(b, hg):
                    g = g_of(b, hg)
                    if not (isinstance(g, int) and g == 0):
                        store(*after(b, hg, -1), 1)
                    b3, g3 = after(b, hg, 3)
                    if there(b3):
                        if not (isinstance(g, int) and g == 0):
                            sp.wait_ge(rows_used, R * g)
                        load(b3, g3)
                    if hg == 2 and there(b + 1):
                        sp.wait_ge(v_spread, g_of(b, 3) + 1)
                        load_v(b + 1)
                    b1, g1 = after(b, hg, 1)
                    if there(b1):
                        load_maxima(b1, g1)
                    store(b, hg, 0)

                over_groups(sp, step)
                store(B - 1, GROUPS - 1, 1)
                for j in range(2):
                    sp.wait_ge(o_stored[j], 16 * B * GROUPS)

            @block.gpsimd
            def _(pool):
                own = Chain(pool, own_p)
                own.done(pool.memset(ident[:], 0.0))
                own.done(pool.memset(mask[:], 0.0))
                own.wait()
                own.done(pool.affine_select(out=ident[:], in_=ident[:], compare_op=ALU.not_equal, fill=1.0, base=0,
                                            pattern=[[-1, P]], channel_multiplier=1))
                own.done(pool.affine_select(out=mask[:, S - P:S], in_=mask[:, S - P:S], compare_op=ALU.is_ge,
                                            fill=MASKED, base=0, pattern=[[-1, P]], channel_multiplier=1))
                own.wait()
                for g in range(2):
                    own.done(pool.memset(V1[g][:], 1.0))
                own.done(pool.memset(NB[:], 0.0))
                own.wait()
                pool.drain().then_inc(setup, 1)

                def spread(b, hg):
                    g = g_of(b, hg)
                    wait_apart(pool, v_loaded, 16 * b + 16)
                    if not (isinstance(g, int) and g < 2):
                        wait_apart(pool, rows_used, R * g - R)
                    for h in range(HG):
                        c = (hg * HG + h) * DK
                        ins = pool.tensor_tensor(V1[hg % 2][:, :, h, 0:DK], Vraw[:, :, c:c + DK],
                                                 bv[:, c:c + DK].unsqueeze(1).to_broadcast([P, KT, DK]), ALU.add)
                    ins.then_inc(v_spread, 1)

                pool.wait_ge(bv_loaded, 16)
                spread(0, 0)

                def step(b, hg):
                    b1, g1 = after(b, hg, 1)
                    if there(b1):
                        spread(b1, g1)
                    for r, (j, kt, c0, diag) in enumerate(plan):
                        if diag:
                            row = g_of(b, hg) * R + r
                            wait_apart(pool, exps, HG * (row + 1))
                            Wd = W[r % SLOTS][:, :, c0:c0 + P]
                            pool.affine_select(out=Wd, in_=Wd, compare_op=ALU.is_ge, fill=0.0, base=0,
                                               pattern=[[0, HG], [1, P]], channel_multiplier=-1).then_inc(kept, 1)

                over_groups(pool, step)

            @block.vector
            def _(dve):
                own = Chain(dve, own_d)
                for g in range(GROUPS):
                    own.done(dve.memset(Q[g][64:P].bitcast(F32), 0.0))
                for g in range(GROUPS):
                    own.done(dve.memset(K[g][64:P].bitcast(F32), 1.0))
                own.wait()
                dve.drain().then_inc(setup, 7)
                dve.wait_ge(setup, 8)

                def max_tile(b, hg, t):
                    h, qt = t // KT, t % KT
                    w = (qt + 1) * P
                    n = g_of(b, hg) * MT + t
                    wait_apart(dve, scores_m, n + 1)
                    tile = psM[:, columns(hg, t, w)]
                    dve.tensor_tensor_reduce(tile, tile, mask[:, S - w:S], 1.0, LOWEST, ALU.add, ALU.max,
                                             mx[:, qt, h:h + 1]).then_inc(maxed, 1)

                def negate(b, hg):
                    g = g_of(b, hg)
                    dve.wait_ge(maxed, (g + 1) * MT)
                    own.done(dve.tensor_scalar(nm[:], mx[:], -1.0, None, ALU.mult))
                    own.wait()
                    own.done(dve.tensor_copy(nh[:], nm[:]))
                    own.wait()
                    if not (isinstance(g, int) and g == 0):
                        dve.wait_ge(m_turned, g)
                    own.done(dve.tensor_copy(NB[:, :, 0:HG], nh[:].bitcast(F32)))
                    dve.tensor_tensor(NB[:, :, HG:2 * HG], nm[:], nh[:].bitcast(F32),
                                      ALU.subtract).then_inc(nb_ready, 1)

                for g in range(2):
                    for t in range(MT):
                        max_tile(0, g, t)
                    negate(0, g)

                def take_sums(b, hg, half):
                    g = g_of(b, hg)
                    dve.wait_ge(rows_used, g * R + (4, R)[half])
                    if not (isinstance(g, int) and g == 0):
                        dve.wait_ge(o_stored[half], 16 * g)
                    dve.tensor_copy(O[half][:], psO[:]).then_inc(sums_out, 1)

                def step(b, hg):
                    b2, g2 = after(b, hg, 2)
                    g = g_of(b, hg)
                    for kind, r, k in order:
                        if kind == "max" and there(b2):
                            max_tile(b2, g2, k)
                        if kind == "weigh" and r == R - 1 and not (isinstance(g, int) and g == 0):
                            take_sums(*after(b, hg, -1), 1)
                        if kind == "weigh" and r == 3:
                            take_sums(b, hg, 0)
                    if there(b2):
                        negate(b2, g2)

                over_groups(dve, step, own, 3)
                take_sums(B - 1, GROUPS - 1, 1)

            @block.scalar
            def _(act):
                def m_copy(b, hg):
                    g = g_of(b, hg)
                    act.wait_ge(m_turned, g + 1)
                    if not (isinstance(g, int) and g == 0):
                        pb, pg = after(b, hg, -1)
                        act.wait_ge(m_loaded[pg], 32 * pb + 32)
                    act.activation(mT[:], psM[0:2 * HG, columns(hg + 1, "turn", S)], ACT.Copy).then_inc(m_out, 1)

                m_copy(0, 0)

                def step(b, hg):
                    for kind, r, h in order:
                        if kind == "score":
                            row = g_of(b, hg) * R + r
                            act.wait_ge(scores, row * HG + h + 1)
                            if h == 0 and not (isinstance(row, int) and row < SLOTS):
                                act.wait_ge(rows_used, row - SLOTS + 1)
                            c0 = plan[r][2]
                            act.activation(W[r % SLOTS][:, h, c0:512], psS[(r * HG + h) % 3][:, c0:512], ACT.Exp,
                                           scale=float(DK) ** -0.5).then_inc(exps, 1)
                        if kind == "turn" and there(after(b, hg, 1)[0]):
                            m_copy(*after(b, hg, 1))

                over_groups(act, step)

            @block.tensor
            def _(pe):
                pe.wait_ge(setup, 8)

                def wait_banks(g, item):
                    user, back = last_user(item)
                    first = isinstance(g, int) and g == 0
                    if user == "turn" and first:
                        user, back = last_user("turn")
                    if back and first:
                        return
                    if user == "turn":
                        pe.wait_ge(m_out, g - back)
                    else:
                        pe.wait_ge(maxed, g * MT + user + 1 - back * MT)

                def max_tile(b, hg, t):
                    h, qt = t // KT, t % KT
                    g = g_of(b, hg)
                    if t == 0:
                        pe.wait_ge(qk_loaded[hg], 96 * b + 96)
                    wait_banks(g, t)
                    w = (qt + 1) * P
                    for c in range(0, w, 512):
                        n = min(512, max(w - c, 256))
                        at = columns(hg, t, c).stop
                        ins = pe.matmul(psM[:, at:at + n], Q[hg][0:MAXROWS, h, qt * P:(qt + 1) * P],
                                        K[hg][0:MAXROWS, h, c:c + n], start=True, stop=True)
                    ins.then_inc(scores_m, 1)

                def turn_maxima(b, hg):
                    g = g_of(b, hg)
                    if isinstance(g, int) and g == B * GROUPS - 1:
                        pe.wait_ge(maxed, (g + 1) * MT)
                    else:
                        wait_banks(g + 1, "turn")
                    pe.wait_ge(nb_ready, g + 1)
                    for qt in range(KT):
                        ins = pe.transpose(psM[:, columns(hg + 1, "turn", S)][:, qt * P:(qt + 1) * P], NB[:, qt, :], ident[:])
                    ins.then_inc(m_turned, 1)

                for g in range(2):
                    for t in range(MT):
                        if g == 1 and t == TURN:
                            turn_maxima(0, 0)
                        max_tile(0, g, t)

                def score(b, hg, r, h):
                    j, kt, c0, diag = plan[r]
                    n = (g_of(b, hg) * R + r) * HG + h
                    if not (isinstance(n, int) and n < 3):
                        pe.wait_ge(exps, n - 2)
                    c = min(c0, 256)
                    pe.matmul(psS[(r * HG + h) % 3][:, c:512], K[hg][0:ROWS, h, kt * P:(kt + 1) * P],
                              Q[hg][0:ROWS, h, j * 512 + c:(j + 1) * 512], start=True, stop=True).then_inc(scores, 1)

                def weigh(b, hg, r):
                    j, kt, c0, diag = plan[r]
                    g = g_of(b, hg)
                    if diag:
                        pe.wait_ge(kept, g * DIAG + sum(q[3] for q in plan[:r + 1]))
                    else:
                        pe.wait_ge(exps, (g * R + r + 1) * HG)
                    if r == 0:
                        pe.wait_ge(v_spread, g + 1)
                    if kt == 0 and not (isinstance(g, int) and g == 0 and j == 0):
                        pe.wait_ge(sums_out, 2 * g + j)
                    last = kt == 4 * j + 3
                    for h in range(HG):
                        ins = pe.matmul(psO[32 * h:32 * h + 32, c0:512], V1[hg % 2][:, kt, h, :],
                                        W[r % SLOTS][:, h, c0:512], start=(kt == 0), stop=last)
                    ins.then_inc(rows_used, 1)

                def step(b, hg):
                    g = g_of(b, hg)
                    b2, g2 = after(b, hg, 2)
                    pe.wait_ge(m_loaded[hg], 32 * b + 32)
                    for kind, r, k in order:
                        if kind == "score":
                            score(b, hg, r, k)
                        elif kind == "max" and there(b2):
                            max_tile(b2, g2, k)
                        elif kind == "turn" and there(after(b, hg, 1)[0]):
                            turn_maxima(*after(b, hg, 1))
                        elif kind == "weigh":
                            if r < R - LAG:
                                weigh(b, hg, r)
                            elif not (isinstance(g, int) and g == 0):
                                weigh(*after(b, hg, -1), r)

                over_groups(pe, step)
                for r in range(R - LAG, R):
                    weigh(B - 1, GROUPS - 1, r)

    def pass_c(self):
        nc = self.nc
        with ExitStack() as ctx:
            w = self.weights(ctx, "c", ["Wo"])
            s = self.ffn_state(ctx, "c")
            sb = lambda n, sh, dt=F32: self.sb(ctx, n, sh, dt)
            sem = lambda n: self.sem(ctx, n)
            X1 = [sb(f"X1{h}", [P, TILES, D]) for h in range(2)]
            OT = [sb(f"OT{h}", [P, GROUPS, UNIT]) for h in range(2)]
            attn, rc = sb("attn", [P, TILES, D]), sb("rc", [P, TILES, H])
            aT = [sb(f"aT{k}", [P, KC, UNIT], FR) for k in range(2)]
            bo = sb("bo", [P, D])
            x1_loaded = [sem(f"x1_loaded{h}") for h in range(2)]
            o_loaded = [sem(f"o_loaded{h}") for h in range(2)]
            out_stored = [sem(f"out_stored{h}") for h in range(2)]
            (bo_loaded, o_turned, attn_ready, a_turned, a_hi, a_lo, proj, x2_ready, x1_biased, pool_own, gw_zero) = (
                sem(n) for n in ("bo_loaded", "o_turned", "attn_ready", "a_turned", "a_hi", "a_lo", "proj",
                                 "x2_ready", "x1_biased", "pool_own_c", "gw_zero_c"))
            block = ctx.enter_context(nc.Block())

            @block.sync
            def _(sp):
                sp.dma_start(bo[:], self.bo.partition_broadcast(P)).then_inc(bo_loaded, 16)

                def load(v):
                    sp.dma_start(X1[v[1]][:], rows(self.x1_v, v)).then_inc(x1_loaded[v[1]], 16)
                    sp.dma_start(OT[v[1]][:], self.os[v[0], :, :, v[1] * UNIT:(v[1] + 1) * UNIT].rearrange(
                        "g p n -> p g n")).then_inc(o_loaded[v[1]], 16)

                load((0, 0))

                def step(u):
                    v = shift(u, 3)
                    if exists(v):
                        if not num_below(v, 2):
                            wait_apart(sp, s.acc_set, 2 * num(v) - 2)
                            wait_apart(sp, o_turned, TILES * (num(v) - 1))
                        load(v)
                    if exists(u):
                        sp.wait_ge(s.summed, TILES * num(u) + TILES)
                        sp.dma_start(rows(self.out_v, u), s.acc[u[1]][:]).then_inc(out_stored[u[1]], 16)

                over_units(sp, step)
                for h in range(2):
                    sp.wait_ge(out_stored[h], 16 * UNITS // 2)

            @block.tensor
            def _(pe):
                def turn_sums(n, i):
                    if i < 2 and not num_is(n, 0):
                        pe.wait_ge(x2_ready, 2 * num(n) - 1 + i)
                    if i >= 2:
                        pe.wait_ge(attn_ready, TILES * num(n) + i - 1)
                    for g in range(GROUPS):
                        ins = pe.transpose(s.psW[:, 2 + i % 2, g * P:(g + 1) * P],
                                           OT[n[1]][:, g, i * P:(i + 1) * P], w["ident"][:])
                    ins.then_inc(o_turned, 1)

                def step(u):
                    v, n = shift(u, 1), shift(u, 2)
                    if exists(n):
                        pe.wait_ge(o_loaded[n[1]], 16 * n[0] + 16)
                        turn_sums(n, 0)
                        turn_sums(n, 1)
                    if exists(u):
                        self.pe_experts(pe, s, w, u, 0, 0)
                    if exists(v):
                        self.pe_turn_unit(pe, s, w, v)
                    if exists(n):
                        turn_sums(n, 2)
                        turn_sums(n, 3)
                    if exists(u):
                        self.pe_experts(pe, s, w, u, 0, 1)
                    if exists(v):
                        self.pe_router(pe, s, w, v)
                    if exists(n):
                        pe.wait_ge(attn_ready, TILES * num(n) + 4)
                        for pair in range(2):
                            self.turn(pe, s, w, attn, 2 + pair, pair, a_turned)
                    if exists(u):
                        self.pe_experts(pe, s, w, u, 1, 0)
                    if exists(v):
                        self.pe_logits(pe, s, w, v)
                    if exists(u):
                        self.pe_experts(pe, s, w, u, 1, 1)
                        self.pe_experts(pe, s, w, u, 2, 0)
                    if exists(n):
                        pe.wait_ge(a_hi, 2 * num(n) + 2)
                        pe.wait_ge(a_lo, 2 * num(n) + 2)
                        for pair in range(2):
                            for i in range(2):
                                t = 2 * pair + i
                                ins = self.three(pe, s.psW[:, 2 + pair, i * D:(i + 1) * D],
                                                 lambda a, k: aT[a][:, k, t * P:(t + 1) * P],
                                                 lambda a, k: w["Wo"][a][:, k, :])
                            ins.then_inc(proj, 1)
                    if exists(v):
                        self.pe_gates(pe, s, w, v)
                    if exists(u):
                        self.pe_experts(pe, s, w, u, 2, 1)
                    if exists(v):
                        self.pe_bias(pe, s, w, v)
                    if exists(u):
                        self.pe_experts(pe, s, w, u, 3, 0)
                        self.pe_experts(pe, s, w, u, 3, 1)

                over_units(pe, step)

            @block.scalar
            def _(act):
                def step(u):
                    v, n = shift(u, 1), shift(u, 2)
                    if exists(v):
                        self.act_hi(act, s, v)
                        self.act_router(act, s, v)
                    if exists(n):
                        for pair in range(2):
                            act.wait_ge(a_turned, 2 * num(n) + pair + 1)
                            act.activation(aT[0][:, :, pair * 2 * P:(pair + 1) * 2 * P],
                                           self.turned_view(s, 2 + pair), ACT.Copy).then_inc(a_hi, 1)
                    if exists(v):
                        self.act_gap(act, s, v)
                        self.act_gates(act, s, v)
                    if exists(n):
                        if not num_is(n, 0):
                            act.wait_ge(s.turned, 2 * num(n))
                        self.act_norm(act, s.ln, X1[n[1]], num(n))

                over_units(act, step)

            @block.gpsimd
            def _(pool):
                own = Chain(pool, pool_own)
                pool.wait_ge(bo_loaded, 16)

                def step(u):
                    v, n = shift(u, 1), shift(u, 2)
                    if exists(n):
                        pool.wait_ge(x1_loaded[n[1]], 16 * n[0] + 16)
                        for i in range(TILES):
                            ins = pool.tensor_tensor(X1[n[1]][:, i, :], X1[n[1]][:, i, :], bo[:], ALU.add)
                        ins.then_inc(x1_biased, 1)
                    if exists(u):
                        self.pool_sum(pool, s, u, 0)
                        self.pool_sum(pool, s, u, 1)
                    if exists(n):
                        self.pool_rs(pool, w, s.ln, own, num(n))
                    if exists(u):
                        self.pool_sum(pool, s, u, 2)
                        self.pool_sum(pool, s, u, 3)

                over_units(pool, step, own, 3)

            @block.vector
            def _(dve):
                own = Chain(dve, s.own)
                dve.memset(s.Gw[:], 0.0).then_inc(gw_zero, 1)
                dve.wait_ge(gw_zero, 1)

                def attend(n, i):
                    dve.wait_ge(o_turned, TILES * num(n) + i + 1)
                    if i == 0 and not num_is(n, 0):
                        dve.wait_ge(a_turned, 2 * num(n))
                    ps = s.psW[:, 2 + i % 2, :].rearrange("p (h d) -> p h d", d=2 * DK)
                    own.done(dve.reciprocal(rc[:, i, :], ps[:, :, DK]))
                    own.wait()
                    dve.tensor_tensor(attn[:, i, :].rearrange("p (h d) -> p h d", d=DK), ps[:, :, 0:DK],
                                      rc[:, i, :].unsqueeze(2).to_broadcast([P, H, DK]),
                                      ALU.mult).then_inc(attn_ready, 1)

                def step(u):
                    v, n = shift(u, 1), shift(u, 2)
                    if exists(n):
                        attend(n, 0)
                        attend(n, 1)
                    if exists(u):
                        self.dve_combine(dve, s, own, u, 0, 0)
                    if exists(n):
                        attend(n, 2)
                        attend(n, 3)
                    if exists(v):
                        self.dve_lo(dve, s, v)
                    if exists(u):
                        self.dve_combine(dve, s, own, u, 0, 1)
                    if exists(n):
                        for pair in range(2):
                            dve.wait_ge(a_hi, 2 * num(n) + pair + 1)
                            a = slice(pair * 2 * P, (pair + 1) * 2 * P)
                            dve.tensor_tensor(aT[1][:, :, a], self.turned_view(s, 2 + pair),
                                              aT[0][:, :, a].bitcast(F32), ALU.subtract).then_inc(a_lo, 1)
                    if exists(u):
                        self.dve_combine(dve, s, own, u, 1, 0)
                    if exists(v):
                        self.dve_router(dve, s, w, own, v)
                    if exists(u):
                        self.dve_combine(dve, s, own, u, 1, 1)
                        self.dve_combine(dve, s, own, u, 2, 0)
                    if exists(n):
                        dve.wait_ge(x1_biased, num(n) + 1)
                        for pair in range(2):
                            dve.wait_ge(proj, 2 * num(n) + pair + 1)
                            t = slice(2 * pair, 2 * pair + 2)
                            dve.tensor_tensor(X1[n[1]][:, t, :],
                                              s.psW[:, 2 + pair, :].rearrange("p (i n) -> p i n", i=2),
                                              X1[n[1]][:, t, :], ALU.add).then_inc(x2_ready, 1)
                        dve.wait_ge(x2_ready, 2 * num(n) + 2)
                        self.dve_stats(dve, own, X1[n[1]], s.ln)
                    if exists(u):
                        self.dve_combine(dve, s, own, u, 2, 1)
                    if exists(v):
                        if not num_below(v, 2):
                            dve.wait_ge(out_stored[v[1]], 16 * v[0])
                        self.dve_acc_set(dve, s, v, lambda q: X1[q[1]])
                    if exists(u):
                        self.dve_combine(dve, s, own, u, 3, 0)
                        self.dve_combine(dve, s, own, u, 3, 1)

                over_units(dve, step, own, DVE_C)


def num_is(unit, n):
    return isinstance(unit[0], int) and num(unit) == n


def num_below(unit, n):
    return isinstance(unit[0], int) and num(unit) < n


ROUTER = 4 + 4 + 1 + 1 + 1 + 1 + 1 + 1 + 1 + 1 + 2
DVE_A = TILES + TILES + TILES * 4 + ROUTER + 4
DVE_C = TILES + TILES + TILES * 4 + ROUTER


def macaron_kernel(nc, *args):
    k = Kernel(nc, args)
    k.pass_a()
    k.pass_b()
    k.pass_c()


_INS = ["L0_attn_x", "L0_attn_Wq", "L0_attn_bq", "L0_attn_Wk", "L0_attn_bk", "L0_attn_Wv", "L0_attn_bv",
        "L0_attn_Wo", "L0_attn_bo", "L0_ffn_Wg", "L0_ffn_We", "L0_ffn_be"]


def rope_tables():
    freq = (np.float32(1.0) / np.float32(THETA) ** (np.arange(0, DK, 2, dtype=np.float32) / np.float32(DK)))
    angle = freq.astype(np.float32)[:, None] * np.arange(S, dtype=np.float32)[None, :]
    return [np.ascontiguousarray(np.tile(f(angle).astype(np.float32), (H, 1))) for f in (np.cos, np.sin)]


def kernel(**inputs):
    import concourse.bacc as _bacc
    from concourse.bass_utils import run_bass_kernel_spmd as _run

    nc = _bacc.Bacc("TRN2", target_bir_lowering=False, num_devices=1)
    arrays, args = {}, []
    given = [(n, np.ascontiguousarray(inputs[n])) for n in _INS]
    given += list(zip(("rope_cos", "rope_sin"), rope_tables()))
    for name, a in given:
        arrays[f"in_{name}_dram"] = a
        args.append(nc.dram_tensor(f"in_{name}_dram", a.shape, mybir.dt.from_np(a.dtype), kind="ExternalInput").ap())
    args.append(nc.dram_tensor("out_0_dram", (B, S, D), F32, kind="ExternalOutput").ap())
    macaron_kernel(nc, *args)
    r = _run(nc, [arrays], core_ids=[0])
    return r.results[0]["out_0_dram"]
```

```python
from contextlib import ExitStack

import numpy as np

import concourse.bass as bass
from concourse import mybir

F32 = mybir.dt.float32
FR = mybir.dt.float32r
U32 = mybir.dt.uint32
ALU = mybir.AluOpType
ACT = mybir.ActivationFunctionType

P = 128
B, S, D = 16, 1024, 256
H, DK, E = 16, 16, 8
KC = D // P
UNIT = 512
TILES = UNIT // P
UNITS = B * S // UNIT
HG = 4
GROUPS = H // HG
KT = S // P
EPS = 1e-5
THETA = 10000.0
MASKED = -1e30
LOWEST = -3e38


class Chain:

    def __init__(self, eng, sem):
        self.eng, self.sem, self.base, self.k = eng, sem, 0, 0

    def done(self, ins):
        ins.then_inc(self.sem, 1)
        self.k += 1
        return self.base + self.k

    def wait(self, at=None):
        self.eng.wait_ge(self.sem, self.base + self.k if at is None else at)

    def wait_apart(self):
        wait_apart(self.eng, self.sem, self.base + self.k)


def wait_apart(eng, sem, value):
    if not isinstance(value, int):
        eng.wait_ge(sem, value)
        eng.nop(nofuse=True)
    else:
        eng.wait_ge(sem, value)


def over_units(eng, step, chain=None, per_step=0, ahead=None):
    def at(u):
        return (u // 2, u % 2)

    def count(n):
        if chain is not None:
            assert chain.k == per_step * n, f"steps per unit: {chain.k} for {n}"

    for u in (-2, -1, 0, 1):
        if ahead and u in ahead:
            ahead[u]()
        step(at(u))
    k0 = chain.k if chain else 0
    with eng.Fori(1, UNITS // 2 - 2) as b:
        if chain:
            chain.base, chain.k = (b - 1) * (2 * per_step) + k0, 0
        step((b, 0))
        step((b, 1))
        count(2)
    if chain:
        chain.base, chain.k = k0 + (UNITS // 2 - 3) * 2 * per_step, 0
    for u in range(UNITS - 4, UNITS + 1):
        step(at(u))


def shift(unit, by):
    b, h = unit
    n = h + by
    return (b + n // 2, n % 2)


def num(unit):
    return unit[0] * 2 + unit[1]


def exists(unit):
    b = unit[0]
    return not isinstance(b, int) or 0 <= b < B


def rows(ap, unit):
    return ap[:, bass.ds(num(unit) * TILES, TILES), :]


class State:
    pass


LAG = 2
TURN_AT = 4
SLOTS = 4
BANKS = 4


def max_ring():
    ring, pos = {}, 0
    for t in range(HG * KT):
        if t == TURN_AT:
            ring["turn"] = (pos, 2)
            pos += 2
        size = 1 if t % KT < 4 else 2
        ring[t] = (pos, size)
        pos += size
    assert all(p % size == 0 for p, size in ring.values())
    return ring, pos


def interleave(plan):
    late = {"max": 0, "score": 3, "weigh": 205}
    R, hop = len(plan), 264
    ring, length = max_ring()
    scores = [(r, h) for r in range(R) for h in range(HG)]
    weighs = [(r - LAG) % R for r in range(R)]
    free = [0.0] * BANKS
    exp_done = [0.0] * len(scores)
    row_ready = [0.0] * R
    used = [0.0] * R
    pe = dve = act = pool = 0.0
    for group in range(3):
        order, si, wi, items = [], 0, 0, list(ring)
        base = length * group
        negated = dve + 4 * 150
        while si < len(scores) or wi < R or items:
            can = []
            if items:
                p, size = ring[items[0]]
                at = max(free[(base + p + k) % BANKS] for k in range(size))
                can.append((max(pe, at, negated if items[0] == "turn" else 0), 0, "max"))
            if si < len(scores) and (si // HG < LAG or si // HG - (SLOTS - LAG) < wi):
                can.append((max(pe, exp_done[si - 3]), 1, "score"))
            if wi < R and (wi < LAG or (wi - LAG) * HG + HG <= si):
                can.append((max(pe, row_ready[weighs[wi]]), 2, "weigh"))
            start, _, kind = min(can, key=lambda c: (c[0] + late[c[2]], c[1]))
            if kind == "max":
                item = items.pop(0)
                p, size = ring[item]
                if item == "turn":
                    order.append(("turn", 0, 0))
                    pe = start + 107
                    act = done = max(act, pe + hop) + 160
                else:
                    order.append(("max", 0, item))
                    width = (item % KT + 1) * P
                    pe = start + max(width, 256) * 0.42
                    dve = done = max(dve, pe + hop) + width * 1.05 + 91
                for k in range(size):
                    free[(base + p + k) % BANKS] = done + hop
            elif kind == "score":
                r, h = scores[si]
                c0 = plan[r][2]
                order.append(("score", r, h))
                pe = start + (512 - min(c0, 256)) * 0.42
                act = max(act, pe + hop, used[(r - SLOTS) % R]) + (512 - c0) * 0.83 + 49
                exp_done[si] = act + hop
                if h == HG - 1:
                    row_ready[r] = act + hop
                    if plan[r][3]:
                        pool = max(pool, act + hop) + 800
                        row_ready[r] = pool + hop
                si += 1
            else:
                r = weighs[wi]
                order.append(("weigh", r, 0))
                pe = start + HG * (512 - plan[r][2]) * 0.47
                used[r] = pe + hop
                if r in (3, R - 1):
                    dve = max(dve, pe + hop) + 600
                wi += 1
    return order


class Kernel:
    def __init__(self, nc, args):
        self.nc = nc
        (self.x, self.Wq, self.bq, self.Wk, self.bk, self.Wv, self.bv, self.Wo, self.bo,
         self.Wg, self.We, self.be, self.cos, self.sin, self.out) = args
        nt = "(n p) d -> p n d"
        self.x_v = self.x.rearrange("b s d -> (b s) d").rearrange(nt, p=P)
        self.out_v = self.out.rearrange("b s d -> (b s) d").rearrange(nt, p=P)
        self.x1_v = nc.dram_tensor("x1", (B * S, D), F32, kind="Internal").ap().rearrange(nt, p=P)
        v = nc.dram_tensor("v", (B * S, D), F32, kind="Internal").ap()
        self.v_v = v.rearrange(nt, p=P)
        self.qs = nc.dram_tensor("q_split", (B, 2, DK, H, S), F32, kind="Internal").ap()
        self.ks = nc.dram_tensor("k_split", (B, 2, DK, H, S), F32, kind="Internal").ap()
        self.os = nc.dram_tensor("o_sums", (B, GROUPS, HG, DK + 1, S), F32, kind="Internal").ap()

    def sem(self, ctx, name):
        return ctx.enter_context(self.nc.semaphore(name))

    def sb(self, ctx, name, shape, dt=F32):
        return ctx.enter_context(self.nc.sbuf_tensor(name, shape, dt))

    def weights(self, ctx, tag, squares):
        w = State()
        sb = lambda n, s, dt=F32: self.sb(ctx, f"{n}_{tag}", s, dt)
        w.ident = sb("ident", [P, P])
        w.We = [sb(f"We{k}", [P, KC, E * D], FR) for k in range(2)]
        w.Wg = [sb(f"Wg{k}", [P, KC, P], FR) for k in range(2)]
        w.be = sb("be", [P, TILES, D], FR)
        w.be_parts = [sb(f"be_part{k}", [E, D], FR) for k in range(2)]
        w.iota, w.nhalf = sb("iota", [P, E]), sb("nhalf", [P, TILES])
        w.names = squares
        w.square = {n: [sb(f"{n}{k}", [P, KC, D], FR) for k in range(2)] for n in squares}
        w.raw = sb("rawE", [P, KC, E * D])
        w.rawg, w.rawb = sb("rawg", [P, KC, E]), sb("rawb", [E, D])
        w.rawi = sb("rawi", [P, E], mybir.dt.int32)
        w.rawsq = sb("rawsq", [P, len(squares), KC, D])
        sem = lambda n: self.sem(ctx, f"{n}_{tag}")
        w.router_loaded, w.bias_loaded, w.squares_loaded = (
            sem(n) for n in ("w_router_loaded", "w_bias_loaded", "w_squares_loaded"))
        w.experts_loaded = [sem(f"w_experts_loaded{c}") for c in range(E // 2)]
        w.made, w.zeroed, w.turned, w.own = (sem(n) for n in ("w_made", "w_zeroed", "w_turned", "w_own"))
        w.small_ready, w.experts_hi, w.experts_lo, w.bias_spread = (
            sem(n) for n in ("w_small", "w_experts_hi", "w_experts_lo", "w_bias_spread"))
        return w

    def load_small(self, sp, w):
        for n, name in enumerate(w.names):
            src = {"Wq": self.Wq, "Wk": self.Wk, "Wv": self.Wv, "Wo": self.Wo}[name]
            sp.dma_start(w.rawsq[:, n], src.rearrange("(k p) n -> p k n", p=P)).then_inc(w.squares_loaded, 16)
        sp.dma_start(w.rawg[:], self.Wg.rearrange("(k p) e -> p k e", p=P)).then_inc(w.router_loaded, 16)
        sp.dma_start(w.rawb[:], self.be).then_inc(w.bias_loaded, 16)

    def spread_bias(self, sp, w):
        sp.wait_ge(w.small_ready, 1)
        for i in range(TILES):
            for n, part in enumerate((0, 0, 1)):
                row = 32 * i + E * n
                sp.dma_start(w.be[row:row + E, i, :].bitcast(F32),
                             w.be_parts[part][:].bitcast(F32)).then_inc(w.bias_spread, 16)

    def load_experts(self, sp, w):
        for e in range(E):
            sp.dma_start(w.raw[:, :, e * D:(e + 1) * D],
                         self.We[e].rearrange("(k p) n -> p k n", p=P)).then_inc(w.experts_loaded[e // 2], 16)

    def pool_constants(self, pool, w):
        pool.memset(w.ident[:], 0.0).then_inc(w.made, 1)
        pool.wait_ge(w.made, 1)
        pool.affine_select(out=w.ident[:], in_=w.ident[:], compare_op=ALU.not_equal, fill=1.0,
                           base=0, pattern=[[-1, P]], channel_multiplier=1).then_inc(w.made, 1)
        pool.iota(w.rawi[:], pattern=[[1, E]], base=0, channel_multiplier=0).then_inc(w.made, 1)
        pool.wait_ge(w.made, 3)
        pool.tensor_copy(w.iota[:], w.rawi[:]).then_inc(w.made, 1)
        pool.memset(w.nhalf[:], -0.5).then_inc(w.made, 1)
        pool.wait_ge(w.made, 5)

    def pe_turn_squares(self, pe, s, w):
        pe.wait_ge(w.made, 2)
        pe.wait_ge(w.squares_loaded, 16 * len(w.names))
        for n in range(len(w.names)):
            for ki in range(KC):
                for ko in range(KC):
                    ins = pe.transpose(s.psE[:, n, ki * D + ko * P:ki * D + (ko + 1) * P],
                                       w.rawsq[:, n, ko, ki * P:(ki + 1) * P], w.ident[:])
            ins.then_inc(w.turned, 1)

    def dve_small(self, dve, s, w):
        own = Chain(dve, w.own)

        def split(hi, lo, src):
            own.done(dve.tensor_copy(hi, src))
            own.wait()
            own.done(dve.tensor_tensor(lo, src, hi.bitcast(F32), ALU.subtract))

        dve.memset(w.be[:].bitcast(F32), 0.0).then_inc(w.zeroed, 1)
        for k in range(2):
            dve.memset(w.Wg[k][:].bitcast(F32), 0.0).then_inc(w.zeroed, 1)
        dve.wait_ge(w.made, 5)
        for n, name in enumerate(w.names):
            dve.wait_ge(w.turned, n + 1)
            hi, lo = (w.square[name][k][:].rearrange("p k n -> p (k n)") for k in range(2))
            split(hi, lo, s.psE[:, n, :])
        dve.wait_ge(w.zeroed, 3)
        dve.wait_ge(w.router_loaded, 16)
        split(w.Wg[0][:, :, 0:E], w.Wg[1][:, :, 0:E], w.rawg[:])
        dve.wait_ge(w.bias_loaded, 16)
        split(w.be_parts[0][:], w.be_parts[1][:], w.rawb[:])
        own.wait()
        dve.drain().then_inc(w.small_ready, 1)

    def act_experts_hi(self, act, w):
        for c in range(E // 2):
            act.wait_ge(w.experts_loaded[c], 32)
            a = slice(c * 512, (c + 1) * 512)
            act.activation(w.We[0][:, :, a], w.raw[:, :, a], ACT.Copy).then_inc(w.experts_hi, 1)

    def dve_experts_lo(self, dve, w):
        for c in range(E // 2):
            dve.wait_ge(w.experts_hi, c + 1)
            a = slice(c * 512, (c + 1) * 512)
            dve.tensor_tensor(w.We[1][:, :, a], w.raw[:, :, a], w.We[0][:, :, a].bitcast(F32),
                              ALU.subtract).then_inc(w.experts_lo, 1)

    def ffn_state(self, ctx, tag):
        s = State()
        sb = lambda n, sh, dt=F32: self.sb(ctx, f"{n}_{tag}", sh, dt)
        s.ln = self.layernorm_state(ctx, tag)
        s.xT = [[sb(f"xT{h}{k}", [P, KC, UNIT], FR) for k in range(2)] for h in range(2)]
        s.lT = sb("lT", [P, P])
        s.m8, s.i8 = sb("m8", [P, TILES, 8]), sb("i8", [P, TILES, 8], U32)
        s.top = sb("top", [P, TILES, 2])
        s.d, s.e2, s.den = (sb(n, [P, TILES]) for n in ("gap", "e2", "den"))
        s.g = sb("g", [P, TILES, 2])
        s.hot, s.G = sb("hot", [P, TILES, 2, E]), sb("G", [P, TILES, 2, E])
        s.gates = [sb(f"gates{h}", [P, TILES, E]) for h in range(2)]
        s.odd = [sb(f"odd{h}", [P, TILES, D]) for h in range(2)]
        s.Gh = sb("Gh", [P, TILES, E], FR)
        s.Gw = sb("Gw", [P, TILES, 32])
        s.GT = sb("GT", [P, P], FR)
        s.acc = [sb(f"acc{h}", [P, TILES, D]) for h in range(2)]
        psum = lambda n, sh: ctx.enter_context(self.nc.psum_tensor(f"{n}_{tag}", sh, F32))
        s.psE = psum("psE", [P, 4, 512])
        s.psW = psum("psW", [P, 4, 512])
        s.turned = self.sem(ctx, f"turned_{tag}")
        s.hi_ready = self.sem(ctx, f"hi_ready_{tag}")
        s.lo_ready = self.sem(ctx, f"lo_ready_{tag}")
        s.logitsT = self.sem(ctx, f"logitsT_{tag}")
        s.logitsT_out = self.sem(ctx, f"logitsT_out_{tag}")
        s.logits = self.sem(ctx, f"logits_{tag}")
        s.gap_ready = self.sem(ctx, f"gap_ready_{tag}")
        s.e2_ready = self.sem(ctx, f"e2_ready_{tag}")
        s.gates_ready = self.sem(ctx, f"gates_ready_{tag}")
        s.gates_turned = self.sem(ctx, f"gates_turned_{tag}")
        s.gates_out = self.sem(ctx, f"gates_out_{tag}")
        s.bias_ready = self.sem(ctx, f"bias_ready_{tag}")
        s.acc_set = self.sem(ctx, f"acc_set_{tag}")
        s.experts = self.sem(ctx, f"experts_{tag}")
        s.combined = self.sem(ctx, f"combined_{tag}")
        s.summed = self.sem(ctx, f"summed_{tag}")
        s.own = self.sem(ctx, f"own_{tag}")
        return s

    def turn(self, pe, s, w, src, bank, pair, signal):
        for i in range(2):
            for k in range(KC):
                ins = pe.transpose(s.psW[:, bank, (k * 2 + i) * P:(k * 2 + i + 1) * P],
                                   src[:, 2 * pair + i, k * P:(k + 1) * P], w.ident[:])
        ins.then_inc(signal, 1)

    def turned_view(self, s, bank):
        return s.psW[:, bank, :].rearrange("p (k n) -> p k n", k=KC)

    def three(self, pe, out, stationary, moving, first=True, last=True):
        n, total = 0, 3 * KC
        for k in range(KC):
            for a, b in ((0, 0), (0, 1), (1, 0)):
                ins = pe.matmul(out, stationary(a, k), moving(b, k), start=(n == 0), stop=(n == total - 1))
                n += 1
        return ins

    def pe_experts(self, pe, s, w, unit, i, half):
        xT = s.xT[unit[1]]
        for c in (2 * half, 2 * half + 1):
            tile = num(unit) * TILES + i
            if isinstance(tile, int) and tile == 0:
                pe.wait_ge(w.experts_lo, c + 1)
            if not (isinstance(tile, int) and tile == 0):
                pe.wait_ge(s.combined, (tile - 1) * 4 + c + 1)
            self.three(pe, s.psE[:, c, :], lambda a, k: xT[a][:, k, i * P:(i + 1) * P],
                       lambda a, k: w.We[a][:, k, c * 512:(c + 1) * 512]).then_inc(s.experts, 1)

    def pe_turn_unit(self, pe, s, w, v):
        pe.wait_ge(s.ln.xn_ready, num(v) + 1)
        for pair in range(2):
            if not (isinstance(v[0], int) and num(v) == 0):
                pe.wait_ge(s.acc_set, 2 * num(v))
            self.turn(pe, s, w, s.ln.xn, pair, pair, s.turned)

    def pe_router(self, pe, s, w, v):
        pe.wait_ge(s.hi_ready, 2 * num(v) + 2)
        pe.wait_ge(s.lo_ready, 2 * num(v) + 2)
        xT = s.xT[v[1]]
        if num_is(v, 0):
            pe.wait_ge(w.small_ready, 1)
        self.three(pe, s.psW[:, 0, :], lambda a, k: w.Wg[a][:, k, :],
                   lambda a, k: xT[a][:, k, :]).then_inc(s.logitsT, 1)

    def pe_logits(self, pe, s, w, v):
        pe.wait_ge(s.logitsT_out, num(v) + 1)
        pe.transpose(s.psW[:, 1, 0:P], s.lT[:], w.ident[:]).then_inc(s.logits, 1)

    def pe_gates(self, pe, s, w, v):
        pe.wait_ge(s.gates_ready, num(v) + 1)
        pe.transpose(s.psW[:, 0, 0:P], s.Gw[:].rearrange("p i c -> p (i c)"), w.ident[:]).then_inc(s.gates_turned, 1)

    def pe_bias(self, pe, s, w, v):
        pe.wait_ge(s.gates_out, num(v) + 1)
        if num_is(v, 0):
            pe.wait_ge(w.bias_spread, 16 * 3 * TILES)
        for pair in range(2):
            pe.matmul(s.psW[:, 1 - pair, :], s.GT[:], w.be[:, 2 * pair:2 * pair + 2, :].rearrange(
                "p i n -> p (i n)"), start=True, stop=True).then_inc(s.bias_ready, 1)

    def act_hi(self, act, s, v):
        for pair in range(2):
            act.wait_ge(s.turned, 2 * num(v) + pair + 1)
            act.activation(s.xT[v[1]][0][:, :, pair * 2 * P:(pair + 1) * 2 * P],
                           self.turned_view(s, pair), ACT.Copy).then_inc(s.hi_ready, 1)

    def act_router(self, act, s, v):
        act.wait_ge(s.logitsT, num(v) + 1)
        for i in range(TILES):
            ins = act.activation(s.lT[32 * i:32 * i + 32, :], s.psW[0:32, 0, i * P:(i + 1) * P], ACT.Copy)
        ins.then_inc(s.logitsT_out, 1)

    def act_gap(self, act, s, v):
        act.wait_ge(s.gap_ready, num(v) + 1)
        act.activation(s.e2[:], s.d[:], ACT.Exp).then_inc(s.e2_ready, 1)

    def act_gates(self, act, s, v):
        act.wait_ge(s.gates_turned, num(v) + 1)
        act.activation(s.GT[:], s.psW[:, 0, 0:P], ACT.Copy).then_inc(s.gates_out, 1)

    def dve_stats(self, dve, own, src, ln):
        for i in range(TILES):
            own.done(dve.bn_stats(ln.st[:, i, :], src[:, i, :]))
        own.wait_apart()
        for i in range(TILES):
            ins = dve.bn_aggr(ln.mv[:, i, :], ln.st[:, i, :])
        ins.then_inc(ln.mv_ready, 1)

    def pool_rs(self, pool, w, ln, own, n):
        wait_apart(pool, ln.mv_ready, n + 1)
        own.done(pool.tensor_scalar(ln.ve[:], ln.mv[:, :, 1], EPS, None, ALU.add))
        own.done(pool.tensor_scalar(ln.nm[:], ln.mv[:, :, 0], -1.0, None, ALU.mult))
        own.wait()
        own.done(pool.tensor_tensor(ln.rs[:], ln.ve[:], w.nhalf[:], ALU.pow))
        own.wait()
        pool.tensor_tensor(ln.nb[:], ln.nm[:], ln.rs[:], ALU.mult).then_inc(ln.rs_ready, 1)

    def act_norm(self, act, ln, src, n):
        act.wait_ge(ln.rs_ready, n + 1)
        for i in range(TILES):
            ins = act.activation(ln.xn[:, i, :], src[:, i, :], ACT.Identity, scale=ln.rs[:, i:i + 1],
                                 bias=ln.nb[:, i:i + 1])
        ins.then_inc(ln.xn_ready, 1)

    def layernorm_state(self, ctx, tag):
        ln = State()
        sb = lambda n, sh: self.sb(ctx, f"{n}_{tag}", sh)
        ln.st, ln.mv = sb("st", [P, TILES, 6]), sb("mv", [P, TILES, 2])
        ln.ve, ln.nm, ln.rs, ln.nb = (sb(n, [P, TILES]) for n in ("ve", "nmean", "rs", "nb"))
        ln.xn = sb("xn", [P, TILES, D])
        ln.mv_ready = self.sem(ctx, f"mv_ready_{tag}")
        ln.rs_ready = self.sem(ctx, f"rs_ready_{tag}")
        ln.xn_ready = self.sem(ctx, f"xn_ready_{tag}")
        return ln

    def dve_lo(self, dve, s, v):
        for pair in range(2):
            dve.wait_ge(s.hi_ready, 2 * num(v) + pair + 1)
            a = slice(pair * 2 * P, (pair + 1) * 2 * P)
            dve.tensor_tensor(s.xT[v[1]][1][:, :, a], self.turned_view(s, pair),
                              s.xT[v[1]][0][:, :, a].bitcast(F32), ALU.subtract).then_inc(s.lo_ready, 1)

    def dve_router(self, dve, s, w, own, v):
        wait_apart(dve, s.logits, num(v) + 1)
        L = s.psW[:, 1, 0:P].rearrange("p (i n) -> p i n", i=TILES)
        for i in range(TILES):
            own.done(dve.max(s.m8[:, i, :], L[:, i, 0:E]))
        own.wait_apart()
        for i in range(TILES):
            own.done(dve.max_index(s.i8[:, i, :], s.m8[:, i, :], L[:, i, 0:E]))
        dve.tensor_tensor(s.d[:], s.m8[:, :, 1], s.m8[:, :, 0], ALU.subtract).then_inc(s.gap_ready, 1)
        own.wait()
        own.done(dve.tensor_copy(s.top[:], s.i8[:, :, 0:2]))
        dve.wait_ge(s.e2_ready, num(v) + 1)
        own.done(dve.tensor_scalar(s.den[:], s.e2[:], 2.0, 2.0, ALU.mult, ALU.add))
        own.wait()
        own.done(dve.reciprocal(s.g[:, :, 0], s.den[:]))
        own.wait()
        own.done(dve.tensor_tensor(s.g[:, :, 1], s.e2[:], s.g[:, :, 0], ALU.mult))
        wide = [P, TILES, 2, E]
        own.done(dve.tensor_tensor(s.hot[:], w.iota[:].unsqueeze(1).unsqueeze(1).to_broadcast(wide),
                                   s.top[:].unsqueeze(3).to_broadcast(wide), ALU.is_equal))
        own.wait()
        own.done(dve.tensor_tensor(s.G[:], s.hot[:], s.g[:].unsqueeze(3).to_broadcast(wide), ALU.mult))
        own.wait()
        gates = s.gates[v[1]]
        own.done(dve.tensor_tensor(gates[:], s.G[:, :, 0, :], s.G[:, :, 1, :], ALU.add))
        own.wait()
        own.done(dve.tensor_copy(s.Gh[:], gates[:]))
        own.wait()
        own.done(dve.tensor_copy(s.Gw[:, :, 0:E], s.Gh[:].bitcast(F32)))
        own.done(dve.tensor_copy(s.Gw[:, :, 2 * E:3 * E], s.Gh[:].bitcast(F32)))
        dve.tensor_tensor(s.Gw[:, :, E:2 * E], gates[:], s.Gh[:].bitcast(F32),
                          ALU.subtract).then_inc(s.gates_ready, 1)

    def dve_acc_set(self, dve, s, v, x_of):
        for pair in range(2):
            dve.wait_ge(s.bias_ready, 2 * num(v) + pair + 1)
            t = slice(2 * pair, 2 * pair + 2)
            dve.tensor_tensor(s.acc[v[1]][:, t, :], s.psW[:, 1 - pair, :].rearrange("p (i n) -> p i n", i=2),
                              x_of(v)[:, t, :], ALU.add).then_inc(s.acc_set, 1)

    def dve_combine(self, dve, s, own, unit, i, half):
        acc, odd, gates = s.acc[unit[1]][:, i, :], s.odd[unit[1]][:, i, :], s.gates[unit[1]]
        tile = num(unit) * TILES + i
        if i == 0 and half == 0:
            dve.wait_ge(s.acc_set, 2 * num(unit) + 2)
        for c in (2 * half, 2 * half + 1):
            if c:
                own.wait()
            dve.wait_ge(s.experts, tile * 4 + c + 1)
            own.done(dve.scalar_tensor_tensor(out=acc, in0=s.psE[:, c, 0:D], scalar=gates[:, i, 2 * c:2 * c + 1],
                                              in1=acc, op0=ALU.mult, op1=ALU.add))
            gate = gates[:, i, 2 * c + 1:2 * c + 2]
            if c == 0:
                ins = dve.tensor_scalar(odd, s.psE[:, c, D:2 * D], gate, None, ALU.mult)
            else:
                dve.wait_ge(s.combined, tile * 4 + c)
                ins = dve.scalar_tensor_tensor(out=odd, in0=s.psE[:, c, D:2 * D], scalar=gate, in1=odd,
                                               op0=ALU.mult, op1=ALU.add)
            ins.then_inc(s.combined, 1)

    def pool_sum(self, pool, s, unit, i):
        pool.wait_ge(s.combined, (num(unit) * TILES + i) * 4 + 4)
        acc = s.acc[unit[1]][:, i, :]
        pool.tensor_tensor(acc, acc, s.odd[unit[1]][:, i, :], ALU.add).then_inc(s.summed, 1)

    def pass_a(self):
        nc = self.nc
        with ExitStack() as ctx:
            w = self.weights(ctx, "a", ["Wq", "Wk", "Wv"])
            s = self.ffn_state(ctx, "a")
            sb = lambda n, sh, dt=F32: self.sb(ctx, n, sh, dt)
            sem = lambda n: self.sem(ctx, n)
            X = [sb(f"X{h}", [P, TILES, D]) for h in range(2)]
            ln2 = self.layernorm_state(ctx, "a2")
            x2T = [sb(f"x2T{k}", [P, KC, UNIT], FR) for k in range(2)]
            cos, sin = sb("cos", [P, S]), sb("sin", [P, S])
            bqk = sb("bqk", [P, 2, 2])
            raw = [[sb(f"raw{t}{e}", [P, UNIT]) for e in range(2)] for t in range(2)]
            prod = [[sb(f"prod{t}{n}", [P, UNIT]) for n in range(2)] for t in range(2)]
            rot = [[sb(f"rot{t}{e}", [P, UNIT]) for e in range(2)] for t in range(2)]
            parts = [[[sb(f"part{t}{e}{k}", [P, UNIT], FR) for k in range(2)] for e in range(2)] for t in range(2)]
            V = sb("V", [P, TILES, D])
            x_loaded = [sem(f"x_loaded{h}") for h in range(2)]
            x1_stored = [sem(f"x1_stored{h}") for h in range(2)]
            (consts, turned2, hi2, lo2, qk_ready, qk_out, v_ready, v_out,
             rot_q, rot_k, qk_stored, v_stored, pool_own, x1_done) = (sem(n) for n in (
                 "consts", "turned2", "hi2", "lo2", "qk_ready", "qk_out",
                 "v_ready", "v_out", "rot_q", "rot_k", "qk_stored", "v_stored", "pool_own",
                 "x1_done"))
            gw_zero = sem("gw_zero")
            qk_hi, qk_lo = ([sem(f"{q}_{k}") for q in ("q", "k")] for k in ("hi", "lo"))

            block = ctx.enter_context(nc.Block())

            @block.sync
            def _(sp):
                sp.dma_start(X[0][:], rows(self.x_v, (0, 0))).then_inc(x_loaded[0], 16)
                self.load_small(sp, w)
                self.load_experts(sp, w)
                sp.dma_start(cos[:], self.cos).then_inc(consts, 16)
                sp.dma_start(sin[:], self.sin).then_inc(consts, 16)
                for t, b in enumerate((self.bq, self.bk)):
                    sp.dma_start(bqk[:, t, :], b.rearrange("(p e) -> p e", e=2)).then_inc(consts, 16)

                def step(u):
                    v, p, c = shift(u, 3), shift(u, -1), u
                    if exists(p):
                        for t in range(2):
                            dst = (self.qs, self.ks)[t].rearrange("b t (e i) h n -> b t e h i n", e=2)
                            for e in range(2):
                                for k in range(2):
                                    sp.wait_ge((qk_hi, qk_lo)[k][t], 2 * num(p) + e + 1)
                                    sp.dma_start(dst[p[0], k, e, :, :, bass.ds(p[1] * UNIT, UNIT)],
                                                 parts[t][e][k][:].bitcast(F32)).then_inc(qk_stored, 16)
                        sp.wait_ge(v_out, 2 * num(p) + 2)
                        sp.dma_start(rows(self.v_v, p), V[:]).then_inc(v_stored, 16)
                        sp.wait_ge(qk_stored, 128 * num(p) + 128)
                        sp.wait_ge(v_stored, 16 * num(p) + 16)
                    if exists(c):
                        sp.wait_ge(s.summed, TILES * num(c) + TILES)
                        sp.dma_start(rows(self.x1_v, c), s.acc[c[1]][:]).then_inc(x1_stored[c[1]], 16)
                    if exists(v) and not num_is(v, 0):
                        if not num_below(v, 2):
                            wait_apart(sp, s.acc_set, 2 * num(v) - 2)
                        sp.dma_start(X[v[1]][:], rows(self.x_v, v)).then_inc(x_loaded[v[1]], 16)

                over_units(sp, step, ahead={-1: lambda: self.spread_bias(sp, w)})
                for h in range(2):
                    sp.wait_ge(x1_stored[h], 16 * UNITS // 2)

            @block.tensor
            def _(pe):
                def turn_x1(p):
                    pe.wait_ge(ln2.xn_ready, num(p) + 1)
                    for pair in range(2):
                        if not num_is(p, 0):
                            pe.wait_ge(v_out, 2 * num(p) - 1 + pair)
                        self.turn(pe, s, w, ln2.xn, 2 + pair, pair, turned2)

                def project(p, t):
                    if t == 0:
                        pe.wait_ge(hi2, 2 * num(p) + 2)
                        pe.wait_ge(lo2, 2 * num(p) + 2)
                    for e in range(2):
                        if t == 1:
                            pe.wait_ge(qk_out, num(p) * 4 + e + 1)
                        W = w.square["WqWk"[2 * t:2 * t + 2]]
                        self.three(pe, s.psW[:, 2 + e, :], lambda a, k: W[a][:, k, e:D:2],
                                   lambda a, k: x2T[a][:, k, :]).then_inc(qk_ready, 1)

                def project_v(p):
                    for pair in range(2):
                        pe.wait_ge(qk_out, num(p) * 4 + 3 + pair)
                        for i in range(2):
                            t = 2 * pair + i
                            ins = self.three(pe, s.psW[:, 2 + pair, i * D:(i + 1) * D],
                                             lambda a, k: x2T[a][:, k, t * P:(t + 1) * P],
                                             lambda a, k: w.square["Wv"][a][:, k, :])
                        ins.then_inc(v_ready, 1)

                def step(u):
                    v, p = shift(u, 1), shift(u, -1)
                    if exists(u):
                        self.pe_experts(pe, s, w, u, 0, 0)
                        self.pe_experts(pe, s, w, u, 0, 1)
                    if exists(v):
                        self.pe_turn_unit(pe, s, w, v)
                    if exists(u):
                        self.pe_experts(pe, s, w, u, 1, 0)
                    if exists(v):
                        self.pe_router(pe, s, w, v)
                    if exists(u):
                        self.pe_experts(pe, s, w, u, 1, 1)
                    if exists(p):
                        turn_x1(p)
                    if exists(v):
                        self.pe_logits(pe, s, w, v)
                    if exists(u):
                        self.pe_experts(pe, s, w, u, 2, 0)
                    if exists(p):
                        project(p, 0)
                    if exists(v):
                        self.pe_gates(pe, s, w, v)
                    if exists(p):
                        project(p, 1)
                    if exists(u):
                        self.pe_experts(pe, s, w, u, 2, 1)
                    if exists(v):
                        self.pe_bias(pe, s, w, v)
                    if exists(p):
                        project_v(p)
                    if exists(u):
                        self.pe_experts(pe, s, w, u, 3, 0)
                        self.pe_experts(pe, s, w, u, 3, 1)

                self.pe_turn_squares(pe, s, w)
                over_units(pe, step)

            @block.scalar
            def _(act):
                def evacuate(p, t):
                    if num_is(p, 0) and t == 0:
                        act.wait_ge(consts, 64)
                    for e in range(2):
                        act.wait_ge(qk_ready, num(p) * 4 + 2 * t + e + 1)
                        act.activation(raw[t][e][:], s.psW[:, 2 + e, :], ACT.Identity,
                                       bias=bqk[:, t, e:e + 1]).then_inc(qk_out, 1)

                def part_hi(p, t):
                    for e in range(2):
                        act.wait_ge((rot_q, rot_k)[t], 2 * num(p) + e + 1)
                        act.activation(parts[t][e][0][:], rot[t][e][:], ACT.Copy).then_inc(qk_hi[t], 1)

                def step(u):
                    v, n, p = shift(u, 1), shift(u, 2), shift(u, -1)
                    if exists(v):
                        self.act_hi(act, s, v)
                        if num_is(v, 0):
                            self.act_experts_hi(act, w)
                    if exists(p):
                        if not num_is(p, 0):
                            act.wait_ge(turned2, 2 * num(p))
                        self.act_norm(act, ln2, s.acc[p[1]], num(p))
                    if exists(v):
                        self.act_router(act, s, v)
                    if exists(p):
                        for pair in range(2):
                            act.wait_ge(turned2, 2 * num(p) + pair + 1)
                            act.activation(x2T[0][:, :, pair * 2 * P:(pair + 1) * 2 * P],
                                           self.turned_view(s, 2 + pair), ACT.Copy).then_inc(hi2, 1)
                    if exists(v):
                        self.act_gap(act, s, v)
                    if exists(n):
                        if not num_is(n, 0):
                            act.wait_ge(s.turned, 2 * num(n))
                        self.act_norm(act, s.ln, X[n[1]], num(n))
                    if exists(p):
                        if not num_is(p, 0):
                            act.wait_ge(rot_q, 2 * num(p))
                            act.wait_ge(rot_k, 2 * num(p))
                        evacuate(p, 0)
                    if exists(v):
                        self.act_gates(act, s, v)
                    if exists(p):
                        evacuate(p, 1)
                        if not num_is(p, 0):
                            act.wait_ge(qk_stored, 128 * num(p))
                        part_hi(p, 0)
                        if not num_is(p, 0):
                            act.wait_ge(v_stored, 16 * num(p))
                        for pair in range(2):
                            act.wait_ge(v_ready, 2 * num(p) + pair + 1)
                            act.activation(V[:, 2 * pair:2 * pair + 2, :],
                                           s.psW[:, 2 + pair, :].rearrange("p (i n) -> p i n", i=2),
                                           ACT.Copy).then_inc(v_out, 1)
                        part_hi(p, 1)

                over_units(act, step)

            def rotate(eng, own, t, p, signal):
                at = slice(p[1] * UNIT, (p[1] + 1) * UNIT)
                if num_is(p, 0):
                    eng.wait_ge(consts, 64)
                eng.wait_ge(qk_out, num(p) * 4 + 2 * t + 2)
                for e in range(2):
                    own.done(eng.tensor_tensor(prod[t][0][:], raw[t][0][:], (cos, sin)[e][:, at], ALU.mult))
                    own.done(eng.tensor_tensor(prod[t][1][:], raw[t][1][:], (sin, cos)[e][:, at], ALU.mult))
                    own.wait()
                    if not num_is(p, 0) and e == 0:
                        eng.wait_ge(qk_lo[t], 2 * num(p))
                        eng.wait_ge(qk_hi[t], 2 * num(p))
                    eng.tensor_tensor(rot[t][e][:], prod[t][0][:], prod[t][1][:],
                                      (ALU.subtract, ALU.add)[e]).then_inc(signal, 1)
                    eng.wait_ge(signal, 2 * num(p) + e + 1)

            def split_lo(eng, t, p):
                if not num_is(p, 0):
                    eng.wait_ge(qk_stored, 128 * num(p))
                for e in range(2):
                    eng.wait_ge(qk_hi[t], 2 * num(p) + e + 1)
                    eng.tensor_tensor(parts[t][e][1][:], rot[t][e][:], parts[t][e][0][:].bitcast(F32),
                                      ALU.subtract).then_inc(qk_lo[t], 1)

            @block.gpsimd
            def _(pool):
                own = Chain(pool, pool_own)
                self.pool_constants(pool, w)

                def step(u):
                    n, p = shift(u, 2), shift(u, -1)
                    if exists(p):
                        self.pool_rs(pool, w, ln2, own, num(p))
                    if exists(u):
                        self.pool_sum(pool, s, u, 0)
                    if exists(n):
                        self.pool_rs(pool, w, s.ln, own, num(n))
                    if exists(u):
                        self.pool_sum(pool, s, u, 1)
                    if exists(p):
                        rotate(pool, own, 1, p, rot_k)
                        split_lo(pool, 1, p)
                    if exists(u):
                        self.pool_sum(pool, s, u, 2)
                        self.pool_sum(pool, s, u, 3)

                over_units(pool, step, own, 3 + 3 + 4)

            @block.vector
            def _(dve):
                own = Chain(dve, s.own)
                dve.memset(s.Gw[:], 0.0).then_inc(gw_zero, 1)
                dve.wait_ge(gw_zero, 1)

                def step(u):
                    v, n, p = shift(u, 1), shift(u, 2), shift(u, -1)
                    if exists(u):
                        self.dve_combine(dve, s, own, u, 0, 0)
                    if exists(p):
                        dve.wait_ge(s.summed, TILES * num(p) + TILES)
                        self.dve_stats(dve, own, s.acc[p[1]], ln2)
                    if exists(u):
                        self.dve_combine(dve, s, own, u, 0, 1)
                    if exists(v):
                        self.dve_lo(dve, s, v)
                        if num_is(v, 0):
                            self.dve_experts_lo(dve, w)
                    if exists(u):
                        self.dve_combine(dve, s, own, u, 1, 0)
                    if exists(n):
                        dve.wait_ge(x_loaded[n[1]], 16 * n[0] + 16)
                        self.dve_stats(dve, own, X[n[1]], s.ln)
                    if exists(u):
                        self.dve_combine(dve, s, own, u, 1, 1)
                    if exists(p):
                        for pair in range(2):
                            dve.wait_ge(hi2, 2 * num(p) + pair + 1)
                            a = slice(pair * 2 * P, (pair + 1) * 2 * P)
                            dve.tensor_tensor(x2T[1][:, :, a], self.turned_view(s, 2 + pair),
                                              x2T[0][:, :, a].bitcast(F32), ALU.subtract).then_inc(lo2, 1)
                    if exists(v):
                        self.dve_router(dve, s, w, own, v)
                    if exists(u):
                        self.dve_combine(dve, s, own, u, 2, 0)
                    if exists(p):
                        rotate(dve, own, 0, p, rot_q)
                    if exists(u):
                        self.dve_combine(dve, s, own, u, 2, 1)
                    if exists(v):
                        if not num_below(v, 2):
                            dve.wait_ge(x1_stored[v[1]], 16 * v[0])
                            dve.wait_ge(ln2.xn_ready, num(v) - 1)
                        self.dve_acc_set(dve, s, v, lambda q: X[q[1]])
                    if exists(p):
                        split_lo(dve, 0, p)
                    if exists(u):
                        self.dve_combine(dve, s, own, u, 3, 0)
                        self.dve_combine(dve, s, own, u, 3, 1)

                over_units(dve, step, own, DVE_A, {-1: lambda: self.dve_small(dve, s, w)})

    def pass_b(self):
        nc = self.nc
        with ExitStack() as ctx:
            sb = lambda n, sh, dt=F32: self.sb(ctx, n, sh, dt)
            sem = lambda n: self.sem(ctx, n)
            ROWS, MAXROWS = P, P - 2
            Q = [sb(f"Qop{g}", [P, HG, S], FR) for g in range(GROUPS)]
            K = [sb(f"Kop{g}", [P, HG, S], FR) for g in range(GROUPS)]
            Vraw = sb("Vraw", [P, KT, D])
            V1 = [sb(f"V1{g}", [P, KT, HG, 2 * DK]) for g in range(2)]
            W = [sb(f"W{n}", [P, HG, 512]) for n in range(SLOTS)]
            bv = sb("bv_b", [P, D])
            mask = sb("mask", [P, S])
            ident = sb("ident_b", [P, P])
            mx, nm = sb("mx", [P, HG, KT]), sb("nm", [P, HG, KT])
            NB = sb("NB", [P, P // (HG * KT), HG, KT], FR)
            mT = sb("mT", [2 * HG * KT, P], FR)
            O = [sb(f"O{n}", [P, S]) for n in range(2)]
            psM = ctx.enter_context(nc.psum_tensor("psM", [P, BANKS * 512], F32))
            psS = [ctx.enter_context(nc.psum_tensor(f"psS{n}", [P, 512], F32)) for n in range(3)]
            psO = ctx.enter_context(nc.psum_tensor("psO", [P, 512], F32))
            qk_loaded = [sem(f"qk_loaded{g}") for g in range(GROUPS)]
            bv_loaded = sem("bv_loaded")
            rows_set = [sem(f"rows_set{g}") for g in range(GROUPS)]
            m_loaded = [sem(f"m_loaded{g}") for g in range(GROUPS)]
            o_stored = [sem(f"o_stored{n}") for n in range(2)]
            (v_loaded, v_spread, setup, own_p, scores_m, maxed, nb_ready, m_turned, m_out, scores, exps, kept,
             rows_used, sums_out, own_d) = (sem(n) for n in (
                 "v_loaded", "v_spread", "setup", "own_p", "scores_m", "maxed", "nb_ready", "m_turned", "m_out",
                 "scores", "exps", "kept", "rows_used", "sums_out", "own_d"))

            plan = [(j, kt, max(0, kt - 4 * j) * P, kt >= 4 * j) for j in range(2) for kt in range(4 * j + 4)]
            R = len(plan)
            DIAG = sum(r[3] for r in plan)
            MT = HG * KT
            order = interleave(plan)

            def g_of(b, hg):
                return b * GROUPS + hg

            ring, ring_length = max_ring()

            def columns(hg, item, width):
                c = (ring_length * hg + ring[item][0]) % BANKS * 512
                return slice(c, c + width)

            assert GROUPS * ring_length % BANKS == 0

            def last_user(item):
                p = ring[item][0] + ring[item][1] - 1 - BANKS
                for back in range(2):
                    for other, (q, size) in ring.items():
                        if q <= p + back * ring_length < q + size:
                            return other, back

            def after(b, hg, by):
                n = hg + by
                return b + n // GROUPS, n % GROUPS

            def there(b):
                return not isinstance(b, int) or 0 <= b < B

            def over_groups(eng, step, chain=None, per_step=0):
                for hg in range(GROUPS):
                    step(0, hg)
                k0 = chain.k if chain else 0
                with eng.Fori(1, B - 1) as b:
                    if chain:
                        chain.base, chain.k = (b - 1) * (GROUPS * per_step) + k0, 0
                    for hg in range(GROUPS):
                        step(b, hg)
                    assert not chain or chain.k == GROUPS * per_step, chain.k
                if chain:
                    chain.base, chain.k = k0 + (B - 2) * GROUPS * per_step, 0
                for hg in range(GROUPS):
                    step(B - 1, hg)

            block = ctx.enter_context(nc.Block())

            @block.sync
            def _(sp):
                def load(b, hg):
                    h = slice(hg * HG, (hg + 1) * HG)
                    hi, lo = self.qs[b, 0, :, h, :], self.qs[b, 1, :, h, :]
                    sp.dma_start(Q[hg][0:2 * DK].bitcast(F32),
                                 hi.unsqueeze(0).to_broadcast([2, DK, HG, S])).then_inc(qk_loaded[hg], 16)
                    sp.dma_start(Q[hg][2 * DK:3 * DK].bitcast(F32), lo).then_inc(qk_loaded[hg], 16)
                    sp.dma_start(K[hg][0:2 * DK].bitcast(F32), self.ks[b, :, :, h, :].rearrange(
                        "t d h n -> (t d) h n")).then_inc(qk_loaded[hg], 16)
                    sp.dma_start(K[hg][2 * DK:3 * DK].bitcast(F32),
                                 self.ks[b, 0, :, h, :]).then_inc(qk_loaded[hg], 16)

                def load_v(b):
                    sp.dma_start(Vraw[:], self.v_v[:, bass.ds(b * KT, KT), :]).then_inc(v_loaded, 16)

                sp.dma_start(bv[:], self.bv.partition_broadcast(P)).then_inc(bv_loaded, 16)
                for hg in range(3):
                    sp.wait_ge(rows_set[hg], 2)
                    load(0, hg)
                    if hg == 0:
                        load_v(0)

                def load_maxima(b, hg):
                    sp.wait_ge(m_out, g_of(b, hg) + 1)
                    for part in range(2):
                        row = Q[hg][MAXROWS + part:MAXROWS + part + 1].bitcast(F32)
                        sp.dma_start(row.rearrange("p h (t n) -> p (h t) n", n=P),
                                     mT[part * HG * KT:(part + 1) * HG * KT, :].bitcast(F32)
                                     ).then_inc(m_loaded[hg], 16)

                def store(b, hg):
                    wait_apart(sp, sums_out, 2 * g_of(b, hg) + 2)
                    for h in range(HG):
                        sp.dma_start(self.os[b, hg, h], O[hg % 2][32 * h:32 * h + DK + 1, :]
                                     ).then_inc(o_stored[hg % 2], 16)

                load_maxima(0, 0)

                def step(b, hg):
                    g = g_of(b, hg)
                    if not (isinstance(g, int) and g == 0):
                        store(*after(b, hg, -1))
                    b3, g3 = after(b, hg, 3)
                    if there(b3):
                        if not (isinstance(g, int) and g == 0):
                            sp.wait_ge(rows_used, R * g)
                        if isinstance(g, int) and g == 0:
                            sp.wait_ge(rows_set[g3], 2)
                        load(b3, g3)
                    if hg == 2 and there(b + 1):
                        sp.wait_ge(v_spread, g_of(b, 3) + 1)
                        load_v(b + 1)
                    b1, g1 = after(b, hg, 1)
                    if there(b1):
                        load_maxima(b1, g1)

                over_groups(sp, step)
                store(B - 1, GROUPS - 1)
                for n in range(2):
                    sp.wait_ge(o_stored[n], 16 * HG * B * GROUPS // 2)

            @block.gpsimd
            def _(pool):
                own = Chain(pool, own_p)
                pool.memset(K[0][:].bitcast(F32), 1.0).then_inc(rows_set[0], 1)
                own.done(pool.memset(ident[:], 0.0))
                own.done(pool.memset(mask[:], 0.0))
                own.wait()
                pool.affine_select(out=ident[:], in_=ident[:], compare_op=ALU.not_equal, fill=1.0, base=0,
                                   pattern=[[-1, P]], channel_multiplier=1).then_inc(setup, 1)
                pool.affine_select(out=mask[:, S - P:S], in_=mask[:, S - P:S], compare_op=ALU.is_ge, fill=MASKED,
                                   base=0, pattern=[[-1, P]], channel_multiplier=1).then_inc(setup, 1)
                pool.memset(NB[:].bitcast(F32), 0.0).then_inc(setup, 1)
                pool.memset(K[1][:].bitcast(F32), 1.0).then_inc(rows_set[1], 1)
                for g in (2, 3):
                    pool.memset(Q[g][:].bitcast(F32), 0.0).then_inc(rows_set[g], 1)
                    pool.memset(K[g][:].bitcast(F32), 1.0).then_inc(rows_set[g], 1)
                for g in range(2):
                    own.done(pool.memset(V1[g][:], 1.0))
                own.wait()

                def spread(b, hg):
                    g = g_of(b, hg)
                    wait_apart(pool, v_loaded, 16 * b + 16)
                    if not (isinstance(g, int) and g < 2):
                        wait_apart(pool, rows_used, R * g - R)
                    for h in range(HG):
                        c = (hg * HG + h) * DK
                        ins = pool.tensor_tensor(V1[hg % 2][:, :, h, 0:DK], Vraw[:, :, c:c + DK],
                                                 bv[:, c:c + DK].unsqueeze(1).to_broadcast([P, KT, DK]), ALU.add)
                    ins.then_inc(v_spread, 1)

                pool.wait_ge(bv_loaded, 16)
                spread(0, 0)

                def step(b, hg):
                    b1, g1 = after(b, hg, 1)
                    if there(b1):
                        spread(b1, g1)
                    for r, (j, kt, c0, diag) in enumerate(plan):
                        if diag:
                            row = g_of(b, hg) * R + r
                            wait_apart(pool, exps, HG * (row + 1))
                            Wd = W[r % SLOTS][:, :, c0:c0 + P]
                            pool.affine_select(out=Wd, in_=Wd, compare_op=ALU.is_ge, fill=0.0, base=0,
                                               pattern=[[0, HG], [1, P]], channel_multiplier=-1).then_inc(kept, 1)

                over_groups(pool, step)

            @block.vector
            def _(dve):
                own = Chain(dve, own_d)
                for g in range(2):
                    dve.memset(Q[g][:].bitcast(F32), 0.0).then_inc(rows_set[g], 1)
                dve.wait_ge(setup, 2)

                def max_tile(b, hg, t):
                    h, qt = t // KT, t % KT
                    w = (qt + 1) * P
                    n = g_of(b, hg) * MT + t
                    wait_apart(dve, scores_m, n + 1)
                    tile = psM[:, columns(hg, t, w)]
                    dve.tensor_tensor_reduce(tile, tile, mask[:, S - w:S], 1.0, LOWEST, ALU.add, ALU.max,
                                             mx[:, h, qt:qt + 1]).then_inc(maxed, 1)

                def negate(b, hg):
                    g = g_of(b, hg)
                    dve.wait_ge(maxed, (g + 1) * MT)
                    own.done(dve.tensor_scalar(nm[:], mx[:], -1.0, None, ALU.mult))
                    own.wait()
                    if not (isinstance(g, int) and g == 0):
                        dve.wait_ge(m_turned, g)
                    own.done(dve.tensor_copy(NB[:, 0], nm[:]))
                    own.wait()
                    dve.tensor_tensor(NB[:, 1], nm[:], NB[:, 0].bitcast(F32),
                                      ALU.subtract).then_inc(nb_ready, 1)

                for g in range(2):
                    for t in range(MT):
                        max_tile(0, g, t)
                    dve.wait_ge(setup, 3)
                    negate(0, g)

                def take_sums(b, hg, half):
                    g = g_of(b, hg)
                    dve.wait_ge(rows_used, g * R + (4, R)[half])
                    if half == 0 and not (isinstance(g, int) and g < 2):
                        dve.wait_ge(o_stored[hg % 2], 16 * HG * (b * (GROUPS // 2) + hg // 2))
                    dve.tensor_copy(O[hg % 2][:, half * 512:(half + 1) * 512], psO[:]).then_inc(sums_out, 1)

                def step(b, hg):
                    b2, g2 = after(b, hg, 2)
                    g = g_of(b, hg)
                    for kind, r, k in order:
                        if kind == "max" and there(b2):
                            max_tile(b2, g2, k)
                        if kind == "weigh" and r == R - 1 and not (isinstance(g, int) and g == 0):
                            take_sums(*after(b, hg, -1), 1)
                        if kind == "weigh" and r == 3:
                            take_sums(b, hg, 0)
                    if there(b2):
                        negate(b2, g2)

                over_groups(dve, step, own, 2)
                take_sums(B - 1, GROUPS - 1, 1)

            @block.scalar
            def _(act):
                def m_copy(b, hg):
                    g = g_of(b, hg)
                    act.wait_ge(m_turned, g + 1)
                    if not (isinstance(g, int) and g == 0):
                        pb, pg = after(b, hg, -1)
                        act.wait_ge(m_loaded[pg], 32 * pb + 32)
                    act.activation(mT[:], psM[0:2 * HG * KT, columns(hg + 1, "turn", P)], ACT.Copy).then_inc(m_out, 1)

                m_copy(0, 0)

                def step(b, hg):
                    for kind, r, h in order:
                        if kind == "score":
                            row = g_of(b, hg) * R + r
                            act.wait_ge(scores, row * HG + h + 1)
                            if h == 0 and not (isinstance(row, int) and row < SLOTS):
                                act.wait_ge(rows_used, row - SLOTS + 1)
                            c0 = plan[r][2]
                            act.activation(W[r % SLOTS][:, h, c0:512], psS[(r * HG + h) % 3][:, c0:512], ACT.Exp,
                                           scale=float(DK) ** -0.5).then_inc(exps, 1)
                        if kind == "turn" and there(after(b, hg, 1)[0]):
                            m_copy(*after(b, hg, 1))

                over_groups(act, step)

            @block.tensor
            def _(pe):
                pe.wait_ge(setup, 1)

                def wait_banks(g, item):
                    user, back = last_user(item)
                    first = isinstance(g, int) and g == 0
                    if user == "turn" and first:
                        user, back = last_user("turn")
                    if back and first:
                        return
                    if user == "turn":
                        pe.wait_ge(m_out, g - back)
                    else:
                        pe.wait_ge(maxed, g * MT + user + 1 - back * MT)

                def max_tile(b, hg, t):
                    h, qt = t // KT, t % KT
                    g = g_of(b, hg)
                    if t == 0:
                        pe.wait_ge(qk_loaded[hg], 64 * b + 64)
                    wait_banks(g, t)
                    w = (qt + 1) * P
                    for c in range(0, w, 512):
                        n = min(512, max(w - c, 256))
                        at = columns(hg, t, c).stop
                        ins = pe.matmul(psM[:, at:at + n], Q[hg][0:MAXROWS, h, qt * P:(qt + 1) * P],
                                        K[hg][0:MAXROWS, h, c:c + n], start=True, stop=True)
                    ins.then_inc(scores_m, 1)

                def turn_maxima(b, hg):
                    g = g_of(b, hg)
                    if isinstance(g, int) and g == B * GROUPS - 1:
                        pe.wait_ge(maxed, (g + 1) * MT)
                    else:
                        wait_banks(g + 1, "turn")
                    pe.wait_ge(nb_ready, g + 1)
                    pe.transpose(psM[:, columns(hg + 1, "turn", P)],
                                 NB[:].bitcast(F32).rearrange("p k h t -> p (k h t)"), ident[:]).then_inc(m_turned, 1)

                for g in range(2):
                    for t in range(MT):
                        if g == 1 and t == TURN_AT:
                            turn_maxima(0, 0)
                        max_tile(0, g, t)

                def score(b, hg, r, h):
                    j, kt, c0, diag = plan[r]
                    n = (g_of(b, hg) * R + r) * HG + h
                    if not (isinstance(n, int) and n < 3):
                        pe.wait_ge(exps, n - 2)
                    c = min(c0, 256)
                    pe.matmul(psS[(r * HG + h) % 3][:, c:512], K[hg][0:ROWS, h, kt * P:(kt + 1) * P],
                              Q[hg][0:ROWS, h, j * 512 + c:(j + 1) * 512], start=True, stop=True).then_inc(scores, 1)

                def weigh(b, hg, r):
                    j, kt, c0, diag = plan[r]
                    g = g_of(b, hg)
                    if diag:
                        pe.wait_ge(kept, g * DIAG + sum(q[3] for q in plan[:r + 1]))
                    else:
                        pe.wait_ge(exps, (g * R + r + 1) * HG)
                    if r == 0:
                        pe.wait_ge(v_spread, g + 1)
                    if kt == 0 and not (isinstance(g, int) and g == 0 and j == 0):
                        pe.wait_ge(sums_out, 2 * g + j)
                    last = kt == 4 * j + 3
                    for h in range(HG):
                        ins = pe.matmul(psO[32 * h:32 * h + 32, c0:512], V1[hg % 2][:, kt, h, :],
                                        W[r % SLOTS][:, h, c0:512], start=(kt == 0), stop=last)
                    ins.then_inc(rows_used, 1)

                def step(b, hg):
                    g = g_of(b, hg)
                    b2, g2 = after(b, hg, 2)
                    pe.wait_ge(m_loaded[hg], 32 * b + 32)
                    for kind, r, k in order:
                        if kind == "score":
                            score(b, hg, r, k)
                        elif kind == "max" and there(b2):
                            max_tile(b2, g2, k)
                        elif kind == "turn" and there(after(b, hg, 1)[0]):
                            turn_maxima(*after(b, hg, 1))
                        elif kind == "weigh":
                            if r < R - LAG:
                                weigh(b, hg, r)
                            elif not (isinstance(g, int) and g == 0):
                                weigh(*after(b, hg, -1), r)

                over_groups(pe, step)
                for r in range(R - LAG, R):
                    weigh(B - 1, GROUPS - 1, r)

    def pass_c(self):
        nc = self.nc
        with ExitStack() as ctx:
            w = self.weights(ctx, "c", ["Wo"])
            s = self.ffn_state(ctx, "c")
            sb = lambda n, sh, dt=F32: self.sb(ctx, n, sh, dt)
            sem = lambda n: self.sem(ctx, n)
            X1 = [sb(f"X1{h}", [P, TILES, D]) for h in range(2)]
            SUMS = H * (DK + 1)
            WHOLE, REST = SUMS // P, SUMS % P
            OT = [sb(f"OT{h}", [P, WHOLE + 1, UNIT]) for h in range(2)]
            attn, rc = sb("attn", [P, TILES, D]), sb("rc", [P, TILES, H])
            aT = [sb(f"aT{k}", [P, KC, UNIT], FR) for k in range(2)]
            bo = sb("bo", [P, D])
            x1_loaded = [sem(f"x1_loaded{h}") for h in range(2)]
            o_loaded = [sem(f"o_loaded{h}") for h in range(2)]
            out_stored = [sem(f"out_stored{h}") for h in range(2)]
            (bo_loaded, o_turned, attn_ready, a_turned, a_hi, a_lo, proj, x2_ready, x1_biased, pool_own, gw_zero) = (
                sem(n) for n in ("bo_loaded", "o_turned", "attn_ready", "a_turned", "a_hi", "a_lo", "proj",
                                 "x2_ready", "x1_biased", "pool_own_c", "gw_zero_c"))
            block = ctx.enter_context(nc.Block())

            @block.sync
            def _(sp):
                def load_x1(v):
                    sp.dma_start(X1[v[1]][:], rows(self.x1_v, v)).then_inc(x1_loaded[v[1]], 16)

                def load_sums(v):
                    src = self.os[v[0], :, :, :, v[1] * UNIT:(v[1] + 1) * UNIT].rearrange("g h r n -> (g h r) n")
                    sp.dma_start(OT[v[1]][:, 0:WHOLE, :], src[0:WHOLE * P].rearrange(
                        "(c p) n -> p c n", p=P)).then_inc(o_loaded[v[1]], 16)
                    sp.dma_start(OT[v[1]][0:REST, WHOLE, :], src[WHOLE * P:SUMS]).then_inc(o_loaded[v[1]], 16)

                load_sums((0, 0))
                self.load_small(sp, w)
                sp.dma_start(bo[:], self.bo.partition_broadcast(P)).then_inc(bo_loaded, 16)
                load_x1((0, 0))
                self.load_experts(sp, w)

                def step(u):
                    v = shift(u, 3)
                    if exists(v):
                        if not num_below(v, 2):
                            wait_apart(sp, o_turned, TILES * (num(v) - 1))
                        load_sums(v)
                        if not num_below(v, 2):
                            wait_apart(sp, s.acc_set, 2 * num(v) - 2)
                        load_x1(v)
                    if exists(u):
                        sp.wait_ge(s.summed, TILES * num(u) + TILES)
                        sp.dma_start(rows(self.out_v, u), s.acc[u[1]][:]).then_inc(out_stored[u[1]], 16)

                over_units(sp, step, ahead={-1: lambda: self.spread_bias(sp, w)})
                for h in range(2):
                    sp.wait_ge(out_stored[h], 16 * UNITS // 2)

            @block.tensor
            def _(pe):
                def turn_sums(n, i):
                    if i < 2 and not num_is(n, 0):
                        pe.wait_ge(x2_ready, 2 * num(n) - 1 + i)
                    if i >= 2:
                        pe.wait_ge(attn_ready, TILES * num(n) + i - 1)
                    for c, r in enumerate([P] * WHOLE + [REST]):
                        ins = pe.transpose(s.psW[:, 2 + i % 2, c * P:c * P + r], OT[n[1]][0:r, c, i * P:(i + 1) * P],
                                           w.ident[0:r, 0:r])
                    ins.then_inc(o_turned, 1)

                def step(u):
                    v, n = shift(u, 1), shift(u, 2)
                    if exists(n):
                        pe.wait_ge(o_loaded[n[1]], 32 * n[0] + 32)
                        turn_sums(n, 0)
                        turn_sums(n, 1)
                    if exists(u):
                        self.pe_experts(pe, s, w, u, 0, 0)
                    if exists(v):
                        self.pe_turn_unit(pe, s, w, v)
                    if exists(n):
                        turn_sums(n, 2)
                        turn_sums(n, 3)
                    if exists(u):
                        self.pe_experts(pe, s, w, u, 0, 1)
                    if exists(v):
                        self.pe_router(pe, s, w, v)
                    if exists(n):
                        pe.wait_ge(attn_ready, TILES * num(n) + 4)
                        for pair in range(2):
                            self.turn(pe, s, w, attn, 2 + pair, pair, a_turned)
                    if exists(u):
                        self.pe_experts(pe, s, w, u, 1, 0)
                    if exists(v):
                        self.pe_logits(pe, s, w, v)
                    if exists(u):
                        self.pe_experts(pe, s, w, u, 1, 1)
                        self.pe_experts(pe, s, w, u, 2, 0)
                    if exists(n):
                        pe.wait_ge(a_hi, 2 * num(n) + 2)
                        pe.wait_ge(a_lo, 2 * num(n) + 2)
                        if num_is(n, 0):
                            pe.wait_ge(w.small_ready, 1)
                        for pair in range(2):
                            for i in range(2):
                                t = 2 * pair + i
                                ins = self.three(pe, s.psW[:, 2 + pair, i * D:(i + 1) * D],
                                                 lambda a, k: aT[a][:, k, t * P:(t + 1) * P],
                                                 lambda a, k: w.square["Wo"][a][:, k, :])
                            ins.then_inc(proj, 1)
                    if exists(v):
                        self.pe_gates(pe, s, w, v)
                    if exists(u):
                        self.pe_experts(pe, s, w, u, 2, 1)
                    if exists(v):
                        self.pe_bias(pe, s, w, v)
                    if exists(u):
                        self.pe_experts(pe, s, w, u, 3, 0)
                        self.pe_experts(pe, s, w, u, 3, 1)

                self.pe_turn_squares(pe, s, w)
                over_units(pe, step)

            @block.scalar
            def _(act):
                def step(u):
                    v, n = shift(u, 1), shift(u, 2)
                    if exists(v):
                        self.act_hi(act, s, v)
                        self.act_router(act, s, v)
                    if exists(n):
                        for pair in range(2):
                            act.wait_ge(a_turned, 2 * num(n) + pair + 1)
                            act.activation(aT[0][:, :, pair * 2 * P:(pair + 1) * 2 * P],
                                           self.turned_view(s, 2 + pair), ACT.Copy).then_inc(a_hi, 1)
                    if exists(v):
                        self.act_gap(act, s, v)
                        self.act_gates(act, s, v)
                    if exists(n):
                        if not num_is(n, 0):
                            act.wait_ge(s.turned, 2 * num(n))
                        self.act_norm(act, s.ln, X1[n[1]], num(n))

                self.act_experts_hi(act, w)
                over_units(act, step)

            @block.gpsimd
            def _(pool):
                own = Chain(pool, pool_own)
                self.pool_constants(pool, w)
                pool.wait_ge(bo_loaded, 16)

                def step(u):
                    v, n = shift(u, 1), shift(u, 2)
                    if exists(n):
                        pool.wait_ge(x1_loaded[n[1]], 16 * n[0] + 16)
                        for i in range(TILES):
                            ins = pool.tensor_tensor(X1[n[1]][:, i, :], X1[n[1]][:, i, :], bo[:], ALU.add)
                        ins.then_inc(x1_biased, 1)
                    if exists(u):
                        self.pool_sum(pool, s, u, 0)
                        self.pool_sum(pool, s, u, 1)
                    if exists(n):
                        self.pool_rs(pool, w, s.ln, own, num(n))
                    if exists(u):
                        self.pool_sum(pool, s, u, 2)
                        self.pool_sum(pool, s, u, 3)

                over_units(pool, step, own, 3)

            @block.vector
            def _(dve):
                own = Chain(dve, s.own)
                dve.memset(s.Gw[:], 0.0).then_inc(gw_zero, 1)
                dve.wait_ge(gw_zero, 1)
                self.dve_small(dve, s, w)

                def attend(n, i):
                    dve.wait_ge(o_turned, TILES * num(n) + i + 1)
                    if i == 0 and not num_is(n, 0):
                        dve.wait_ge(a_turned, 2 * num(n))
                    ps = s.psW[:, 2 + i % 2, 0:SUMS].rearrange("p (h d) -> p h d", d=DK + 1)
                    own.done(dve.reciprocal(rc[:, i, :], ps[:, :, DK]))
                    own.wait()
                    dve.tensor_tensor(attn[:, i, :].rearrange("p (h d) -> p h d", d=DK), ps[:, :, 0:DK],
                                      rc[:, i, :].unsqueeze(2).to_broadcast([P, H, DK]),
                                      ALU.mult).then_inc(attn_ready, 1)

                def step(u):
                    v, n = shift(u, 1), shift(u, 2)
                    if exists(n):
                        attend(n, 0)
                        attend(n, 1)
                    if exists(u):
                        self.dve_combine(dve, s, own, u, 0, 0)
                    if exists(n):
                        attend(n, 2)
                        attend(n, 3)
                    if exists(v):
                        self.dve_lo(dve, s, v)
                    if exists(u):
                        self.dve_combine(dve, s, own, u, 0, 1)
                    if exists(n):
                        for pair in range(2):
                            dve.wait_ge(a_hi, 2 * num(n) + pair + 1)
                            a = slice(pair * 2 * P, (pair + 1) * 2 * P)
                            dve.tensor_tensor(aT[1][:, :, a], self.turned_view(s, 2 + pair),
                                              aT[0][:, :, a].bitcast(F32), ALU.subtract).then_inc(a_lo, 1)
                    if exists(u):
                        self.dve_combine(dve, s, own, u, 1, 0)
                    if exists(v):
                        self.dve_router(dve, s, w, own, v)
                    if exists(u):
                        self.dve_combine(dve, s, own, u, 1, 1)
                        self.dve_combine(dve, s, own, u, 2, 0)
                    if exists(n):
                        dve.wait_ge(x1_biased, num(n) + 1)
                        for pair in range(2):
                            dve.wait_ge(proj, 2 * num(n) + pair + 1)
                            t = slice(2 * pair, 2 * pair + 2)
                            dve.tensor_tensor(X1[n[1]][:, t, :],
                                              s.psW[:, 2 + pair, :].rearrange("p (i n) -> p i n", i=2),
                                              X1[n[1]][:, t, :], ALU.add).then_inc(x2_ready, 1)
                        dve.wait_ge(x2_ready, 2 * num(n) + 2)
                        self.dve_stats(dve, own, X1[n[1]], s.ln)
                    if exists(u):
                        self.dve_combine(dve, s, own, u, 2, 1)
                    if exists(v):
                        if not num_below(v, 2):
                            dve.wait_ge(out_stored[v[1]], 16 * v[0])
                        self.dve_acc_set(dve, s, v, lambda q: X1[q[1]])
                    if exists(u):
                        self.dve_combine(dve, s, own, u, 3, 0)
                        self.dve_combine(dve, s, own, u, 3, 1)

                over_units(dve, step, own, DVE_C, {-1: lambda: self.dve_experts_lo(dve, w)})


def num_is(unit, n):
    return isinstance(unit[0], int) and num(unit) == n


def num_below(unit, n):
    return isinstance(unit[0], int) and num(unit) < n


ROUTER = 4 + 4 + 1 + 1 + 1 + 1 + 1 + 1 + 1 + 1 + 2
DVE_A = TILES + TILES + TILES * 4 + ROUTER + 4
DVE_C = TILES + TILES + TILES * 4 + ROUTER


def macaron_kernel(nc, *args):
    k = Kernel(nc, args)
    k.pass_a()
    k.pass_b()
    k.pass_c()


_INS = ["L0_attn_x", "L0_attn_Wq", "L0_attn_bq", "L0_attn_Wk", "L0_attn_bk", "L0_attn_Wv", "L0_attn_bv",
        "L0_attn_Wo", "L0_attn_bo", "L0_ffn_Wg", "L0_ffn_We", "L0_ffn_be"]


def rope_tables():
    freq = (np.float32(1.0) / np.float32(THETA) ** (np.arange(0, DK, 2, dtype=np.float32) / np.float32(DK)))
    angle = freq.astype(np.float32)[:, None] * np.arange(S, dtype=np.float32)[None, :]
    return [np.ascontiguousarray(np.tile(f(angle).astype(np.float32), (H, 1))) for f in (np.cos, np.sin)]


def kernel(**inputs):
    import concourse.bacc as _bacc
    from concourse.bass_utils import run_bass_kernel_spmd as _run

    nc = _bacc.Bacc("TRN2", target_bir_lowering=False, num_devices=1)
    arrays, args = {}, []
    given = [(n, np.ascontiguousarray(inputs[n])) for n in _INS]
    given += list(zip(("rope_cos", "rope_sin"), rope_tables()))
    for name, a in given:
        arrays[f"in_{name}_dram"] = a
        args.append(nc.dram_tensor(f"in_{name}_dram", a.shape, mybir.dt.from_np(a.dtype), kind="ExternalInput").ap())
    args.append(nc.dram_tensor("out_0_dram", (B, S, D), F32, kind="ExternalOutput").ap())
    macaron_kernel(nc, *args)
    r = _run(nc, [arrays], core_ids=[0])
    return r.results[0]["out_0_dram"]
```
